# Optimizing a Trainium2 kernel written in Bass

```python
import numpy as np
import jax
import jax.numpy as jnp

def _softmax(x, axis=-1):
    return jax.nn.softmax(x, axis=axis)

def _gelu(x):
    return jax.nn.gelu(x, approximate=True)

def _silu(x):
    return jax.nn.silu(x)

def _sigmoid(x):
    return jax.nn.sigmoid(x)

def _layernorm(x, axis=-1, eps=1e-05):
    m = jnp.mean(x, axis=axis, keepdims=True)
    v = jnp.var(x, axis=axis, keepdims=True)
    return (x - m) / jnp.sqrt(v + eps)

def _scatter_add(tgt, idx, src, axis=0):
    return tgt.at[idx].add(src)

def _segment_sum(src, seg, n):
    return jax.ops.segment_sum(src, seg, n)
kernel_name = 'mk_gnn_resnorm_d4_gnn_r8_ddeac1'

def setup_inputs(seed: int=0):
    np.random.seed(seed)
    _w = jnp.asarray

    def _rec_inputs():
        import jax
        import jax.numpy as jnp
        _gk = jax.random.key(seed)
        x = -0.0003713 + 1 * jax.random.normal(jax.random.fold_in(_gk, 1), (6250, 256), jnp.float32)
        src = jax.random.randint(jax.random.fold_in(_gk, 2), (100000,), 0, 6250, jnp.int32)
        dst = jax.random.randint(jax.random.fold_in(_gk, 3), (100000,), 0, 6250, jnp.int32)
        _o = jnp.argsort(dst, stable=True)
        src = src[_o]
        dst = dst[_o]
        return (x, src, dst)
    x, src, dst = _rec_inputs()

    def _L0_gnn_setup():
        import jax, jax.numpy as jnp
        import numpy as np
        N, E, FIN, H, FO = (6250, 100000, 256, 8, 32)
        key = jax.random.key(seed)
        ks = jax.random.split(key, 7)
        node_features = jax.random.normal(ks[0], (N, FIN), dtype=jnp.float32)
        edge_index = jax.random.randint(ks[1], (2, E), 0, N, dtype=jnp.int32).astype(jnp.int64)
        Wp = jax.random.normal(ks[2], (H * FO, FIN), dtype=jnp.float32) * (1.0 / np.sqrt(FIN))
        a_src = jax.random.normal(ks[3], (1, H, FO), dtype=jnp.float32) * 0.1
        a_trg = jax.random.normal(ks[4], (1, H, FO), dtype=jnp.float32) * 0.1
        Wskip = jax.random.normal(ks[5], (H * FO, FIN), dtype=jnp.float32) * (1.0 / np.sqrt(FIN))
        bias = jnp.zeros((H * FO,), dtype=jnp.float32)
        return {'node_features': node_features, 'edge_index': edge_index, 'Wp': Wp, 'a_src': a_src, 'a_trg': a_trg, 'Wskip': Wskip, 'bias': bias}
    _L0_gnn_all = _L0_gnn_setup()
    _L0_gnn_in = {k: v for k, v in _L0_gnn_all.items() if k in ('Wp', 'a_src', 'a_trg', 'Wskip', 'bias')}
    del _L0_gnn_all

    def _L1_gnn_setup():
        import jax, jax.numpy as jnp
        import numpy as np
        N_NODES = 6250
        LN_EPS = 1e-05

        def _sage_conv(x, src, dst, W_l, b_l, W_r):
            msg_sum = jax.ops.segment_sum(x[src], dst, num_segments=N_NODES)
            cnt = jax.ops.segment_sum(jnp.ones((src.shape[0],), x.dtype), dst, num_segments=N_NODES)
            mean = msg_sum / jnp.maximum(cnt, 1.0)[:, None]
            return mean @ W_l + b_l + x @ W_r

        def _layer_norm(x, g, b):
            mu = jnp.mean(x, axis=-1, keepdims=True)
            var = jnp.mean(jnp.square(x - mu), axis=-1, keepdims=True)
            return (x - mu) * jax.lax.rsqrt(var + LN_EPS) * g + b
        key = jax.random.key(seed)
        ks = jax.random.split(key, 6)
        d_in, d_hid, d_out = (256, 256, 256)
        E = 100000
        s = lambda d: 1.0 / np.sqrt(d)
        return {'x': jax.random.normal(ks[0], (N_NODES, d_in), jnp.float32), 'edge_index': jax.random.randint(ks[1], (2, E), 0, N_NODES, jnp.int64), 'W_l1': jax.random.normal(ks[2], (d_in, d_hid), jnp.float32) * s(d_in), 'b_l1': jnp.zeros((d_hid,), jnp.float32), 'W_r1': jax.random.normal(ks[3], (d_in, d_hid), jnp.float32) * s(d_in), 'ln1_g': jnp.ones((d_hid,), jnp.float32), 'ln1_b': jnp.zeros((d_hid,), jnp.float32), 'W_l2': jax.random.normal(ks[4], (d_hid, d_out), jnp.float32) * s(d_hid), 'b_l2': jnp.zeros((d_out,), jnp.float32), 'W_r2': jax.random.normal(ks[5], (d_hid, d_out), jnp.float32) * s(d_hid), 'ln2_g': jnp.ones((d_out,), jnp.float32), 'ln2_b': jnp.zeros((d_out,), jnp.float32)}
    _L1_gnn_all = _L1_gnn_setup()
    _L1_gnn_in = {k: v for k, v in _L1_gnn_all.items() if k in ('W_l1', 'b_l1', 'W_r1', 'ln1_g', 'ln1_b', 'W_l2', 'b_l2', 'W_r2', 'ln2_g', 'ln2_b')}
    del _L1_gnn_all

    def _L2_gnn_setup():
        import jax, jax.numpy as jnp
        import numpy as np
        ALPHA = 0.2
        LN_EPS = 1e-05

        def _gat_layer(x, src, dst, W, b, a, g, beta, N, concat):
            h = x @ W.T + b
            d = W.shape[0]
            s_src = h @ a[:d]
            s_dst = h @ a[d:]
            score = s_src[src] + s_dst[dst]
            e = jnp.exp(-jax.nn.leaky_relu(score, ALPHA))
            h_prime = jax.ops.segment_sum(e[:, None] * h[dst], src, num_segments=N)
            mu = jnp.mean(h_prime, axis=-1, keepdims=True)
            var = jnp.var(h_prime, axis=-1, keepdims=True)
            h_prime = (h_prime - mu) * jax.lax.rsqrt(var + LN_EPS) * g + beta
            return jax.nn.elu(h_prime) if concat else h_prime
        key = jax.random.key(seed)
        ks = jax.random.split(key, 13)
        N, E, F, D, H = (6250, 100000, 256, 64, 8)
        S = 0.02
        inp = {'embeds': jax.random.normal(ks[0], (N, F), dtype=jnp.float32), 'W_heads': jax.random.normal(ks[1], (H, D, F), dtype=jnp.float32) * S, 'b_heads': jax.random.normal(ks[2], (H, D), dtype=jnp.float32) * S, 'a_heads': jax.random.normal(ks[3], (H, 2 * D), dtype=jnp.float32) * S, 'g_heads': jnp.ones((H, D), dtype=jnp.float32), 'beta_heads': jnp.zeros((H, D), dtype=jnp.float32), 'W_out': jax.random.normal(ks[4], (F, D * H), dtype=jnp.float32) * S, 'b_out': jax.random.normal(ks[5], (F,), dtype=jnp.float32) * S, 'a_out': jax.random.normal(ks[6], (2 * F,), dtype=jnp.float32) * S, 'g_out': jnp.ones((F,), dtype=jnp.float32), 'beta_out': jnp.zeros((F,), dtype=jnp.float32), 'edge_index': jax.random.randint(ks[7], (2, E), 0, N, dtype=jnp.int32)}
        return inp
    _L2_gnn_all = _L2_gnn_setup()
    _L2_gnn_in = {k: v for k, v in _L2_gnn_all.items() if k in ('W_heads', 'b_heads', 'a_heads', 'g_heads', 'beta_heads', 'W_out', 'b_out', 'a_out', 'g_out', 'beta_out')}
    del _L2_gnn_all

    def _L3_gnn_setup():
        import jax, jax.numpy as jnp
        import numpy as np
        N = 6250
        E = 100000
        H = 256
        HEADS = 4
        OUT = H // HEADS
        NEG_SLOPE = 0.2
        EPS = 1e-05
        key = jax.random.key(seed)
        ks = jax.random.split(key, 6)
        s = 1.0 / np.sqrt(H)
        x = jax.random.normal(ks[0], (N, H), dtype=jnp.float32)
        edge_index = jax.random.randint(ks[1], (2, E), 0, N, dtype=jnp.int32)
        W = jax.random.normal(ks[2], (H, HEADS * OUT), dtype=jnp.float32) * s
        att_src = jax.random.normal(ks[3], (HEADS, OUT), dtype=jnp.float32) * s
        att_dst = jax.random.normal(ks[4], (HEADS, OUT), dtype=jnp.float32) * s
        bias = jnp.zeros((H,), dtype=jnp.float32)
        gamma = jnp.ones((H,), dtype=jnp.float32)
        beta = jnp.zeros((H,), dtype=jnp.float32)
        return {'x': x, 'edge_index': edge_index, 'W': W, 'att_src': att_src, 'att_dst': att_dst, 'bias': bias, 'gamma': gamma, 'beta': beta}
    _L3_gnn_all = _L3_gnn_setup()
    _L3_gnn_in = {k: v for k, v in _L3_gnn_all.items() if k in ('W', 'att_src', 'att_dst', 'bias', 'gamma', 'beta')}
    del _L3_gnn_all
    return {'x': x, 'src': src, 'dst': dst, 'L0_gnn_Wp': _L0_gnn_in['Wp'], 'L0_gnn_a_src': _L0_gnn_in['a_src'], 'L0_gnn_a_trg': _L0_gnn_in['a_trg'], 'L0_gnn_Wskip': _L0_gnn_in['Wskip'], 'L0_gnn_bias': _L0_gnn_in['bias'], 'L1_gnn_W_l1': _L1_gnn_in['W_l1'], 'L1_gnn_b_l1': _L1_gnn_in['b_l1'], 'L1_gnn_W_r1': _L1_gnn_in['W_r1'], 'L1_gnn_ln1_g': _L1_gnn_in['ln1_g'], 'L1_gnn_ln1_b': _L1_gnn_in['ln1_b'], 'L1_gnn_W_l2': _L1_gnn_in['W_l2'], 'L1_gnn_b_l2': _L1_gnn_in['b_l2'], 'L1_gnn_W_r2': _L1_gnn_in['W_r2'], 'L1_gnn_ln2_g': _L1_gnn_in['ln2_g'], 'L1_gnn_ln2_b': _L1_gnn_in['ln2_b'], 'L2_gnn_W_heads': _L2_gnn_in['W_heads'], 'L2_gnn_b_heads': _L2_gnn_in['b_heads'], 'L2_gnn_a_heads': _L2_gnn_in['a_heads'], 'L2_gnn_g_heads': _L2_gnn_in['g_heads'], 'L2_gnn_beta_heads': _L2_gnn_in['beta_heads'], 'L2_gnn_W_out': _L2_gnn_in['W_out'], 'L2_gnn_b_out': _L2_gnn_in['b_out'], 'L2_gnn_a_out': _L2_gnn_in['a_out'], 'L2_gnn_g_out': _L2_gnn_in['g_out'], 'L2_gnn_beta_out': _L2_gnn_in['beta_out'], 'L3_gnn_W': _L3_gnn_in['W'], 'L3_gnn_att_src': _L3_gnn_in['att_src'], 'L3_gnn_att_dst': _L3_gnn_in['att_dst'], 'L3_gnn_bias': _L3_gnn_in['bias'], 'L3_gnn_gamma': _L3_gnn_in['gamma'], 'L3_gnn_beta': _L3_gnn_in['beta']}

def reference(x, src, dst, L0_gnn_Wp, L0_gnn_a_src, L0_gnn_a_trg, L0_gnn_Wskip, L0_gnn_bias, L1_gnn_W_l1, L1_gnn_b_l1, L1_gnn_W_r1, L1_gnn_ln1_g, L1_gnn_ln1_b, L1_gnn_W_l2, L1_gnn_b_l2, L1_gnn_W_r2, L1_gnn_ln2_g, L1_gnn_ln2_b, L2_gnn_W_heads, L2_gnn_b_heads, L2_gnn_a_heads, L2_gnn_g_heads, L2_gnn_beta_heads, L2_gnn_W_out, L2_gnn_b_out, L2_gnn_a_out, L2_gnn_g_out, L2_gnn_beta_out, L3_gnn_W, L3_gnn_att_src, L3_gnn_att_dst, L3_gnn_bias, L3_gnn_gamma, L3_gnn_beta):
    import jax
    import jax.numpy as jnp

    def _L0_gnn_ref(node_features, edge_index, Wp, a_src, a_trg, Wskip, bias):
        import jax, jax.numpy as jnp
        import numpy as np
        N, E, FIN, H, FO = (6250, 100000, 256, 8, 32)
        x = node_features
        src, trg = (edge_index[0], edge_index[1])
        proj = (x @ Wp.T).reshape(-1, H, FO)
        scores_src = jnp.sum(proj * a_src, axis=-1)
        scores_trg = jnp.sum(proj * a_trg, axis=-1)
        s = scores_src[src] + scores_trg[trg]
        s = jax.nn.leaky_relu(s, negative_slope=0.2)
        s = s - jnp.max(s)
        exp_s = jnp.exp(s)
        denom = jax.ops.segment_sum(exp_s, trg, num_segments=N)
        attn = exp_s / (denom[trg] + 1e-16)
        weighted = proj[src] * attn[:, :, None]
        out = jax.ops.segment_sum(weighted, trg, num_segments=N)
        out = out + (x @ Wskip.T).reshape(-1, H, FO)
        out = out.reshape(-1, H * FO) + bias
        return jax.nn.elu(out)

    def _L1_gnn_ref(x, edge_index, W_l1, b_l1, W_r1, ln1_g, ln1_b, W_l2, b_l2, W_r2, ln2_g, ln2_b):
        import jax, jax.numpy as jnp
        import numpy as np
        N_NODES = 6250
        LN_EPS = 1e-05

        def _sage_conv(x, src, dst, W_l, b_l, W_r):
            msg_sum = jax.ops.segment_sum(x[src], dst, num_segments=N_NODES)
            cnt = jax.ops.segment_sum(jnp.ones((src.shape[0],), x.dtype), dst, num_segments=N_NODES)
            mean = msg_sum / jnp.maximum(cnt, 1.0)[:, None]
            return mean @ W_l + b_l + x @ W_r

        def _layer_norm(x, g, b):
            mu = jnp.mean(x, axis=-1, keepdims=True)
            var = jnp.mean(jnp.square(x - mu), axis=-1, keepdims=True)
            return (x - mu) * jax.lax.rsqrt(var + LN_EPS) * g + b
        src, dst = (edge_index[0], edge_index[1])
        h = _sage_conv(x, src, dst, W_l1, b_l1, W_r1)
        h = jax.nn.relu(_layer_norm(h, ln1_g, ln1_b))
        h = _sage_conv(h, src, dst, W_l2, b_l2, W_r2)
        h = jax.nn.relu(_layer_norm(h, ln2_g, ln2_b))
        return h

    def _L2_gnn_ref(embeds, W_heads, b_heads, a_heads, g_heads, beta_heads, W_out, b_out, a_out, g_out, beta_out, edge_index):
        import jax, jax.numpy as jnp
        import numpy as np
        ALPHA = 0.2
        LN_EPS = 1e-05

        def _gat_layer(x, src, dst, W, b, a, g, beta, N, concat):
            h = x @ W.T + b
            d = W.shape[0]
            s_src = h @ a[:d]
            s_dst = h @ a[d:]
            score = s_src[src] + s_dst[dst]
            e = jnp.exp(-jax.nn.leaky_relu(score, ALPHA))
            h_prime = jax.ops.segment_sum(e[:, None] * h[dst], src, num_segments=N)
            mu = jnp.mean(h_prime, axis=-1, keepdims=True)
            var = jnp.var(h_prime, axis=-1, keepdims=True)
            h_prime = (h_prime - mu) * jax.lax.rsqrt(var + LN_EPS) * g + beta
            return jax.nn.elu(h_prime) if concat else h_prime
        N = embeds.shape[0]
        src, dst = (edge_index[0], edge_index[1])
        H = W_heads.shape[0]
        heads = [_gat_layer(embeds, src, dst, W_heads[i], b_heads[i], a_heads[i], g_heads[i], beta_heads[i], N, concat=True) for i in range(H)]
        x = jnp.concatenate(heads, axis=1)
        out = _gat_layer(x, src, dst, W_out, b_out, a_out, g_out, beta_out, N, concat=False)
        return jax.nn.elu(out)

    def _L3_gnn_ref(x, edge_index, W, att_src, att_dst, bias, gamma, beta):
        import jax, jax.numpy as jnp
        import numpy as np
        N = 6250
        E = 100000
        H = 256
        HEADS = 4
        OUT = H // HEADS
        NEG_SLOPE = 0.2
        EPS = 1e-05
        n = x.shape[0]
        loop = jnp.arange(n, dtype=edge_index.dtype)
        src = jnp.concatenate([edge_index[0], loop])
        dst = jnp.concatenate([edge_index[1], loop])
        h = (x @ W).reshape(n, HEADS, OUT)
        a_s = jnp.einsum('nhd,hd->nh', h, att_src)
        a_d = jnp.einsum('nhd,hd->nh', h, att_dst)
        alpha = jax.nn.leaky_relu(a_s[src] + a_d[dst], NEG_SLOPE)
        amax = jax.ops.segment_max(alpha, dst, num_segments=n)
        ex = jnp.exp(alpha - amax[dst])
        denom = jax.ops.segment_sum(ex, dst, num_segments=n)
        coef = ex / denom[dst]
        msg = coef[:, :, None] * h[src]
        agg = jax.ops.segment_sum(msg, dst, num_segments=n)
        out = agg.reshape(n, H) + bias
        out = jax.nn.relu(out)
        y = out + x
        mu = jnp.mean(y, axis=-1, keepdims=True)
        var = jnp.var(y, axis=-1, keepdims=True)
        return (y - mu) * jax.lax.rsqrt(var + EPS) * gamma + beta
    edge_index = jnp.stack([src, dst])
    x = _layernorm(x + _L0_gnn_ref(x, edge_index, L0_gnn_Wp, L0_gnn_a_src, L0_gnn_a_trg, L0_gnn_Wskip, L0_gnn_bias), axis=-1)
    x = _layernorm(x + _L1_gnn_ref(x, edge_index, L1_gnn_W_l1, L1_gnn_b_l1, L1_gnn_W_r1, L1_gnn_ln1_g, L1_gnn_ln1_b, L1_gnn_W_l2, L1_gnn_b_l2, L1_gnn_W_r2, L1_gnn_ln2_g, L1_gnn_ln2_b), axis=-1)
    x = _layernorm(x + _L2_gnn_ref(x, L2_gnn_W_heads, L2_gnn_b_heads, L2_gnn_a_heads, L2_gnn_g_heads, L2_gnn_beta_heads, L2_gnn_W_out, L2_gnn_b_out, L2_gnn_a_out, L2_gnn_g_out, L2_gnn_beta_out, edge_index), axis=-1)
    x = _layernorm(x + _L3_gnn_ref(x, edge_index, L3_gnn_W, L3_gnn_att_src, L3_gnn_att_dst, L3_gnn_bias, L3_gnn_gamma, L3_gnn_beta), axis=-1)
    return x

_drawn_inputs = setup_inputs


def setup_inputs(seed=0):
    import zlib

    import numpy as np

    out = dict(_drawn_inputs(seed))
    spreads = {'L0_gnn_bias': (0.0, 0.1),
     'L1_gnn_b_l1': (0.0, 0.1),
     'L1_gnn_ln1_g': (1.0, 0.2),
     'L1_gnn_ln1_b': (0.0, 0.1),
     'L1_gnn_b_l2': (0.0, 0.1),
     'L1_gnn_ln2_g': (1.0, 0.2),
     'L1_gnn_ln2_b': (0.0, 0.1),
     'L2_gnn_g_heads': (1.0, 0.2),
     'L2_gnn_beta_heads': (0.0, 0.1),
     'L2_gnn_g_out': (1.0, 0.2),
     'L2_gnn_beta_out': (0.0, 0.1),
     'L3_gnn_bias': (0.0, 0.1),
     'L3_gnn_gamma': (1.0, 0.2),
     'L3_gnn_beta': (0.0, 0.1)}
    factors = {'L0_gnn_a_trg': 2.888,
     'L2_gnn_a_heads': 7.461,
     'L2_gnn_a_out': 8.0,
     'L3_gnn_att_src': 3.609,
     'L3_gnn_att_dst': 8.0}
    for name, (base, spread) in spreads.items():
        noise = np.random.default_rng([zlib.crc32(name.encode()), seed]).standard_normal(out[name].shape)
        drawn = base * np.exp(spread * noise) if base else spread * noise
        out[name] = jnp.asarray(drawn.astype(out[name].dtype))
    for name, factor in factors.items():
        out[name] = (out[name] * factor).astype(out[name].dtype)
    return out
```

```python
from contextlib import ExitStack

import concourse.bass as bass
from concourse import mybir

F32 = mybir.dt.float32
BF16 = mybir.dt.bfloat16
I32 = mybir.dt.int32
ALU = mybir.AluOpType
ACT = mybir.ActivationFunctionType
AX_X = mybir.AxisListType.X
RMAX = bass.bass_isa.ReduceOp.max

P = 128
N_NODES = 6250
N_EDGES = 100000
D = 256
NB = -(-N_NODES // P)
NP = NB * P
EP = 125
EC = N_EDGES // EP
G = 2
C = 4
U = 4
GC = C // G
GB = GC * U
GROUPS = -(-((N_EDGES + NB * (G * P - 1)) // (G * P)) // GB) * GB
CHUNKS = GROUPS // GC
BODIES = CHUNKS // U
TILES = GROUPS * G
TILES_P = TILES + C
TG = GC + GROUPS + GB
SC = 8
STAGES = EC // SC
KB = 7
BATCHES = NB // KB
BIG = 1.0e30
LN_EPS = 1e-5
SLOPE = 0.2
EMPTY = 200


class Shared:
    pass


class Tally:

    def __init__(self, start):
        self.start = start
        self.value = start
        self.n = 0
        self.per_turn = 0

    def turn(self, i):
        if isinstance(i, int):
            self.start, self.value = self.value + self.n, self.value + self.n
        else:
            self.per_turn = self.n
            self.value = self.start + i * self.per_turn
        self.n = 0

    def next(self):
        self.n += 1
        return self.value + self.n

    def after(self, turns):
        assert self.n == self.per_turn
        self.value, self.n = self.start + turns * self.per_turn, 0


def wait(eng, sem, value):
    if isinstance(value, int) and value <= 0:
        return
    eng.wait_ge(sem, value)


def turns(eng, n, body):
    body(0)
    with eng.Fori(1, n) as i:
        body(i)


def wide(ap, shape):
    return ap.to_broadcast(shape)


def place_edges(nc, m, way, key, other):
    sc = ExitStack()
    with sc:
        def sb(name, shape, dt=F32):
            return sc.enter_context(nc.sbuf_tensor(f"{name}_{way}", shape, dt))

        def ps(name):
            return sc.enter_context(nc.psum_tensor(f"{name}_{way}", [P, 512], F32))

        key_i = sb("key_i", [EP, EC], I32)
        other_i = sb("other_i", [EP, EC], I32)
        tile_i = sb("tile_i", [EP, EC], I32)
        slotted = sb("slotted", [EP, EC, 3], I32)
        blk = sb("blk", [EP, EC], BF16)
        zero = sb("zero", [EP, EC], BF16)
        count = sb("count", [EP, EC])
        chosen = sb("chosen", [EP, EC])
        rank = sb("rank", [EP, EC])
        member = m.acc[:].bitcast(BF16)[0:EP, 0:NB * EC]
        below = sb("below", [P, P])
        total = sb("total", [EP, NB])
        groups_i = sb("groups_i", [P, NB], I32)
        groups_f = sb("groups_f", [P, NB])
        group_end = sb("group_end", [P, NB])
        zeros_b = sb("zeros_b", [P, NB])
        first = sb("first", [EP, NB])
        end_col = sb("end_col", [P, 1])
        group_i = sb("group_i", [NB, GROUPS], I32)
        passed = sb("passed", [NB, GROUPS])
        block_f = sb("block_f", [1, GROUPS])
        fill = sb("fill", [P, TILES_P, 2], I32)
        stage = sb("stage", [EP, 2, SC, 3], I32)
        ps_before, ps_total, ps_end, ps_group = ps("ps_before"), ps("ps_total"), ps("ps_end"), ps("ps_group")
        chain0 = m.at["vec"]

        with nc.Block() as block:
            @block.sync
            def _(sp):
                sp.dma_start(key_i[:], key.rearrange("(p e) -> p e", e=EC)).then_inc(m.loaded, 16)
                sp.dma_start(other_i[:], other.rearrange("(p e) -> p e", e=EC)).then_inc(m.loaded, 16)
                sp.wait_ge(m.fill_made, 2 * (way + 1))
                sp.dma_start(m.meta[way].rearrange("(p t) k -> p (t k)", p=P),
                             fill[:].rearrange("p t k -> p (t k)")).then_inc(m.prefilled, 16)
                sp.wait_ge(m.prefilled, 16 * (way + 1))

            @block.gpsimd
            def _(pool):
                pool.iota(group_i[:], pattern=[[1, GROUPS]], base=0, channel_multiplier=0).then_inc(m.numbered, 1)
                pool.wait_ge(m.prefilled, 16 * (way + 1))

                def part(i):
                    for h in range(2):
                        pool.wait_ge(m.staged, way * STAGES + 2 * i + h + 1)
                        pool.sem_inc(m.pool_passed, 1)
                        for j in range(SC):
                            pool.indirect_dma_start(
                                m.meta[way], bass.IndirectOffsetOnAxis(ap=stage[:, h, j, 0:1], axis=0),
                                stage[:, h, j, 1:3], None).then_inc(m.scattered[h], 16)

                turns(pool, STAGES // 2, part)
                for h in range(2):
                    pool.wait_ge(m.scattered[h], 16 * SC * (STAGES // 2) * (way + 1))

            @block.scalar
            def _(act):
                act.wait_ge(m.slotted, way + 1)

                def part(i):
                    for h in range(2):
                        wait(act, m.scattered[h], 16 * SC * ((STAGES // 2) * way + i))
                        act.copy(stage[:, h, :, :], slotted[:, bass.ds((2 * i + h) * SC, SC), :]).then_inc(m.staged, 1)

                turns(act, STAGES // 2, part)

            @block.tensor
            def _(pe):
                pe.wait_ge(m.counted, way + 1)
                pe.matmul(ps_before[0:EP, 0:NB], below[0:EP, 0:EP], total[:], start=True, stop=True)
                pe.matmul(ps_total[:, 0:NB], m.ones[0:EP, :], total[:], start=True, stop=True).then_inc(m.summed_up, 1)
                pe.wait_ge(m.ended, 2 * way + 1)
                pe.matmul(ps_end[0:NB, 0:1], group_end[0:1, 0:NB], m.ones[0:1, 0:1], start=True, stop=True).then_inc(m.summed_up, 1)
                pe.wait_ge(m.ended, 2 * way + 2)
                pe.matmul(ps_group[0:1, 0:GROUPS], m.ones[0:NB, 0:1], passed[:], start=True, stop=True).then_inc(m.summed_up, 1)

            @block.vector
            def _(dve):
                chain = Tally(chain0)

                def settled(ins):
                    ins.then_inc(m.vec_step, 1)
                    dve.wait_ge(m.vec_step, chain.next())

                dve.memset(fill[:, :, 0:1], 0).then_inc(m.fill_made, 1)
                dve.memset(fill[:, :, 1:2], EMPTY).then_inc(m.fill_made, 1)
                dve.memset(zero[:], 0.0)
                dve.memset(zeros_b[:], 0.0)
                dve.memset(rank[:], 0.0)
                dve.memset(m.group_block[way][:], 0)
                dve.tensor_scalar(below[:], m.iota_row[:], m.part_col[:, 0:1], None, ALU.is_gt)
                dve.wait_ge(m.loaded, 32 * (way + 1))
                dve.tensor_copy(slotted[:, :, 1], other_i[:])
                dve.tensor_scalar(slotted[:, :, 2], key_i[:], P - 1, None, ALU.bitwise_and)
                settled(dve.tensor_scalar(tile_i[:], key_i[:], 7, None, ALU.logical_shift_right))
                settled(dve.tensor_copy(blk[:], tile_i[:]))

                head = chain.value + chain.n
                with dve.Fori(0, NB) as b:
                    dve.tensor_scalar(member[:, bass.ds(b * EC, EC)], blk[:], m.iota_row[0:EP, bass.ds(b, 1)], 0.0,
                                      ALU.is_equal, ALU.add, accum_out=total[:, bass.ds(b, 1)]).then_inc(m.vec_step, 1)
                chain = Tally(head + NB)
                dve.wait_ge(m.vec_step, head + NB)
                dve.memset(m.mark[:], 0.0).then_inc(m.counted, 1)

                dve.wait_ge(m.summed_up, 3 * way + 1)
                settled(dve.tensor_scalar(groups_f[:], ps_total[:, 0:NB], float(G * P - 1), None, ALU.add))
                settled(dve.tensor_copy(groups_i[:], groups_f[:]))
                settled(dve.tensor_scalar(groups_i[:], groups_i[:], 8, None, ALU.logical_shift_right))
                settled(dve.tensor_copy(groups_f[:], groups_i[:]))
                dve.tensor_tensor_scan(group_end[:], groups_f[:], zeros_b[:], 0.0, ALU.add, ALU.add).then_inc(m.ended, 1)
                dve.wait_ge(m.ended, 2 * way + 1)
                settled(dve.tensor_tensor(groups_f[:], group_end[:], groups_f[:], ALU.subtract))
                settled(dve.scalar_tensor_tensor(first[:], groups_f[0:EP, :], float(G * P), ps_before[0:EP, 0:NB], ALU.mult, ALU.add))
                settled(dve.tensor_scalar(first[:], first[:], -1.0, None, ALU.add))

                dve.wait_ge(m.summed_up, 3 * way + 2)
                settled(dve.tensor_copy(end_col[0:NB, :], ps_end[0:NB, 0:1]))
                dve.wait_ge(m.numbered, way + 1)
                settled(dve.tensor_copy(passed[:], group_i[:]))
                dve.tensor_scalar(passed[:], passed[:], end_col[0:NB, 0:1], None, ALU.is_ge).then_inc(m.ended, 1)
                dve.wait_ge(m.summed_up, 3 * way + 3)
                settled(dve.tensor_scalar(block_f[:], ps_group[0:1, 0:GROUPS], float(NB - 1), None, ALU.min))
                settled(dve.tensor_copy(m.group_block[way][0:1, GC:GC + GROUPS], block_f[:]))

                head = chain.value + chain.n
                with dve.Fori(0, NB) as b:
                    dve.tensor_tensor_scan(count[:], member[:, bass.ds(b * EC, EC)], zero[:], first[:, bass.ds(b, 1)], ALU.add, ALU.add).then_inc(m.vec_step, 1)
                    dve.wait_ge(m.vec_step, head + 3 * b + 1)
                    dve.tensor_tensor(chosen[:], count[:], member[:, bass.ds(b * EC, EC)], ALU.mult).then_inc(m.vec_step, 1)
                    dve.wait_ge(m.vec_step, head + 3 * b + 2)
                    dve.tensor_tensor(rank[:], rank[:], chosen[:], ALU.add).then_inc(m.vec_step, 1)
                    dve.wait_ge(m.vec_step, head + 3 * b + 3)
                chain = Tally(head + 3 * NB)

                settled(dve.tensor_copy(key_i[:], rank[:]))
                settled(dve.tensor_scalar(tile_i[:], key_i[:], 7, None, ALU.logical_shift_right))
                settled(dve.tensor_scalar(key_i[:], key_i[:], P - 1, None, ALU.bitwise_and))
                settled(dve.tensor_scalar(count[:], key_i[:], float(TILES_P), None, ALU.mult))
                dve.tensor_tensor(slotted[:, :, 0], count[:], tile_i[:], ALU.add).then_inc(m.slotted, 1)
                dve.wait_ge(m.slotted, way + 1)
                m.at["vec"] = chain.value + chain.n


def edge_phase(nc, m, way, table, width, feat, heads, own, mode):
    sc = ExitStack()
    summed_cols = feat if mode in ("sum", "neg") else width
    acc = m.acc[:, 0:NB * summed_cols].rearrange("p (b w) -> p b w", w=summed_cols)
    m.acc_view = acc
    weights = mode != "sum"
    T = m.T[table]
    at = dict(m.at)
    hw = feat // heads if heads else 0
    with sc:
        def sb(name, shape, dt=F32):
            return sc.enter_context(nc.sbuf_tensor(f"{name}_{table}", shape, dt))

        slots = sb("slots", [P, U, C, 2], I32)
        rows = sb("rows", [P, U, C, width])
        node = sb("node", [P, 2, C])
        onehot = sb("onehot", [P, 2, C, P])
        turned = sb("turned", [P, 2, C, P])
        raw = sb("raw", [P, 2, C, 8])
        score = sb("score", [P, 2, C, 8])
        pad = sb("pad", [P, 2, C])
        ps_turned = [sc.enter_context(nc.psum_tensor(f"ps_turned{k}_{table}", [P, C, P], F32)) for k in range(2)]
        ps_own = [sc.enter_context(nc.psum_tensor(f"ps_own{k}_{table}", [P, 512], F32)) for k in range(2)]
        ps_sum = [sc.enter_context(nc.psum_tensor(f"ps_sum{k}_{table}", [P, 512], F32)) for k in range(2 * GC)]
        c0, a0, w0, g0 = at["onehots"], at["ahead"], at["wchunk"], at["chunk"] * GC
        iota_b = m.iota_row[:].rearrange("p (c n) -> p c n", c=1).to_broadcast([P, C, P])

        with nc.Block() as block:
            @block.sync
            def _(sp):
                def body(i):
                    for u in range(U):
                        if isinstance(i, int):
                            sp.dma_start(slots[:, u, :, :],
                                         m.meta[way].rearrange("(p t) k -> p t k", p=P)[:, u * C:(u + 1) * C, :]).then_inc(m.slots_in[u], 16)
                        else:
                            sp.wait_ge(m.summed, g0 + GC * (U * i + u - U + 1))
                            sp.dma_start(slots[:, u, :, :],
                                         m.meta[way].rearrange("(p t) k -> p t k", p=P)[:, bass.ds((U * i + u) * C, C), :]).then_inc(m.slots_in[u], 16)

                turns(sp, BODIES, body)
                sp.wait_ge(m.summed, g0 + GC * (CHUNKS - U + 1))
                sp.dma_start(slots[:, 0, :, :],
                             m.meta[way].rearrange("(p t) k -> p t k", p=P)[:, CHUNKS * C:(CHUNKS + 1) * C, :]).then_inc(m.slots_in[0], 16)

            @block.gpsimd
            def _(pool):
                def body(i):
                    for u in range(U):
                        if not isinstance(i, int):
                            pool.wait_ge(m.summed, g0 + GC * (U * i + u - U + 1))
                        pool.wait_ge(m.slots_in[u], at[f"slots{u}"] + 16 * (i + 1))
                        pool.sem_inc(m.pool_passed, 1)
                        for j in range(C):
                            pool.indirect_dma_start(
                                rows[:, u, j, :], None, T,
                                bass.IndirectOffsetOnAxis(ap=slots[:, u, j, 0:1], axis=0)).then_inc(m.gathered[u], 16)

                turns(pool, BODIES, body)
                for u in range(U):
                    pool.wait_ge(m.gathered[u], at["gathered"] + 16 * C * BODIES)

            @block.scalar
            def _(act):
                if not weights:
                    return

                def copy_turned(n, k):
                    act.wait_ge(m.onehot_turned, a0 + n + 1)
                    act.copy(turned[:, k, :, :], ps_turned[k][:]).then_inc(m.onehot_copied, 1)

                copy_turned(0, 0)

                def body(i):
                    for u in range(U):
                        n, k = U * i + u, u % 2
                        act.wait_ge(m.scored, w0 + n + 1)
                        if mode in ("gat", "shift"):
                            out = rows[:, u, :, feat:feat + heads]
                        else:
                            out = raw[:, k, :, 0:heads]
                        act.activation(out, score[:, k, :, 0:heads], ACT.Exp,
                                       bias=m.neg_bound[:, 0:1] if mode == "gat" else 0.0,
                                       scale=-1.0 if mode == "neg" else 1.0).then_inc(m.exped, 1)
                        copy_turned(n + 1, 1 - k)

                turns(act, BODIES, body)

            @block.tensor
            def _(pe):
                regs = [pe.alloc_register(f"pe_block{q}_{table}") for q in range(GB)]

                def own_scores(n, k, blocks):
                    pe.wait_ge(m.onehot_built, c0 + n + 1)
                    if not (isinstance(n, int) and n < 2):
                        pe.wait_ge(m.onehot_copied, a0 + n - 1)
                    for j in range(C):
                        last = pe.transpose(ps_turned[k][:, j, :], onehot[:, k, j, :], m.ident[:])
                    last.then_inc(m.onehot_turned, 1)
                    pe.wait_ge(m.onehot_copied, a0 + n + 1)
                    if not (isinstance(n, int) and n < 2):
                        pe.wait_ge(m.scored, w0 + n - 1)
                    for j in range(C):
                        last = pe.matmul(ps_own[k][:, j * 8:j * 8 + own], turned[:, k, j, :],
                                         m.sall[:, bass.ds(blocks[j // G], 1), 8:8 + own],
                                         start=True, stop=True)
                    last.then_inc(m.own_scored, 1)

                def load_blocks(start):
                    pe.reg_load(regs, m.group_block[way][0:1, bass.ds(start, GB)])
                    return [pe.snap(r, min_val=0, max_val=NB - 1) for r in regs]

                if weights:
                    own_scores(0, 0, load_blocks(GC))

                def body(i):
                    if weights:
                        blocks = load_blocks(GB * i + 2 * GC)
                    for u in range(U):
                        n, k = U * i + u, u % 2
                        if weights:
                            own_scores(n + 1, 1 - k, blocks[GC * u:GC * u + GC])
                            pe.wait_ge(m.weighted, w0 + n + 1)
                        else:
                            pe.wait_ge(m.onehot_built, c0 + n + 1)
                            pe.wait_ge(m.gathered[u], at["gathered"] + 16 * C * (i + 1))
                        for q in range(GC):
                            s = GC * k + q
                            if not (isinstance(n, int) and n < 2):
                                pe.wait_ge(m.added, g0 + GC * (n - 2) + q + 1)
                            for j in range(G):
                                last = pe.matmul(ps_sum[s][:, 0:summed_cols], onehot[:, k, G * q + j, :],
                                                 rows[:, u, G * q + j, 0:summed_cols],
                                                 start=(j == 0), stop=(j == G - 1))
                            last.then_inc(m.summed, 1)

                turns(pe, BODIES, body)

            @block.vector
            def _(dve):
                regs = [dve.alloc_register(f"dve_block{q}_{table}") for q in range(GB)]
                chain = Tally(at["vec"])

                def settled(ins):
                    ins.then_inc(m.vec_step, 1)
                    dve.wait_ge(m.vec_step, chain.next())

                def build_onehot(n, k, u, fetched):
                    dve.wait_ge(m.slots_in[u], fetched)
                    if not (isinstance(n, int) and n < 2):
                        dve.wait_ge(m.summed, g0 + GC * (n - 1))
                    settled(dve.tensor_copy(node[:, k, :], slots[:, u, :, 1]))
                    if weights:
                        dve.tensor_scalar(pad[:, k, :], node[:, k, :], float(P), BIG if mode == "neg" else -BIG,
                                          ALU.is_ge, ALU.mult).then_inc(m.padded, 1)
                    dve.tensor_tensor(onehot[:, k, :, :], iota_b, wide(node[:, k, :].rearrange("p (c n) -> p c n", n=1), [P, C, P]),
                                      ALU.is_equal).then_inc(m.onehot_built, 1)

                def scores(n, k, u, i):
                    dve.wait_ge(m.own_scored, a0 + n + 1)
                    dve.wait_ge(m.gathered[u], at["gathered"] + 16 * C * (i + 1))
                    if not (isinstance(n, int) and n < 2):
                        dve.wait_ge(m.exped, w0 + n - 1)
                    mine = ps_own[k][:, 0:C * 8].rearrange("p (c h) -> p c h", h=8)
                    r, s = raw[:, k, :, 0:heads], score[:, k, :, 0:heads]
                    settled(dve.tensor_tensor(r, mine[:, :, 0:heads], rows[:, u, :, feat:feat + heads], ALU.add))
                    settled(dve.scalar_tensor_tensor(s, r, SLOPE, r, ALU.mult, ALU.max))
                    dve.wait_ge(m.padded, a0 + n + 1)
                    pads = wide(pad[:, k, :].rearrange("p (c n) -> p c n", n=1), [P, C, heads])
                    if mode == "shift":
                        settled(dve.tensor_tensor(s, s, mine[:, :, heads:2 * heads], ALU.subtract))
                    ins = dve.tensor_tensor(s, s, pads, ALU.add)
                    if mode == "gat":
                        settled(ins)
                        best = m.score_max[:].rearrange("p (c h) -> p c h", h=8)
                        dve.tensor_tensor(best, best, s, ALU.max).then_inc(m.scored, 1)
                    else:
                        ins.then_inc(m.scored, 1)

                def weigh(n, k, u):
                    dve.wait_ge(m.exped, w0 + n + 1)
                    w = rows[:, u, :, feat:feat + heads] if mode in ("gat", "shift") else raw[:, k, :, 0:heads]
                    for j in range(C):
                        r = rows[:, u, j, 0:feat].rearrange("p (h w) -> p h w", w=hw)
                        ins = dve.tensor_tensor(r, r, wide(w[:, j, :].rearrange("p (h w) -> p h w", w=1), [P, heads, hw]), ALU.mult)
                    ins.then_inc(m.weighted, 1)

                def add_sums(n, k, blocks):
                    for q in range(GC):
                        dve.wait_ge(m.summed, g0 + GC * n + q + 1)
                        wait(dve, m.added, g0 + GC * n + q)
                        place = acc[:, bass.ds(blocks[q], 1), :]
                        dve.tensor_tensor(place, place, ps_sum[GC * k + q][:, 0:summed_cols].rearrange("p (b w) -> p b w", b=1),
                                          ALU.add).then_inc(m.added, 1)

                def load_blocks(start):
                    dve.reg_load(regs, m.group_block[way][0:1, bass.ds(start, GB)])
                    return [dve.snap(r, min_val=0, max_val=NB - 1) for r in regs]

                settled(dve.memset(m.acc[:, 0:NB * summed_cols], 0.0))
                build_onehot(0, 0, 0, at["slots0"] + 16)
                def body(i):
                    chain.turn(i)
                    blocks = load_blocks(GB * i)
                    for u in range(U):
                        n, k = U * i + u, u % 2
                        if weights:
                            scores(n, k, u, i)
                        ahead = (u + 1) % U
                        build_onehot(n + 1, 1 - k, ahead, at[f"slots{ahead}"] + 16 * (i + 1 + (u + 1) // U))
                        if weights:
                            weigh(n, k, u)
                        if not (isinstance(n, int) and n == 0):
                            add_sums(n - 1, 1 - k, blocks[GC * u:GC * u + GC])

                turns(dve, BODIES, body)
                chain.after(BODIES)
                add_sums(CHUNKS - 1, 1, load_blocks(GROUPS))
                dve.wait_ge(m.added, g0 + GROUPS)
                m.at["vec"] = chain.value

    m.at["chunk"] += CHUNKS
    m.at["onehots"] += CHUNKS + 1
    if weights:
        m.at["wchunk"] += CHUNKS
        m.at["ahead"] += CHUNKS + 1
    m.at["gathered"] += 16 * C * BODIES
    for u in range(U):
        m.at[f"slots{u}"] += 16 * (BODIES + (u == 0))


def make_products(pe, m, ph, p, tiles, w, cols):
    def turned(kb):
        wait(pe, m.x_copied, p + kb - (kb > 0))
        parts = tiles(kb)
        for c, part in enumerate(parts):
            last = pe.transpose(ph.ps_x[kb % 2][:, c * P:(c + 1) * P], part, m.ident[:])
        last.then_inc(m.x_turned, 1)
        return len(parts)

    n = turned(0)
    for kb in range(KB):
        if kb + 1 < KB:
            turned(kb + 1)
        pe.wait_ge(m.x_copied, p + kb + 1)
        wait(pe, m.product_taken, p + kb - (kb > 0))
        for c in range(n):
            for a in range(0, cols, 512):
                b = min(a + 512, cols)
                last = pe.matmul(ph.ps_y[kb % 2][:, a:b], ph.xT[:, kb % 2, c * P:(c + 1) * P], w[:, c, a:b],
                                 start=(c == 0), stop=(c == n - 1))
        last.then_inc(m.product, 1)


def copy_turned(act, m, ph, p, n):
    for kb in range(KB):
        act.wait_ge(m.x_turned, p + kb + 1)
        wait(act, m.product, p + kb - (kb > 0))
        act.copy(ph.xT[:, kb % 2, 0:n * P], ph.ps_x[kb % 2][:, 0:n * P]).then_inc(m.x_copied, 1)


def take_products(dve, m, ph, p, take):
    for kb in range(KB):
        dve.wait_ge(m.product, p + kb + 1)
        take(kb, ph.ps_y[kb % 2]).then_inc(m.product_taken, 1)


def normalize(dve, m, ph, v, y):
    for kb in range(KB):
        last = dve.bn_stats(ph.stats[:, kb, :], y[:, kb, :])
    v.settled(last)
    st, s = ph.stats, ph.small
    dve.tensor_tensor(s[:, :, 0], st[:, :, 1], st[:, :, 4], ALU.add)
    dve.tensor_tensor(s[:, :, 1], st[:, :, 1], st[:, :, 4], ALU.subtract)
    v.settled(dve.tensor_tensor(s[:, :, 2], st[:, :, 2], st[:, :, 5], ALU.add))
    dve.tensor_scalar(s[:, :, 3], s[:, :, 0], -0.5, None, ALU.mult)
    v.settled(dve.scalar_tensor_tensor(s[:, :, 4], s[:, :, 1], 0.25, s[:, :, 1], ALU.mult, ALU.mult))
    v.settled(dve.scalar_tensor_tensor(s[:, :, 5], s[:, :, 2], 1.0 / D, s[:, :, 4], ALU.mult, ALU.add))
    v.hand_over(dve.tensor_scalar(s[:, :, 6], s[:, :, 5], LN_EPS, None, ALU.add))
    v.take_over()
    v.settled(dve.reciprocal(s[:, :, 0], s[:, :, 7]))
    for kb in range(KB):
        last = dve.tensor_scalar(y[:, kb, :], y[:, kb, :], s[:, kb, 3:4], s[:, kb, 0:1], ALU.add, ALU.mult)
    v.settled(last)


def root(act, m, ph, a):
    a.take_over()
    a.hand_over(act.activation(ph.small[:, :, 7], ph.small[:, :, 6], ACT.Sqrt))


def elu_parts(act, m, a, z, e):
    a.take_over()
    a.settled(act.activation(e, z, ACT.Relu, scale=-1.0))
    a.settled(act.activation(e, e, ACT.Exp, scale=-1.0))
    a.hand_over(act.activation(z, z, ACT.Relu))


class Hand:

    def __init__(self, eng, own, out, into, at_own, at_out, at_in):
        self.eng, self.own, self.out, self.into = eng, own, out, into
        self.steps, self.outs, self.ins = Tally(at_own), Tally(at_out), Tally(at_in)

    def settled(self, ins):
        ins.then_inc(self.own, 1)
        self.eng.wait_ge(self.own, self.steps.next())

    def hand_over(self, ins):
        ins.then_inc(self.out, 1)
        self.outs.next()

    def take_over(self):
        self.eng.wait_ge(self.into, self.ins.next())

    def turn(self, i):
        for t in (self.steps, self.outs, self.ins):
            t.turn(i)

    def after(self, turns):
        for t in (self.steps, self.outs, self.ins):
            t.after(turns)


def vector_side(dve, m):
    return Hand(dve, m.vec_step, m.for_act, m.for_vec, m.at["vec"], m.at["for_act"], m.at["for_vec"])


def scalar_side(act, m):
    return Hand(act, m.act_step, m.for_vec, m.for_act, m.at["act"], m.at["for_vec"], m.at["for_act"])


def rows_of(table, i):
    return table.rearrange("(b p) w -> p b w", p=P)[:, bass.ds(i * KB, KB), :]


def fold(pe, m, ps, rows, heads, n_rows, n_cols, count):
    for k in range(n_cols):
        for c in range(n_rows):
            last = pe.matmul(ps[:, k * 16:k * 16 + count], rows[:, c, k * P:(k + 1) * P], heads[:, c, 0:count],
                             start=(c == 0), stop=(c == n_rows - 1))
    return last


class NodePhase:

    def __init__(self, nc, m, name):
        self.nc, self.m, self.name = nc, m, name
        self.scope = ExitStack()

    def sb(self, name, shape, dt=F32):
        return self.scope.enter_context(self.nc.sbuf_tensor(f"{name}_{self.name}", shape, dt))

    def buffers(self, parts):
        self.stats = self.sb("stats", [P, KB, 6])
        self.small = self.sb("small", [P, KB, 8])
        self.xT = self.sb("xT", [P, 2, parts * P])
        self.ps_x = [self.scope.enter_context(self.nc.psum_tensor(f"ps_x{k}_{self.name}", [P, 512], F32)) for k in range(2)]
        self.ps_y = [self.scope.enter_context(self.nc.psum_tensor(f"ps_y{k}_{self.name}", [P, 1024], F32)) for k in range(2)]
        self.ps_f = self.scope.enter_context(self.nc.psum_tensor(f"ps_f_{self.name}", [P, 512], F32))

    def traffic(self, sp, weights, loads, stores):
        m = self.m
        for tile, src in weights:
            sp.dma_start(tile, src).then_inc(m.weights_in, 16)

        def body(i):
            for tile, table in loads:
                sp.dma_start(tile, rows_of(table, i)).then_inc(m.rows_in, 16)
            sp.wait_ge(m.rows_made, m.at["rows_made"] + i + 1)
            for tile, table in stores:
                sp.dma_start(rows_of(table, i), tile).then_inc(m.rows_out, 16)
            if stores:
                sp.wait_ge(m.rows_out, m.at["rows_out"] + 16 * len(stores) * (i + 1))
                sp.sem_inc(m.sync_passed, 1)

        turns(sp, BATCHES, body)

    def close(self, weights, loads, stores, products, for_pe, sides):
        at = self.m.at
        at["weights_in"] += 16 * len(weights)
        at["rows_in"] += 16 * len(loads) * BATCHES
        at["rows_out"] += 16 * len(stores) * BATCHES
        at["rows_made"] += BATCHES
        at["product"] += products * KB * BATCHES
        at["for_pe"] += for_pe * BATCHES
        v, a = sides
        at["vec"] = v.steps.value
        assert v.outs.value == (a.ins.value if a else v.outs.value)
        assert v.ins.value == (a.outs.value if a else v.ins.value)
        at["for_act"], at["for_vec"] = v.outs.value, v.ins.value
        if a:
            at["act"] = a.steps.value
        self.scope.close()


def per_block(row, shape):
    return row.rearrange("p (b w) -> p b w", b=1).to_broadcast(shape)


def per_row(col, shape):
    return col.rearrange("p (b w) -> p b w", w=1).to_broadcast(shape)


def on_all(row):
    return row.rearrange("(a n) -> a n", a=1).to_broadcast([P, row.shape[0]])


def chunks_of(w):
    return w.rearrange("(c p) n -> p c n", p=P)


def phase_0(nc, m, A):
    ph = NodePhase(nc, m, "n0")
    ph.buffers(2)
    x = ph.sb("x", [P, KB, D])
    rows = ph.sb("rows", [P, KB, D + 9])
    w = ph.sb("w", [P, 2, D + 16])
    wr = ph.sb("wr", [P, 2, D])
    heads = ph.sb("heads", [P, 2, 16])
    top = ph.sb("top", [P, 16])
    top_all = ph.sb("top_all", [P, 16])
    both = ph.sb("both", [P, 8])
    one = ph.sb("one", [P, 2])
    weights = [(w[:, :, 0:D], chunks_of(A["L0_WpT"])), (wr[:], chunks_of(A["L0_gnn_Wp"])), (heads[:], chunks_of(A["L0_heads"]))]
    loads, stores = [(x[:], A["x"])], [(rows[:], m.T[0])]
    at = dict(m.at)
    sides = [None, None]
    with nc.Block() as block:
        @block.sync
        def _(sp):
            ph.traffic(sp, weights, loads, stores)

        @block.tensor
        def _(pe):
            pe.wait_ge(m.weights_in, at["weights_in"] + 16 * len(weights))
            fold(pe, m, ph.ps_f, wr, heads, 2, 2, 16).then_inc(m.folded, 1)
            pe.wait_ge(m.fold_taken, at["fold"] + 1)

            def body(i):
                pe.wait_ge(m.rows_in, at["rows_in"] + 16 * (i + 1))
                make_products(pe, m, ph, at["product"] + KB * i, lambda kb: [x[:, kb, 0:P], x[:, kb, P:D]], w, D + 16)

            turns(pe, BATCHES, body)

        @block.scalar
        def _(act):
            turns(act, BATCHES, lambda i: copy_turned(act, m, ph, at["product"] + KB * i, 2))

        @block.vector
        def _(dve):
            v = sides[0] = vector_side(dve, m)
            dve.wait_ge(m.folded, at["fold"] + 1)
            dve.wait_ge(m.weights_in, at["weights_in"] + 16 * len(weights))
            dve.tensor_copy(w[:, :, D:D + 16], ph.ps_f[:, 0:32].rearrange("p (c h) -> p c h", h=16)).then_inc(m.fold_taken, 1)
            v.settled(dve.memset(rows[:, :, D + 8:D + 9], 1.0))

            def body(i):
                v.turn(i)
                dve.wait_ge(m.rows_in, at["rows_in"] + 16 * (i + 1))

                def take(kb, y):
                    dve.tensor_copy(m.sall[:, bass.ds(i * KB + kb, 1), :], y[:, D:D + 16].rearrange("p (b h) -> p b h", b=1))
                    return dve.tensor_copy(rows[:, kb, 0:D + 8], y[:, 0:D + 8])

                take_products(dve, m, ph, at["product"] + KB * i, take)
                dve.wait_ge(m.product_taken, at["product"] + KB * (i + 1))
                dve.memset(m.mark[:], 0.0).then_inc(m.rows_made, 1)

            turns(dve, BATCHES, body)
            v.after(BATCHES)
            dve.tensor_reduce(top[:], m.sall[:].rearrange("p b h -> p h b"), AX_X, ALU.max).then_inc(m.for_pool, 1)
            dve.wait_ge(m.from_pool, at["pool"] + 1)
            v.settled(dve.tensor_tensor(both[:], top_all[:, 0:8], top_all[:, 8:16], ALU.add))
            v.settled(dve.tensor_reduce(one[:, 0:1], both[:], AX_X, ALU.max))
            v.settled(dve.scalar_tensor_tensor(one[:, 1:2], one[:, 0:1], SLOPE, one[:, 0:1], ALU.mult, ALU.max))
            v.settled(dve.tensor_scalar(m.neg_bound[:], one[:, 1:2], -1.0, None, ALU.mult))
            v.turn(0)

        @block.gpsimd
        def _(pool):
            pool.wait_ge(m.for_pool, at["pool"] + 1)
            pool.partition_all_reduce(top_all[:], top[:], P, RMAX).then_inc(m.from_pool, 1)

    m.at["pool"] += 1
    m.at["fold"] += 1
    ph.close(weights, loads, stores, 1, 0, sides)


def phase_1(nc, m, A):
    ph = NodePhase(nc, m, "n1")
    ph.buffers(2)
    x = ph.sb("x", [P, KB, D])
    z = ph.sb("z", [P, KB, D])
    e = ph.sb("e", [P, KB, D])
    den = ph.sb("den", [P, KB, 8])
    w = ph.sb("w", [P, 2, D])
    bias = ph.sb("bias", [P, D])
    top = ph.sb("top", [P, 1])
    top_all = ph.sb("top_all", [P, 1])
    weights = [(w[:], chunks_of(A["L0_WskipT"])), (bias[:], on_all(A["L0_gnn_bias"]))]
    loads, stores = [(x[:], A["x"])], [(e[:], m.T[1])]
    at = dict(m.at)
    sides = [None, None]
    acc = m.acc_view
    with nc.Block() as block:
        @block.sync
        def _(sp):
            ph.traffic(sp, weights, loads, stores)

        @block.tensor
        def _(pe):
            pe.wait_ge(m.weights_in, at["weights_in"] + 16 * len(weights))

            def body(i):
                pe.wait_ge(m.rows_in, at["rows_in"] + 16 * (i + 1))
                make_products(pe, m, ph, at["product"] + KB * i, lambda kb: [x[:, kb, 0:P], x[:, kb, P:D]], w, D)

            turns(pe, BATCHES, body)

        @block.scalar
        def _(act):
            a = sides[1] = scalar_side(act, m)
            a.take_over()
            a.hand_over(act.activation(m.eps_col[:], top_all[:], ACT.Exp, bias=m.neg_bound[:, 0:1]))

            def body(i):
                a.turn(i)
                copy_turned(act, m, ph, at["product"] + KB * i, 2)
                elu_parts(act, m, a, z[:], e[:])
                root(act, m, ph, a)

            turns(act, BATCHES, body)
            a.after(BATCHES)

        @block.gpsimd
        def _(pool):
            pool.wait_ge(m.for_pool, at["pool"] + 1)
            pool.partition_all_reduce(top_all[:], top[:], P, RMAX).then_inc(m.from_pool, 1)

        @block.vector
        def _(dve):
            v = sides[0] = vector_side(dve, m)
            dve.tensor_reduce(top[:], m.score_max[:], AX_X, ALU.max).then_inc(m.for_pool, 1)
            dve.wait_ge(m.from_pool, at["pool"] + 1)
            v.hand_over(dve.memset(m.mark[:], 0.0))
            v.take_over()
            v.settled(dve.tensor_scalar(m.eps_col[:], m.eps_col[:], 1e-16, None, ALU.mult))
            v.settled(dve.tensor_scalar(m.rcnt[:], acc[:, :, D + 8], 1.0, None, ALU.max))
            v.settled(dve.reciprocal(m.rcnt[:], m.rcnt[:]))
            dve.wait_ge(m.weights_in, at["weights_in"] + 16 * len(weights))

            def body(i):
                v.turn(i)
                dve.wait_ge(m.rows_in, at["rows_in"] + 16 * (i + 1))
                v.settled(dve.tensor_scalar(den[:], acc[:, bass.ds(i * KB, KB), D:D + 8], m.eps_col[:, 0:1], None, ALU.add))
                v.settled(dve.reciprocal(den[:], den[:]))
                for kb in range(KB):
                    last = dve.tensor_tensor(z[:, kb, :].rearrange("p (h w) -> p h w", h=8),
                                             acc[:, bass.ds(i * KB + kb, 1), 0:D].rearrange("p b (h w) -> p (b h) w", h=8),
                                             den[:, kb, :].rearrange("p (h w) -> p h w", w=1).to_broadcast([P, 8, D // 8]), ALU.mult)
                v.settled(last)
                take_products(dve, m, ph, at["product"] + KB * i,
                              lambda kb, y: dve.tensor_tensor(z[:, kb, :], z[:, kb, :], y[:, 0:D], ALU.add))
                dve.wait_ge(m.product_taken, at["product"] + KB * (i + 1))
                v.hand_over(dve.tensor_tensor(z[:], z[:], per_block(bias[:], [P, KB, D]), ALU.add))
                v.take_over()
                v.settled(dve.scalar_tensor_tensor(e[:], e[:], -1.0, z[:], ALU.add, ALU.add))
                v.settled(dve.tensor_tensor(e[:], e[:], x[:], ALU.add))
                normalize(dve, m, ph, v, e)
                dve.memset(m.mark[:], 0.0).then_inc(m.rows_made, 1)

            turns(dve, BATCHES, body)
            v.after(BATCHES)

    m.at["pool"] += 1
    ph.close(weights, loads, stores, 1, 0, sides)


def phase_sage(nc, m, A, layer):
    last_one = layer == 2
    ph = NodePhase(nc, m, f"n{layer + 1}")
    ph.buffers(4)
    h = ph.sb("h", [P, KB, D])
    mean = ph.sb("mean", [P, KB, D])
    z = ph.sb("z", [P, KB, D])
    w = ph.sb("w", [P, 4, D])
    bias = ph.sb("bias", [P, 3, D])
    name = f"L1_gnn_"
    weights = [(w[:, 0:2, :], chunks_of(A[f"{name}W_l{layer}"])), (w[:, 2:4, :], chunks_of(A[f"{name}W_r{layer}"])),
               (bias[:, 0, :], on_all(A[f"{name}b_l{layer}"])), (bias[:, 1, :], on_all(A[f"{name}ln{layer}_g"])),
               (bias[:, 2, :], on_all(A[f"{name}ln{layer}_b"]))]
    loads, stores = [(h[:], m.T[layer])], [(z[:], m.T[2])]
    if last_one:
        F = 2 * D
        x1 = ph.sb("x1", [P, KB, D])
        w2 = ph.sb("w2", [P, 2, F + 16])
        wr2 = ph.sb("wr2", [P, 4, D])
        heads = ph.sb("heads", [P, 4, 16])
        bias2 = ph.sb("bias2", [P, F + 16])
        bcol = ph.sb("bcol", [P, 4])
        brep = ph.sb("brep", [P, 4, P])
        rows = ph.sb("rows", [P, KB, F + 8])
        weights += [(w2[:, :, 0:F], chunks_of(A["L2_WT"])), (wr2[:], chunks_of(A["L2_W"])), (heads[:], chunks_of(A["L2_heads"])),
                    (bias2[:, 0:F], on_all(A["L2_b"])), (bcol[:], A["L2_b"].rearrange("(c p) -> p c", p=P))]
        loads.append((x1[:], m.T[1]))
        stores = [(z[:], m.x2), (rows[:], m.T[3])]
    products = 2 if last_one else 1
    at = dict(m.at)
    sides = [None, None]
    acc = m.acc_view
    with nc.Block() as block:
        @block.sync
        def _(sp):
            with nc.allow_non_contiguous_dma(reason="a small vector as columns"):
                ph.traffic(sp, weights, loads, stores)

        @block.tensor
        def _(pe):
            pe.wait_ge(m.weights_in, at["weights_in"] + 16 * len(weights))
            if last_one:
                fold(pe, m, ph.ps_f, wr2, heads, 4, 2, 16).then_inc(m.folded, 1)
                pe.wait_ge(m.fold_taken, at["fold"] + 1)
                for c in range(4):
                    last = pe.matmul(ph.ps_f[:, 64:80], brep[:, c, :], heads[:, c, :], start=(c == 0), stop=(c == 3))
                last.then_inc(m.folded, 1)
                pe.wait_ge(m.fold_taken, at["fold"] + 2)

            def body(i):
                pe.wait_ge(m.rows_in, at["rows_in"] + 16 * len(loads) * (i + 1))
                pe.wait_ge(m.for_pe, at["for_pe"] + products * i + 1)
                p = at["product"] + products * KB * i
                make_products(pe, m, ph, p, lambda kb: [mean[:, kb, 0:P], mean[:, kb, P:D], h[:, kb, 0:P], h[:, kb, P:D]], w, D)
                if last_one:
                    pe.wait_ge(m.for_pe, at["for_pe"] + products * i + 2)
                    make_products(pe, m, ph, p + KB, lambda kb: [z[:, kb, 0:P], z[:, kb, P:D]], w2, F + 16)

            turns(pe, BATCHES, body)

        @block.scalar
        def _(act):
            a = sides[1] = scalar_side(act, m)

            def body(i):
                a.turn(i)
                p = at["product"] + products * KB * i
                copy_turned(act, m, ph, p, 4)
                root(act, m, ph, a)
                a.take_over()
                a.hand_over(act.activation(z[:], z[:], ACT.Relu))
                if last_one:
                    root(act, m, ph, a)
                    copy_turned(act, m, ph, p + KB, 2)

            turns(act, BATCHES, body)
            a.after(BATCHES)

        @block.vector
        def _(dve):
            v = sides[0] = vector_side(dve, m)
            dve.wait_ge(m.weights_in, at["weights_in"] + 16 * len(weights))
            if last_one:
                dve.wait_ge(m.folded, at["fold"] + 1)
                dve.tensor_copy(w2[:, :, F:F + 16], ph.ps_f[:, 0:32].rearrange("p (c h) -> p c h", h=16))
                dve.tensor_copy(brep[:], bcol[:].rearrange("p (c n) -> p c n", n=1).to_broadcast([P, 4, P])).then_inc(m.fold_taken, 1)
                dve.wait_ge(m.folded, at["fold"] + 2)
                v.settled(dve.tensor_copy(bias2[:, F:F + 16], ph.ps_f[:, 64:80]))
                dve.memset(m.mark[:], 0.0).then_inc(m.fold_taken, 1)

            def body(i):
                v.turn(i)
                p = at["product"] + products * KB * i
                dve.wait_ge(m.rows_in, at["rows_in"] + 16 * len(loads) * (i + 1))
                dve.tensor_tensor(mean[:], acc[:, bass.ds(i * KB, KB), :],
                                  m.rcnt[:, bass.ds(i * KB, KB)].rearrange("p (b w) -> p b w", w=1).to_broadcast([P, KB, D]),
                                  ALU.mult).then_inc(m.for_pe, 1)
                take_products(dve, m, ph, p, lambda kb, y: dve.tensor_tensor(z[:, kb, :], y[:, 0:D], bias[:, 0, :], ALU.add))
                dve.wait_ge(m.product_taken, p + KB)
                normalize(dve, m, ph, v, z)
                v.settled(dve.tensor_tensor(z[:], z[:], per_block(bias[:, 1, :], [P, KB, D]), ALU.mult))
                v.hand_over(dve.tensor_tensor(z[:], z[:], per_block(bias[:, 2, :], [P, KB, D]), ALU.add))
                v.take_over()
                if last_one:
                    v.settled(dve.tensor_tensor(z[:], z[:], x1[:], ALU.add))
                    normalize(dve, m, ph, v, z)
                    dve.memset(m.mark[:], 0.0).then_inc(m.for_pe, 1)

                    def take(kb, y):
                        dve.tensor_tensor(m.sall[:, bass.ds(i * KB + kb, 1), 8:16], y[:, F + 8:F + 16].rearrange("p (b h) -> p b h", b=1),
                                          bias2[:, F + 8:F + 16].rearrange("p (b h) -> p b h", b=1), ALU.add)
                        return dve.tensor_tensor(rows[:, kb, :], y[:, 0:F + 8], bias2[:, 0:F + 8], ALU.add)

                    take_products(dve, m, ph, p + KB, take)
                    dve.wait_ge(m.product_taken, p + 2 * KB)
                dve.memset(m.mark[:], 0.0).then_inc(m.rows_made, 1)

            turns(dve, BATCHES, body)
            v.after(BATCHES)

    if last_one:
        m.at["fold"] += 2
    ph.close(weights, loads, stores, products, products, sides)


def phase_4(nc, m, A):
    ph = NodePhase(nc, m, "n4")
    ph.buffers(4)
    F, H = 2 * D, 8
    HW = F // H
    z = ph.sb("z", [P, KB, F])
    e = ph.sb("e", [P, KB, F])
    rows = ph.sb("rows", [P, KB, D + 1])
    mu = ph.sb("mu", [P, KB * H])
    var = ph.sb("var", [P, KB * H])
    w = ph.sb("w", [P, 4, D + 2])
    wr = ph.sb("wr", [P, 2, F])
    heads = ph.sb("heads", [P, 2, 16])
    gain = ph.sb("gain", [P, 2, F])
    bias = ph.sb("bias", [P, D + 2])
    bcol = ph.sb("bcol", [P, 2])
    brep = ph.sb("brep", [P, 2, P])
    weights = [(w[:, :, 0:D], chunks_of(A["L2_WoutT"])), (wr[:], chunks_of(A["L2_gnn_W_out"])), (heads[:, :, 0:2], chunks_of(A["L2_out_heads"])),
               (gain[:, 0, :], on_all(A["L2_g"])), (gain[:, 1, :], on_all(A["L2_beta"])),
               (bias[:, 0:D], on_all(A["L2_gnn_b_out"])), (bcol[:], A["L2_gnn_b_out"].rearrange("(c p) -> p c", p=P))]
    loads, stores = [], [(rows[:], m.T[4])]
    at = dict(m.at)
    sides = [None, None]
    acc = m.acc_view
    with nc.Block() as block:
        @block.sync
        def _(sp):
            with nc.allow_non_contiguous_dma(reason="a small vector as columns"):
                ph.traffic(sp, weights, loads, stores)

        @block.tensor
        def _(pe):
            pe.wait_ge(m.weights_in, at["weights_in"] + 16 * len(weights))
            fold(pe, m, ph.ps_f, wr, heads, 2, 4, 2).then_inc(m.folded, 1)
            pe.wait_ge(m.fold_taken, at["fold"] + 1)
            for c in range(2):
                last = pe.matmul(ph.ps_f[:, 80:82], brep[:, c, :], heads[:, c, 0:2], start=(c == 0), stop=(c == 1))
            last.then_inc(m.folded, 1)
            pe.wait_ge(m.fold_taken, at["fold"] + 2)

            def body(i):
                pe.wait_ge(m.for_pe, at["for_pe"] + i + 1)
                make_products(pe, m, ph, at["product"] + KB * i, lambda kb: [e[:, kb, c * P:(c + 1) * P] for c in range(4)], w, D + 2)

            turns(pe, BATCHES, body)

        @block.scalar
        def _(act):
            a = sides[1] = scalar_side(act, m)

            def body(i):
                a.turn(i)
                a.take_over()
                a.hand_over(act.activation(e[:], z[:], ACT.Square))
                a.take_over()
                a.hand_over(act.activation(var[:], var[:], ACT.Sqrt))
                elu_parts(act, m, a, z[:], e[:])
                copy_turned(act, m, ph, at["product"] + KB * i, 4)

            turns(act, BATCHES, body)
            a.after(BATCHES)

        @block.vector
        def _(dve):
            v = sides[0] = vector_side(dve, m)
            dve.wait_ge(m.weights_in, at["weights_in"] + 16 * len(weights))
            dve.wait_ge(m.folded, at["fold"] + 1)
            dve.tensor_copy(w[:, :, D:D + 2], ph.ps_f[:, 0:64].rearrange("p (c h) -> p c h", h=16)[:, :, 0:2])
            dve.tensor_copy(brep[:], bcol[:].rearrange("p (c n) -> p c n", n=1).to_broadcast([P, 2, P])).then_inc(m.fold_taken, 1)
            dve.wait_ge(m.folded, at["fold"] + 2)
            v.settled(dve.tensor_copy(bias[:, D:D + 2], ph.ps_f[:, 80:82]))
            dve.memset(m.mark[:], 0.0).then_inc(m.fold_taken, 1)
            zh, eh = (t[:].rearrange("p b (h w) -> p (b h) w", h=H) for t in (z, e))

            def body(i):
                v.turn(i)
                if not isinstance(i, int):
                    dve.wait_ge(m.rows_out, at["rows_out"] + 16 * i)
                sums = acc[:, bass.ds(i * KB, KB), :].rearrange("p b (h w) -> p (b h) w", h=H)
                v.settled(dve.tensor_reduce(mu[:], sums, AX_X, ALU.add))
                v.settled(dve.tensor_scalar(mu[:], mu[:], 1.0 / HW, None, ALU.mult))
                v.hand_over(dve.tensor_tensor(zh, sums, per_row(mu[:], [P, KB * H, HW]), ALU.subtract))
                v.take_over()
                v.settled(dve.tensor_reduce(var[:], eh, AX_X, ALU.add))
                v.hand_over(dve.tensor_scalar(var[:], var[:], 1.0 / HW, LN_EPS, ALU.mult, ALU.add))
                v.take_over()
                v.settled(dve.reciprocal(var[:], var[:]))
                v.settled(dve.tensor_tensor(zh, zh, per_row(var[:], [P, KB * H, HW]), ALU.mult))
                v.settled(dve.tensor_tensor(z[:], z[:], per_block(gain[:, 0, :], [P, KB, F]), ALU.mult))
                v.hand_over(dve.tensor_tensor(z[:], z[:], per_block(gain[:, 1, :], [P, KB, F]), ALU.add))
                v.take_over()
                dve.scalar_tensor_tensor(e[:], e[:], -1.0, z[:], ALU.add, ALU.add).then_inc(m.for_pe, 1)

                def take(kb, y):
                    dve.tensor_tensor(m.sall[:, bass.ds(i * KB + kb, 1), 8:9], y[:, D + 1:D + 2].rearrange("p (b h) -> p b h", b=1),
                                      bias[:, D + 1:D + 2].rearrange("p (b h) -> p b h", b=1), ALU.add)
                    return dve.tensor_tensor(rows[:, kb, :], y[:, 0:D + 1], bias[:, 0:D + 1], ALU.add)

                take_products(dve, m, ph, at["product"] + KB * i, take)
                dve.wait_ge(m.product_taken, at["product"] + KB * (i + 1))
                dve.memset(m.mark[:], 0.0).then_inc(m.rows_made, 1)

            turns(dve, BATCHES, body)
            v.after(BATCHES)

    m.at["fold"] += 2
    ph.close(weights, loads, stores, 1, 1, sides)


def phase_5(nc, m, A):
    ph = NodePhase(nc, m, "n5")
    ph.buffers(2)
    x = ph.sb("x", [P, KB, D])
    z = ph.sb("z", [P, KB, D])
    e = ph.sb("e", [P, KB, D])
    rows = ph.sb("rows", [P, KB, D + 4])
    w = ph.sb("w", [P, 2, D + 8])
    wr = ph.sb("wr", [P, 2, D])
    heads = ph.sb("heads", [P, 2, 16])
    gain = ph.sb("gain", [P, 2, D])
    top = ph.sb("top", [P, 4])
    top_all = ph.sb("top_all", [P, 4])
    weights = [(w[:, :, 0:D], chunks_of(A["L3_gnn_W"])), (wr[:], chunks_of(A["L3_WT"])), (heads[:, :, 0:8], chunks_of(A["L3_heads"])),
               (gain[:, 0, :], on_all(A["L2_gnn_g_out"])), (gain[:, 1, :], on_all(A["L2_gnn_beta_out"]))]
    loads, stores = [(x[:], m.x2)], [(e[:], m.x3), (rows[:], m.T[5])]
    at = dict(m.at)
    sides = [None, None]
    acc = m.acc_view
    with nc.Block() as block:
        @block.sync
        def _(sp):
            ph.traffic(sp, weights, loads, stores)

        @block.tensor
        def _(pe):
            pe.wait_ge(m.weights_in, at["weights_in"] + 16 * len(weights))
            fold(pe, m, ph.ps_f, wr, heads, 2, 2, 8).then_inc(m.folded, 1)
            pe.wait_ge(m.fold_taken, at["fold"] + 1)

            def body(i):
                pe.wait_ge(m.for_pe, at["for_pe"] + i + 1)
                make_products(pe, m, ph, at["product"] + KB * i, lambda kb: [e[:, kb, 0:P], e[:, kb, P:D]], w, D + 8)

            turns(pe, BATCHES, body)

        @block.scalar
        def _(act):
            a = sides[1] = scalar_side(act, m)

            def body(i):
                a.turn(i)
                root(act, m, ph, a)
                elu_parts(act, m, a, z[:], e[:])
                root(act, m, ph, a)
                copy_turned(act, m, ph, at["product"] + KB * i, 2)

            turns(act, BATCHES, body)
            a.after(BATCHES)

        @block.gpsimd
        def _(pool):
            pool.wait_ge(m.for_pool, at["pool"] + 1)
            pool.partition_all_reduce(top_all[:], top[:], P, RMAX).then_inc(m.from_pool, 1)

        @block.vector
        def _(dve):
            v = sides[0] = vector_side(dve, m)
            dve.wait_ge(m.weights_in, at["weights_in"] + 16 * len(weights))
            dve.wait_ge(m.folded, at["fold"] + 1)
            dve.tensor_copy(w[:, :, D:D + 8], ph.ps_f[:, 0:32].rearrange("p (c h) -> p c h", h=16)[:, :, 0:8]).then_inc(m.fold_taken, 1)

            def body(i):
                v.turn(i)
                dve.wait_ge(m.rows_in, at["rows_in"] + 16 * (i + 1))
                v.settled(dve.tensor_copy(z[:], acc[:, bass.ds(i * KB, KB), :]))
                normalize(dve, m, ph, v, z)
                v.settled(dve.tensor_tensor(z[:], z[:], per_block(gain[:, 0, :], [P, KB, D]), ALU.mult))
                v.hand_over(dve.tensor_tensor(z[:], z[:], per_block(gain[:, 1, :], [P, KB, D]), ALU.add))
                v.take_over()
                v.settled(dve.scalar_tensor_tensor(e[:], e[:], -1.0, z[:], ALU.add, ALU.add))
                v.settled(dve.tensor_tensor(e[:], e[:], x[:], ALU.add))
                normalize(dve, m, ph, v, e)
                dve.memset(m.mark[:], 0.0).then_inc(m.for_pe, 1)

                def take(kb, y):
                    s = m.sall[:, bass.ds(i * KB + kb, 1), :]
                    dve.tensor_copy(s[:, :, 8:12], y[:, D + 4:D + 8].rearrange("p (b h) -> p b h", b=1))
                    dve.tensor_copy(s[:, :, 0:4], y[:, D:D + 4].rearrange("p (b h) -> p b h", b=1))
                    return dve.tensor_copy(rows[:, kb, :], y[:, 0:D + 4])

                take_products(dve, m, ph, at["product"] + KB * i, take)
                dve.wait_ge(m.product_taken, at["product"] + KB * (i + 1))
                dve.memset(m.mark[:], 0.0).then_inc(m.rows_made, 1)

            turns(dve, BATCHES, body)
            v.after(BATCHES)
            dve.tensor_reduce(top[:], m.sall[:, :, 0:4].rearrange("p b h -> p h b"), AX_X, ALU.max).then_inc(m.for_pool, 1)
            dve.wait_ge(m.from_pool, at["pool"] + 1)
            v.settled(dve.tensor_tensor(m.sall[:, :, 4:8], m.sall[:, :, 8:12], per_block(top_all[:], [P, NB, 4]), ALU.add))
            v.settled(dve.scalar_tensor_tensor(m.sall[:, :, 12:16], m.sall[:, :, 4:8], SLOPE, m.sall[:, :, 4:8], ALU.mult, ALU.max))
            v.turn(0)

    m.at["pool"] += 1
    m.at["fold"] += 1
    ph.close(weights, loads, stores, 1, 1, sides)


def phase_6(nc, m, A, out):
    ph = NodePhase(nc, m, "n6")
    ph.buffers(1)
    x = ph.sb("x", [P, KB, D])
    z = ph.sb("z", [P, KB, D])
    y = ph.sb("y", [P, KB, D])
    rows = ph.sb("rows", [P, KB, D + 4])
    s = ph.sb("s", [P, KB, 4])
    own = ph.sb("own", [P, KB, 4])
    den = ph.sb("den", [P, KB, 4])
    bias = ph.sb("bias", [P, 3, D])
    weights = [(bias[:, 0, :], on_all(A["L3_gnn_bias"])), (bias[:, 1, :], on_all(A["L3_gnn_gamma"])), (bias[:, 2, :], on_all(A["L3_gnn_beta"]))]
    loads, stores = [(x[:], m.x3), (rows[:], m.T[5])], [(z[:], out)]
    at = dict(m.at)
    sides = [None, None]
    acc = m.acc_view
    with nc.Block() as block:
        @block.sync
        def _(sp):
            ph.traffic(sp, weights, loads, stores)

        @block.scalar
        def _(act):
            a = sides[1] = scalar_side(act, m)

            def body(i):
                a.turn(i)
                a.take_over()
                a.hand_over(act.activation(own[:], s[:], ACT.Exp))
                a.take_over()
                a.hand_over(act.activation(z[:], z[:], ACT.Relu))
                root(act, m, ph, a)
                root(act, m, ph, a)

            turns(act, BATCHES, body)
            a.after(BATCHES)

        @block.vector
        def _(dve):
            v = sides[0] = vector_side(dve, m)
            dve.wait_ge(m.weights_in, at["weights_in"] + 16 * len(weights))

            def body(i):
                v.turn(i)
                dve.wait_ge(m.rows_in, at["rows_in"] + 32 * (i + 1))
                mine = m.sall[:, bass.ds(i * KB, KB), :]
                v.settled(dve.tensor_tensor(s[:], rows[:, :, D:D + 4], mine[:, :, 8:12], ALU.add))
                v.settled(dve.scalar_tensor_tensor(s[:], s[:], SLOPE, s[:], ALU.mult, ALU.max))
                v.hand_over(dve.tensor_tensor(s[:], s[:], mine[:, :, 12:16], ALU.subtract))
                v.take_over()
                v.settled(dve.tensor_tensor(den[:], own[:], acc[:, bass.ds(i * KB, KB), D:D + 4], ALU.add))
                v.settled(dve.reciprocal(den[:], den[:]))
                for kb in range(KB):
                    last = dve.tensor_tensor(z[:, kb, :].rearrange("p (h w) -> p h w", h=4), rows[:, kb, 0:D].rearrange("p (h w) -> p h w", h=4),
                                             own[:, kb, :].rearrange("p (h w) -> p h w", w=1).to_broadcast([P, 4, D // 4]), ALU.mult)
                v.settled(last)
                v.settled(dve.tensor_tensor(z[:], z[:], acc[:, bass.ds(i * KB, KB), 0:D], ALU.add))
                for kb in range(KB):
                    zk = z[:, kb, :].rearrange("p (h w) -> p h w", h=4)
                    last = dve.tensor_tensor(zk, zk, den[:, kb, :].rearrange("p (h w) -> p h w", w=1).to_broadcast([P, 4, D // 4]), ALU.mult)
                v.settled(last)
                v.hand_over(dve.tensor_tensor(z[:], z[:], per_block(bias[:, 0, :], [P, KB, D]), ALU.add))
                v.take_over()
                v.settled(dve.tensor_tensor(z[:], z[:], x[:], ALU.add))
                normalize(dve, m, ph, v, z)
                v.settled(dve.tensor_tensor(z[:], z[:], per_block(bias[:, 1, :], [P, KB, D]), ALU.mult))
                v.settled(dve.tensor_tensor(z[:], z[:], per_block(bias[:, 2, :], [P, KB, D]), ALU.add))
                v.settled(dve.tensor_tensor(z[:], z[:], x[:], ALU.add))
                normalize(dve, m, ph, v, z)
                dve.memset(m.mark[:], 0.0).then_inc(m.rows_made, 1)

            turns(dve, BATCHES, body)
            v.after(BATCHES)

    ph.close(weights, loads, stores, 0, 0, sides)


def build(nc, A, out):
    ctx = ExitStack()
    with ctx:
        def sb(name, shape, dt=F32):
            return ctx.enter_context(nc.sbuf_tensor(name, shape, dt))

        def sem(name):
            return ctx.enter_context(nc.semaphore(name))

        def dram(name, shape, dt=F32):
            return nc.dram_tensor(name, shape, dt, kind="Internal").ap()

        m = Shared()
        m.meta = [dram(f"slots_by_{k}", (P * TILES_P, 2), I32) for k in ("dst", "src")]
        m.T = [dram(f"table{k}", (NP, w)) for k, w in enumerate((D + 9, D, D, 2 * D + 8, D + 1, D + 4))]
        m.x2, m.x3 = dram("x2", (NP, D)), dram("x3", (NP, D))
        m.acc = sb("acc", [P, NB * 2 * D])
        m.sall = sb("sall", [P, NB, 16])
        m.rcnt = sb("rcnt", [P, NB])
        m.group_block = [sb(f"group_block{k}", [1, TG], I32) for k in range(2)]
        m.iota_row = sb("iota_row", [P, P])
        m.part_col = sb("part_col", [P, 1])
        m.ident = sb("ident", [P, P])
        m.ones = sb("ones", [P, P])
        m.neg_bound = sb("neg_bound", [P, 1])
        m.score_max = sb("score_max", [P, C * 8])
        m.eps_col = sb("eps_col", [P, 1])
        m.mark = sb("mark", [1, 1])

        m.consts_ready = sem("consts_ready")
        m.numbered = sem("numbered")
        m.loaded = sem("loaded")
        m.fill_made = sem("fill_made")
        m.prefilled = sem("prefilled")
        m.counted = sem("counted")
        m.summed_up = sem("summed_up")
        m.ended = sem("ended")
        m.slotted = sem("slotted")
        m.staged = sem("staged")
        m.scattered = [sem(f"scattered{h}") for h in range(2)]
        m.pool_passed = sem("pool_passed")
        m.sync_passed = sem("sync_passed")
        m.vec_step = sem("vec_step")
        m.act_step = sem("act_step")
        m.for_act = sem("for_act")
        m.for_vec = sem("for_vec")
        m.for_pe = sem("for_pe")
        m.for_pool = sem("for_pool")
        m.from_pool = sem("from_pool")
        m.weights_in = sem("weights_in")
        m.rows_in = sem("rows_in")
        m.rows_made = sem("rows_made")
        m.rows_out = sem("rows_out")
        m.folded = sem("folded")
        m.fold_taken = sem("fold_taken")
        m.x_turned = sem("x_turned")
        m.x_copied = sem("x_copied")
        m.product = sem("product")
        m.product_taken = sem("product_taken")
        m.slots_in = [sem(f"slots_in{u}") for u in range(U)]
        m.gathered = [sem(f"gathered{u}") for u in range(U)]
        m.onehot_built = sem("onehot_built")
        m.padded = sem("padded")
        m.onehot_turned = sem("onehot_turned")
        m.onehot_copied = sem("onehot_copied")
        m.own_scored = sem("own_scored")
        m.scored = sem("scored")
        m.exped = sem("exped")
        m.weighted = sem("weighted")
        m.summed = sem("summed")
        m.added = sem("added")

        m.at = {k: 0 for k in ("vec", "act", "for_act", "for_vec", "for_pe", "pool", "weights_in", "rows_in",
                               "rows_made", "rows_out", "fold", "product", "chunk", "onehots", "ahead", "wchunk",
                               "gathered", "slots0", "slots1", "slots2", "slots3")}

        with ExitStack() as sc:
            row_i = sc.enter_context(nc.sbuf_tensor("row_i", [P, P], I32))
            col_i = sc.enter_context(nc.sbuf_tensor("col_i", [P, 1], I32))
            with nc.Block() as block:
                @block.gpsimd
                def _(pool):
                    pool.iota(row_i[:], pattern=[[1, P]], base=0, channel_multiplier=0).then_inc(m.consts_ready, 1)
                    pool.iota(col_i[:], pattern=[[0, 1]], base=0, channel_multiplier=1).then_inc(m.consts_ready, 1)

                @block.vector
                def _(dve):
                    dve.memset(m.ones[:], 1.0)
                    dve.memset(m.score_max[:], -BIG)
                    dve.wait_ge(m.consts_ready, 2)
                    dve.tensor_copy(m.iota_row[:], row_i[:]).then_inc(m.consts_ready, 1)
                    dve.tensor_copy(m.part_col[:], col_i[:]).then_inc(m.consts_ready, 1)
                    dve.wait_ge(m.consts_ready, 4)
                    dve.tensor_scalar(m.ident[:], m.iota_row[:], m.part_col[:, 0:1], None, ALU.is_equal).then_inc(m.consts_ready, 1)
                    dve.wait_ge(m.consts_ready, 5)

        place_edges(nc, m, 0, A["dst"], A["src"])
        place_edges(nc, m, 1, A["src"], A["dst"])
        phase_0(nc, m, A)
        edge_phase(nc, m, way=0, table=0, width=D + 9, feat=D, heads=8, own=8, mode="gat")
        phase_1(nc, m, A)
        edge_phase(nc, m, way=0, table=1, width=D, feat=D, heads=0, own=0, mode="sum")
        phase_sage(nc, m, A, 1)
        edge_phase(nc, m, way=0, table=2, width=D, feat=D, heads=0, own=0, mode="sum")
        phase_sage(nc, m, A, 2)
        edge_phase(nc, m, way=1, table=3, width=2 * D + 8, feat=2 * D, heads=8, own=8, mode="neg")
        phase_4(nc, m, A)
        edge_phase(nc, m, way=1, table=4, width=D + 1, feat=D, heads=1, own=1, mode="neg")
        phase_5(nc, m, A)
        edge_phase(nc, m, way=0, table=5, width=D + 4, feat=D, heads=4, own=8, mode="shift")
        phase_6(nc, m, A, out)


def kernel(**inputs):
    import numpy as np
    from concourse import bacc
    from concourse.bass_utils import run_bass_kernel_spmd

    a = {k: np.asarray(v) for k, v in inputs.items()}

    def by_head(*vectors):
        h, w = vectors[0].shape
        out = np.zeros((h * w, h * len(vectors)), vectors[0].dtype)
        for n, v in enumerate(vectors):
            for k in range(h):
                out[k * w:(k + 1) * w, n * h + k] = v[k]
        return out

    x = np.zeros((NP, D), a["x"].dtype)
    x[:N_NODES] = a["x"]
    a_heads, a_out = a["L2_gnn_a_heads"], a["L2_gnn_a_out"].reshape(1, -1)
    half = a_heads.shape[1] // 2
    W2 = a["L2_gnn_W_heads"].reshape(-1, D)
    laid = {
        "x": x, "src": a["src"], "dst": a["dst"],
        "L0_WpT": a["L0_gnn_Wp"].T, "L0_gnn_Wp": a["L0_gnn_Wp"], "L0_WskipT": a["L0_gnn_Wskip"].T,
        "L0_heads": by_head(a["L0_gnn_a_src"][0], a["L0_gnn_a_trg"][0]), "L0_gnn_bias": a["L0_gnn_bias"],
        "L2_W": W2, "L2_WT": W2.T, "L2_b": a["L2_gnn_b_heads"].reshape(-1),
        "L2_heads": by_head(a_heads[:, half:], a_heads[:, :half]),
        "L2_g": a["L2_gnn_g_heads"].reshape(-1), "L2_beta": a["L2_gnn_beta_heads"].reshape(-1),
        "L2_gnn_W_out": a["L2_gnn_W_out"], "L2_WoutT": a["L2_gnn_W_out"].T, "L2_gnn_b_out": a["L2_gnn_b_out"],
        "L2_out_heads": by_head(a_out[:, D:], a_out[:, :D]),
        "L2_gnn_g_out": a["L2_gnn_g_out"], "L2_gnn_beta_out": a["L2_gnn_beta_out"],
        "L3_gnn_W": a["L3_gnn_W"], "L3_WT": a["L3_gnn_W"].T,
        "L3_heads": by_head(a["L3_gnn_att_src"], a["L3_gnn_att_dst"]),
        "L3_gnn_bias": a["L3_gnn_bias"], "L3_gnn_gamma": a["L3_gnn_gamma"], "L3_gnn_beta": a["L3_gnn_beta"],
    }
    for k in ("W_l1", "b_l1", "W_r1", "ln1_g", "ln1_b", "W_l2", "b_l2", "W_r2", "ln2_g", "ln2_b"):
        laid[f"L1_gnn_{k}"] = a[f"L1_gnn_{k}"]
    laid = {k: np.ascontiguousarray(v) for k, v in laid.items()}

    nc = bacc.Bacc("TRN2", target_bir_lowering=False, num_devices=1)
    A = {k: nc.dram_tensor(f"in_{k}", v.shape, mybir.dt.from_np(v.dtype), kind="ExternalInput").ap() for k, v in laid.items()}
    out = nc.dram_tensor("out", (NP, D), F32, kind="ExternalOutput").ap()
    build(nc, A, out)
    r = run_bass_kernel_spmd(nc, [{f"in_{k}": v for k, v in laid.items()}], core_ids=[0])
    return r.results[0]["out"][:N_NODES]
```

```python
from contextlib import ExitStack

import concourse.bass as bass
from concourse import mybir

F32 = mybir.dt.float32
BF16 = mybir.dt.bfloat16
I32 = mybir.dt.int32
ALU = mybir.AluOpType
ACT = mybir.ActivationFunctionType
AX_X = mybir.AxisListType.X
RMAX = bass.bass_isa.ReduceOp.max

P = 128
N_NODES = 6250
N_EDGES = 100000
D = 256
NB = -(-N_NODES // P)
NP = NB * P
EP = 125
EC = N_EDGES // EP
G = 2
C = 4
R = 5
U = 2 * R
GC = C // G
GB = GC * U
GROUPS = -(-((N_EDGES + NB * (G * P - 1)) // (G * P)) // GB) * GB
CHUNKS = GROUPS // GC
BODIES = CHUNKS // U
TILES = GROUPS * G
TG = 2 * GC + GROUPS + GB
SC = 8
STAGES = EC // SC
KB = 7
BATCHES = NB // KB
BIG = 1.0e30
LN_EPS = 1e-5
SLOPE = 0.2
EMPTY = 200


class Shared:
    pass


class Tally:

    def __init__(self, start):
        self.start = start
        self.value = start
        self.n = 0
        self.per_turn = 0

    def turn(self, i):
        if isinstance(i, int) and i == 0:
            self.settle()
            self.start, self.per_turn = self.value, 0
        else:
            self.per_turn = self.per_turn or self.n
            self.value = self.start + i * self.per_turn
        self.n = 0

    def next(self):
        self.n += 1
        return self.value + self.n

    def settle(self, turns=None):
        if turns is not None:
            self.value = self.start + (turns - 1) * self.per_turn
        self.value, self.n = self.value + self.n, 0


def wait(eng, sem, value):
    if isinstance(value, int) and value <= 0:
        return
    eng.wait_ge(sem, value)


def turns(eng, n, body):
    body(0)
    with eng.Fori(1, n - 1) as i:
        body(i)
    body(n - 1)


def is_first(i):
    return isinstance(i, int) and i == 0


def wide(ap, shape):
    return ap.to_broadcast(shape)


def place_edges(nc, m, way, key, other):
    sc = ExitStack()
    with sc:
        def sb(name, shape, dt=F32):
            return sc.enter_context(nc.sbuf_tensor(f"{name}_{way}", shape, dt))

        def ps(name):
            return sc.enter_context(nc.psum_tensor(f"{name}_{way}", [P, 512], F32))

        key_i = sb("key_i", [EP, EC], I32)
        other_i = sb("other_i", [EP, EC], I32)
        tile_i = sb("tile_i", [EP, EC], I32)
        slotted = sb("slotted", [EP, EC, 3], I32)
        blk = sb("blk", [EP, EC], BF16)
        zero = sb("zero", [EP, EC], BF16)
        count = sb("count", [EP, EC])
        chosen = sb("chosen", [EP, EC])
        rank = sb("rank", [EP, EC])
        member = m.acc[:].bitcast(BF16)[0:EP, 0:NB * EC]
        below = sb("below", [P, P])
        total = sb("total", [EP, NB])
        groups_i = sb("groups_i", [P, NB], I32)
        groups_f = sb("groups_f", [P, NB])
        group_end = sb("group_end", [P, NB])
        zeros_b = sb("zeros_b", [P, NB])
        first = sb("first", [EP, NB])
        end_col = sb("end_col", [P, 1])
        group_i = sb("group_i", [NB, GROUPS], I32)
        passed = sb("passed", [NB, GROUPS])
        block_f = sb("block_f", [1, GROUPS])
        fill = sb("fill", [P, TILES, 2], I32)
        stage = sb("stage", [EP, 2, SC, 3], I32)
        ps_before, ps_total, ps_end, ps_group = ps("ps_before"), ps("ps_total"), ps("ps_end"), ps("ps_group")
        chain0 = m.at["vec"]

        with nc.Block() as block:
            @block.sync
            def _(sp):
                sp.dma_start(key_i[:], key.rearrange("(p e) -> p e", e=EC)).then_inc(m.loaded, 16)
                sp.dma_start(other_i[:], other.rearrange("(p e) -> p e", e=EC)).then_inc(m.loaded, 16)
                sp.wait_ge(m.fill_made, 2 * (way + 1))
                sp.dma_start(m.meta[way].rearrange("(p t) k -> p (t k)", p=P),
                             fill[:].rearrange("p t k -> p (t k)")).then_inc(m.prefilled, 16)
                sp.wait_ge(m.prefilled, 16 * (way + 1))

            @block.gpsimd
            def _(pool):
                pool.iota(group_i[:], pattern=[[1, GROUPS]], base=0, channel_multiplier=0).then_inc(m.numbered, 1)
                pool.wait_ge(m.prefilled, 16 * (way + 1))

                def part(i):
                    for h in range(2):
                        pool.wait_ge(m.staged, way * STAGES + 2 * i + h + 1)
                        pool.sem_inc(m.pool_passed, 1)
                        for j in range(SC):
                            pool.indirect_dma_start(
                                m.meta[way], bass.IndirectOffsetOnAxis(ap=stage[:, h, j, 0:1], axis=0),
                                stage[:, h, j, 1:3], None).then_inc(m.scattered[h], 16)

                turns(pool, STAGES // 2, part)
                for h in range(2):
                    pool.wait_ge(m.scattered[h], 16 * SC * (STAGES // 2) * (way + 1))

            @block.scalar
            def _(act):
                act.wait_ge(m.slotted, way + 1)

                def part(i):
                    for h in range(2):
                        wait(act, m.scattered[h], 16 * SC * ((STAGES // 2) * way + i))
                        act.copy(stage[:, h, :, :], slotted[:, bass.ds((2 * i + h) * SC, SC), :]).then_inc(m.staged, 1)

                turns(act, STAGES // 2, part)

            @block.tensor
            def _(pe):
                pe.wait_ge(m.counted, way + 1)
                pe.matmul(ps_before[0:EP, 0:NB], below[0:EP, 0:EP], total[:], start=True, stop=True)
                pe.matmul(ps_total[:, 0:NB], m.ones[0:EP, :], total[:], start=True, stop=True).then_inc(m.summed_up, 1)
                pe.wait_ge(m.ended, 2 * way + 1)
                pe.matmul(ps_end[0:NB, 0:1], group_end[0:1, 0:NB], m.ones[0:1, 0:1], start=True, stop=True).then_inc(m.summed_up, 1)
                pe.wait_ge(m.ended, 2 * way + 2)
                pe.matmul(ps_group[0:1, 0:GROUPS], m.ones[0:NB, 0:1], passed[:], start=True, stop=True).then_inc(m.summed_up, 1)

            @block.vector
            def _(dve):
                chain = Tally(chain0)

                def settled(ins):
                    ins.then_inc(m.vec_step, 1)
                    dve.wait_ge(m.vec_step, chain.next())

                dve.memset(fill[:, :, 0:1], 0).then_inc(m.fill_made, 1)
                dve.memset(fill[:, :, 1:2], EMPTY).then_inc(m.fill_made, 1)
                dve.memset(zero[:], 0.0)
                dve.memset(zeros_b[:], 0.0)
                dve.memset(rank[:], 0.0)
                dve.memset(m.group_block[way][:], 0)
                dve.tensor_scalar(below[:], m.iota_row[:], m.part_col[:, 0:1], None, ALU.is_gt)
                dve.wait_ge(m.loaded, 32 * (way + 1))
                dve.tensor_copy(slotted[:, :, 1], other_i[:])
                dve.tensor_scalar(slotted[:, :, 2], key_i[:], P - 1, None, ALU.bitwise_and)
                settled(dve.tensor_scalar(tile_i[:], key_i[:], 7, None, ALU.logical_shift_right))
                settled(dve.tensor_copy(blk[:], tile_i[:]))

                head = chain.value + chain.n
                with dve.Fori(0, NB) as b:
                    dve.tensor_scalar(member[:, bass.ds(b * EC, EC)], blk[:], m.iota_row[0:EP, bass.ds(b, 1)], 0.0,
                                      ALU.is_equal, ALU.add, accum_out=total[:, bass.ds(b, 1)]).then_inc(m.vec_step, 1)
                chain = Tally(head + NB)
                dve.wait_ge(m.vec_step, head + NB)
                dve.memset(m.mark[:], 0.0).then_inc(m.counted, 1)

                dve.wait_ge(m.summed_up, 3 * way + 1)
                settled(dve.tensor_scalar(groups_f[:], ps_total[:, 0:NB], float(G * P - 1), None, ALU.add))
                settled(dve.tensor_copy(groups_i[:], groups_f[:]))
                settled(dve.tensor_scalar(groups_i[:], groups_i[:], 8, None, ALU.logical_shift_right))
                settled(dve.tensor_copy(groups_f[:], groups_i[:]))
                dve.tensor_tensor_scan(group_end[:], groups_f[:], zeros_b[:], 0.0, ALU.add, ALU.add).then_inc(m.ended, 1)
                dve.wait_ge(m.ended, 2 * way + 1)
                settled(dve.tensor_tensor(groups_f[:], group_end[:], groups_f[:], ALU.subtract))
                settled(dve.scalar_tensor_tensor(first[:], groups_f[0:EP, :], float(G * P), ps_before[0:EP, 0:NB], ALU.mult, ALU.add))
                settled(dve.tensor_scalar(first[:], first[:], -1.0, None, ALU.add))

                dve.wait_ge(m.summed_up, 3 * way + 2)
                settled(dve.tensor_copy(end_col[0:NB, :], ps_end[0:NB, 0:1]))
                dve.wait_ge(m.numbered, way + 1)
                settled(dve.tensor_copy(passed[:], group_i[:]))
                dve.tensor_scalar(passed[:], passed[:], end_col[0:NB, 0:1], None, ALU.is_ge).then_inc(m.ended, 1)
                dve.wait_ge(m.summed_up, 3 * way + 3)
                settled(dve.tensor_scalar(block_f[:], ps_group[0:1, 0:GROUPS], float(NB - 1), None, ALU.min))
                settled(dve.tensor_copy(m.group_block[way][0:1, 2 * GC:2 * GC + GROUPS], block_f[:]))

                head = chain.value + chain.n
                with dve.Fori(0, NB) as b:
                    dve.tensor_tensor_scan(count[:], member[:, bass.ds(b * EC, EC)], zero[:], first[:, bass.ds(b, 1)], ALU.add, ALU.add).then_inc(m.vec_step, 1)
                    dve.wait_ge(m.vec_step, head + 3 * b + 1)
                    dve.tensor_tensor(chosen[:], count[:], member[:, bass.ds(b * EC, EC)], ALU.mult).then_inc(m.vec_step, 1)
                    dve.wait_ge(m.vec_step, head + 3 * b + 2)
                    dve.tensor_tensor(rank[:], rank[:], chosen[:], ALU.add).then_inc(m.vec_step, 1)
                    dve.wait_ge(m.vec_step, head + 3 * b + 3)
                chain = Tally(head + 3 * NB)

                settled(dve.tensor_copy(key_i[:], rank[:]))
                settled(dve.tensor_scalar(tile_i[:], key_i[:], 7, None, ALU.logical_shift_right))
                settled(dve.tensor_scalar(key_i[:], key_i[:], P - 1, None, ALU.bitwise_and))
                settled(dve.tensor_scalar(count[:], key_i[:], float(TILES), None, ALU.mult))
                dve.tensor_tensor(slotted[:, :, 0], count[:], tile_i[:], ALU.add).then_inc(m.slotted, 1)
                dve.wait_ge(m.slotted, way + 1)
                m.at["vec"] = chain.value + chain.n


def edge_phase(nc, m, way, table, width, feat, heads, own, mode):
    sc = ExitStack()
    summed_cols = feat if mode in ("sum", "neg") else width
    acc = m.acc[:, 0:NB * summed_cols].rearrange("p (b w) -> p b w", w=summed_cols)
    m.acc_view = acc
    weights = mode != "sum"
    T = m.T[table]
    at = dict(m.at)
    hw = feat // heads if heads else 0
    slot_rows = m.meta[way].rearrange("(p t) k -> p t k", p=P)
    with sc:
        def sb(name, shape, dt=F32):
            return sc.enter_context(nc.sbuf_tensor(f"{name}_{table}", shape, dt))

        slots = sb("slots", [P, U, C, 2], I32)
        rows = sb("rows", [P, R, C, width])
        node = sb("node", [P, R, C])
        onehot = sb("onehot", [P, R, C, P])
        turned = sb("turned", [P, 2, C, P])
        raw = sb("raw", [P, 2, C, 8])
        score = sb("score", [P, 2, C, 8])
        pad = sb("pad", [P, R, C])
        ps_turned = [sc.enter_context(nc.psum_tensor(f"ps_turned{k}_{table}", [P, C, P], F32)) for k in range(2)]
        ps_own = [sc.enter_context(nc.psum_tensor(f"ps_own{k}_{table}", [P, 512], F32)) for k in range(2)]
        ps_sum = [sc.enter_context(nc.psum_tensor(f"ps_sum{k}_{table}", [P, 512], F32)) for k in range(2 * GC)]
        c0, w0, g0 = at["chunk"], at["wchunk"], at["chunk"] * GC
        iota_b = m.iota_row[:].rearrange("p (c n) -> p c n", c=1).to_broadcast([P, C, P])

        def rounds(i, u):
            return 2 * i + u // R

        with nc.Block() as block:
            @block.sync
            def _(sp):
                def body(i):
                    for u in range(U):
                        n = U * i + u
                        if not is_first(i):
                            sp.wait_ge(m.summed, g0 + GC * (n - U + 1))
                        sp.dma_start(slots[:, u, :, :], slot_rows[:, bass.ds(n * C, C), :]).then_inc(m.slots_in[u], 16)

                turns(sp, BODIES, body)

            @block.gpsimd
            def _(pool):
                def body(i):
                    for u in range(U):
                        n = U * i + u
                        if not (isinstance(n, int) and n < R):
                            pool.wait_ge(m.summed, g0 + GC * (n - R + 1))
                        pool.wait_ge(m.slots_in[u], at["slots"] + 16 * (i + 1))
                        pool.sem_inc(m.pool_passed, 1)
                        for j in range(C):
                            pool.indirect_dma_start(
                                rows[:, u % R, j, :], None, T,
                                bass.IndirectOffsetOnAxis(ap=slots[:, u, j, 0:1], axis=0)).then_inc(m.gathered[u % R], 16)

                turns(pool, BODIES, body)
                for r in range(R):
                    pool.wait_ge(m.gathered[r], at["gathered"] + 16 * C * 2 * BODIES)

            @block.scalar
            def _(act):
                if not weights:
                    return

                def copy_onehot(n, k):
                    act.wait_ge(m.onehot_turned, w0 + n + 1)
                    act.copy(turned[:, k, :, :], ps_turned[k][:]).then_inc(m.onehot_copied, 1)

                def exponentials(n, u):
                    act.wait_ge(m.scored, w0 + n + 1)
                    out = raw[:, u % 2, :, 0:heads] if mode == "neg" else rows[:, u % R, :, feat:feat + heads]
                    act.activation(out, score[:, u % 2, :, 0:heads], ACT.Exp,
                                   bias=m.neg_bound[:, 0:1] if mode == "gat" else 0.0,
                                   scale=-1.0 if mode == "neg" else 1.0).then_inc(m.exped, 1)

                copy_onehot(0, 0)
                copy_onehot(1, 1)
                exponentials(0, 0)

                def body(i):
                    for u in range(U):
                        n = U * i + u
                        if not (isinstance(n, int) and n + 2 >= CHUNKS):
                            copy_onehot(n + 2, u % 2)
                        if not (isinstance(n, int) and n + 1 >= CHUNKS):
                            exponentials(n + 1, u + 1)

                turns(act, BODIES, body)

            @block.tensor
            def _(pe):
                regs = [pe.alloc_register(f"pe_block{q}_{table}") for q in range(GB)]

                def load_blocks(start):
                    pe.reg_load(regs, m.group_block[way][0:1, bass.ds(start, GB)])
                    return [pe.snap(r, min_val=0, max_val=NB - 1) for r in regs]

                def turn_onehot(n, u):
                    pe.wait_ge(m.onehot_built, c0 + n + 1)
                    if not (isinstance(n, int) and n < 2):
                        pe.wait_ge(m.onehot_copied, w0 + n - 1)
                    for j in range(C):
                        last = pe.transpose(ps_turned[u % 2][:, j, :], onehot[:, u % R, j, :], m.ident[:])
                    last.then_inc(m.onehot_turned, 1)

                def own_scores(n, u, blocks):
                    pe.wait_ge(m.onehot_copied, w0 + n + 1)
                    if not (isinstance(n, int) and n < 2):
                        pe.wait_ge(m.scored, w0 + n - 1)
                    for j in range(C):
                        last = pe.matmul(ps_own[u % 2][:, j * 8:j * 8 + own], turned[:, u % 2, j, :],
                                         m.sall[:, bass.ds(blocks[j // G], 1), 8:8 + own],
                                         start=True, stop=True)
                    last.then_inc(m.own_scored, 1)

                def sums(n, i, u):
                    if weights:
                        pe.wait_ge(m.weighted, w0 + n + 1)
                    else:
                        pe.wait_ge(m.onehot_built, c0 + n + 1)
                        pe.wait_ge(m.gathered[u % R], at["gathered"] + 16 * C * (rounds(i, u) + 1))
                    for q in range(GC):
                        if not (isinstance(n, int) and n < 2):
                            pe.wait_ge(m.added, g0 + GC * (n - 2) + q + 1)
                        for j in range(G):
                            last = pe.matmul(ps_sum[GC * (u % 2) + q][:, 0:summed_cols], onehot[:, u % R, G * q + j, :],
                                             rows[:, u % R, G * q + j, 0:summed_cols],
                                             start=(j == 0), stop=(j == G - 1))
                        last.then_inc(m.summed, 1)

                if weights:
                    turn_onehot(0, 0)
                    turn_onehot(1, 1)
                    own_scores(0, 0, load_blocks(2 * GC))

                def body(i):
                    if weights:
                        blocks = load_blocks(GB * i + 3 * GC)
                    for u in range(U):
                        n = U * i + u
                        if weights and not (isinstance(n, int) and n + 1 >= CHUNKS):
                            own_scores(n + 1, u + 1, blocks[GC * u:GC * u + GC])
                        if weights and not (isinstance(n, int) and n + 2 >= CHUNKS):
                            turn_onehot(n + 2, u + 2)
                        if u > 0:
                            sums(n - 1, i, u - 1)
                        elif not is_first(i):
                            sums(n - 1, i - 1, U - 1)

                turns(pe, BODIES, body)
                sums(CHUNKS - 1, BODIES - 1, U - 1)

            @block.vector
            def _(dve):
                regs = [dve.alloc_register(f"dve_block{q}_{table}") for q in range(GB)]
                steps = Tally(at["vec"])

                def step(ins):
                    ins.then_inc(m.vec_step, 1)
                    return steps.next()

                def number_nodes(n, i, u):
                    dve.wait_ge(m.slots_in[u % U], at["slots"] + 16 * (i + u // U + 1))
                    return step(dve.tensor_copy(node[:, u % R, :], slots[:, u % U, :, 1]))

                def build_onehot(n, u, numbered):
                    if not (isinstance(n, int) and n < R):
                        dve.wait_ge(m.summed, g0 + GC * (n - R + 1))
                    dve.wait_ge(m.vec_step, numbered)
                    if weights:
                        dve.tensor_scalar(pad[:, u % R, :], node[:, u % R, :], float(P), BIG if mode == "neg" else -BIG,
                                          ALU.is_ge, ALU.mult).then_inc(m.padded, 1)
                    dve.tensor_tensor(onehot[:, u % R, :, :], iota_b, wide(node[:, u % R, :].rearrange("p (c n) -> p c n", n=1), [P, C, P]),
                                      ALU.is_equal).then_inc(m.onehot_built, 1)

                def score_steps(n, i, u):
                    mine = ps_own[u % 2][:, 0:C * 8].rearrange("p (c h) -> p c h", h=8)
                    r, s = raw[:, u % 2, :, 0:heads], score[:, u % 2, :, 0:heads]
                    dve.wait_ge(m.own_scored, w0 + n + 1)
                    dve.wait_ge(m.gathered[u % R], at["gathered"] + 16 * C * (rounds(i, u) + 1))
                    if mode == "neg" and not (isinstance(n, int) and n < 2):
                        dve.wait_ge(m.weighted, w0 + n - 1)
                    yield step(dve.tensor_tensor(r, mine[:, :, 0:heads], rows[:, u % R, :, feat:feat + heads], ALU.add))
                    yield step(dve.scalar_tensor_tensor(s, r, SLOPE, r, ALU.mult, ALU.max))
                    if mode == "shift":
                        yield step(dve.tensor_tensor(s, s, mine[:, :, heads:2 * heads], ALU.subtract))
                    dve.wait_ge(m.padded, w0 + n + 1)
                    last = dve.tensor_tensor(s, s, wide(pad[:, u % R, :].rearrange("p (c n) -> p c n", n=1), [P, C, heads]), ALU.add)
                    if mode == "gat":
                        yield step(last)
                        best = m.score_max[:].rearrange("p (c h) -> p c h", h=8)
                        last = dve.tensor_tensor(best, best, s, ALU.max)
                    last.then_inc(m.scored, 1)

                def weigh(u, j):
                    r = rows[:, u % R, j, 0:feat]
                    w = raw[:, u % 2, j, 0:heads] if mode == "neg" else rows[:, u % R, j, feat:feat + heads]
                    if heads == 1:
                        return dve.tensor_scalar(r, r, w, None, ALU.mult)
                    r = r.rearrange("p (h w) -> p h w", w=hw)
                    return dve.tensor_tensor(r, r, wide(w.rearrange("p (h w) -> p h w", w=1), [P, heads, hw]), ALU.mult)

                def add_sums(n, u, blocks):
                    for q in range(GC):
                        dve.wait_ge(m.summed, g0 + GC * n + q + 1)
                        wait(dve, m.added, g0 + GC * n + q)
                        place = acc[:, bass.ds(blocks[q], 1), :]
                        dve.tensor_tensor(place, place, ps_sum[GC * (u % 2) + q][:, 0:summed_cols].rearrange("p (b w) -> p b w", b=1),
                                          ALU.add).then_inc(m.added, 1)

                def load_blocks(start):
                    dve.reg_load(regs, m.group_block[way][0:1, bass.ds(start, GB)])
                    return [dve.snap(r, min_val=0, max_val=NB - 1) for r in regs]

                dve.wait_ge(m.vec_step, step(dve.memset(m.acc[:, 0:NB * summed_cols], 0.0)))
                for n in range(3):
                    build_onehot(n, n, number_nodes(n, 0, n))
                if weights:
                    for done in score_steps(0, 0, 0):
                        dve.wait_ge(m.vec_step, done)

                def body(i):
                    steps.turn(i)
                    blocks = load_blocks(GB * i)
                    for u in range(U):
                        n = U * i + u
                        last_one = isinstance(n, int) and n + 1 >= CHUNKS
                        last_three = isinstance(n, int) and n + 3 >= CHUNKS
                        if not last_three:
                            numbered = number_nodes(n + 3, i, u + 3)
                        if weights:
                            scores = iter(()) if last_one else score_steps(n + 1, i, u + 1)
                            done = next(scores, None)
                            dve.wait_ge(m.exped, w0 + n + 1)
                            for j in range(C):
                                last = weigh(u, j)
                                if j == C - 1:
                                    last.then_inc(m.weighted, 1)
                                if j == 0 and not last_three:
                                    build_onehot(n + 3, u + 3, numbered)
                                if done is not None:
                                    dve.wait_ge(m.vec_step, done)
                                    done = next(scores, None)
                            while done is not None:
                                dve.wait_ge(m.vec_step, done)
                                done = next(scores, None)
                        elif not last_three:
                            build_onehot(n + 3, u + 3, numbered)
                        if not (isinstance(n, int) and n < 2):
                            add_sums(n - 2, u, blocks[GC * u:GC * u + GC])

                turns(dve, BODIES, body)
                steps.settle()
                blocks = load_blocks(GROUPS)
                add_sums(CHUNKS - 2, 0, blocks[0:GC])
                add_sums(CHUNKS - 1, 1, blocks[GC:2 * GC])
                dve.wait_ge(m.added, g0 + GROUPS)
                m.at["vec"] = steps.value

    m.at["chunk"] += CHUNKS
    if weights:
        m.at["wchunk"] += CHUNKS
    m.at["gathered"] += 16 * C * 2 * BODIES
    m.at["slots"] += 16 * BODIES


def make_products(pe, m, ph, p, tiles, w, cols):
    def turned(kb):
        wait(pe, m.x_copied, p + kb - (kb > 0))
        parts = tiles(kb)
        for c, part in enumerate(parts):
            last = pe.transpose(ph.ps_x[kb % 2][:, c * P:(c + 1) * P], part, m.ident[:])
        last.then_inc(m.x_turned, 1)
        return len(parts)

    n = turned(0)
    for kb in range(KB):
        if kb + 1 < KB:
            turned(kb + 1)
        pe.wait_ge(m.x_copied, p + kb + 1)
        wait(pe, m.product_taken, p + kb - (kb > 0))
        for c in range(n):
            for a in range(0, cols, 512):
                b = min(a + 512, cols)
                last = pe.matmul(ph.ps_y[kb % 2][:, a:b], ph.xT[:, kb % 2, c * P:(c + 1) * P], w[:, c, a:b],
                                 start=(c == 0), stop=(c == n - 1))
        last.then_inc(m.product, 1)


def copy_turned(act, m, ph, p, n):
    for kb in range(KB):
        act.wait_ge(m.x_turned, p + kb + 1)
        wait(act, m.product, p + kb - (kb > 0))
        act.copy(ph.xT[:, kb % 2, 0:n * P], ph.ps_x[kb % 2][:, 0:n * P]).then_inc(m.x_copied, 1)


def take_products(dve, m, ph, p, take):
    for kb in range(KB):
        dve.wait_ge(m.product, p + kb + 1)
        take(kb, ph.ps_y[kb % 2]).then_inc(m.product_taken, 1)


def normalize(dve, m, ph, v, y):
    for kb in range(KB):
        last = dve.bn_stats(ph.stats[:, kb, :], y[:, kb, :])
    v.settled(last)
    st, s = ph.stats, ph.small
    dve.tensor_tensor(s[:, :, 0], st[:, :, 1], st[:, :, 4], ALU.add)
    dve.tensor_tensor(s[:, :, 1], st[:, :, 1], st[:, :, 4], ALU.subtract)
    v.settled(dve.tensor_tensor(s[:, :, 2], st[:, :, 2], st[:, :, 5], ALU.add))
    dve.tensor_scalar(s[:, :, 3], s[:, :, 0], -0.5, None, ALU.mult)
    v.settled(dve.scalar_tensor_tensor(s[:, :, 4], s[:, :, 1], 0.25, s[:, :, 1], ALU.mult, ALU.mult))
    v.settled(dve.scalar_tensor_tensor(s[:, :, 5], s[:, :, 2], 1.0 / D, s[:, :, 4], ALU.mult, ALU.add))
    v.hand_over(dve.tensor_scalar(s[:, :, 6], s[:, :, 5], LN_EPS, None, ALU.add))
    v.take_over()
    v.settled(dve.reciprocal(s[:, :, 0], s[:, :, 7]))
    for kb in range(KB):
        last = dve.tensor_scalar(y[:, kb, :], y[:, kb, :], s[:, kb, 3:4], s[:, kb, 0:1], ALU.add, ALU.mult)
    v.settled(last)


def root(act, m, ph, a):
    a.take_over()
    a.hand_over(act.activation(ph.small[:, :, 7], ph.small[:, :, 6], ACT.Sqrt))


def elu_parts(act, m, a, z, e):
    a.take_over()
    a.settled(act.activation(e, z, ACT.Relu, scale=-1.0))
    a.settled(act.activation(e, e, ACT.Exp, scale=-1.0))
    a.hand_over(act.activation(z, z, ACT.Relu))


class Hand:

    def __init__(self, eng, own, out, into, at_own, at_out, at_in):
        self.eng, self.own, self.out, self.into = eng, own, out, into
        self.steps, self.outs, self.ins = Tally(at_own), Tally(at_out), Tally(at_in)

    def settled(self, ins):
        ins.then_inc(self.own, 1)
        self.eng.wait_ge(self.own, self.steps.next())

    def hand_over(self, ins):
        ins.then_inc(self.out, 1)
        self.outs.next()

    def take_over(self):
        self.eng.wait_ge(self.into, self.ins.next())

    def turn(self, i):
        for t in (self.steps, self.outs, self.ins):
            t.turn(i)

    def settle(self):
        for t in (self.steps, self.outs, self.ins):
            t.settle()


def vector_side(dve, m):
    return Hand(dve, m.vec_step, m.for_act, m.for_vec, m.at["vec"], m.at["for_act"], m.at["for_vec"])


def scalar_side(act, m):
    return Hand(act, m.act_step, m.for_vec, m.for_act, m.at["act"], m.at["for_vec"], m.at["for_act"])


def rows_of(table, i):
    return table.rearrange("(b p) w -> p b w", p=P)[:, bass.ds(i * KB, KB), :]


def fold(pe, m, ps, rows, heads, n_rows, n_cols, count):
    for k in range(n_cols):
        for c in range(n_rows):
            last = pe.matmul(ps[:, k * 16:k * 16 + count], rows[:, c, k * P:(k + 1) * P], heads[:, c, 0:count],
                             start=(c == 0), stop=(c == n_rows - 1))
    return last


class NodePhase:

    def __init__(self, nc, m, name):
        self.nc, self.m, self.name = nc, m, name
        self.scope = ExitStack()

    def sb(self, name, shape, dt=F32):
        return self.scope.enter_context(self.nc.sbuf_tensor(f"{name}_{self.name}", shape, dt))

    def buffers(self, parts):
        self.stats = self.sb("stats", [P, KB, 6])
        self.small = self.sb("small", [P, KB, 8])
        self.xT = self.sb("xT", [P, 2, parts * P])
        self.ps_x = [self.scope.enter_context(self.nc.psum_tensor(f"ps_x{k}_{self.name}", [P, 512], F32)) for k in range(2)]
        self.ps_y = [self.scope.enter_context(self.nc.psum_tensor(f"ps_y{k}_{self.name}", [P, 1024], F32)) for k in range(2)]
        self.ps_f = self.scope.enter_context(self.nc.psum_tensor(f"ps_f_{self.name}", [P, 512], F32))

    def traffic(self, sp, weights, loads, stores):
        m = self.m
        for tile, src in weights:
            sp.dma_start(tile, src).then_inc(m.weights_in, 16)

        def body(i):
            for tile, table in loads:
                sp.dma_start(tile, rows_of(table, i)).then_inc(m.rows_in, 16)
            sp.wait_ge(m.rows_made, m.at["rows_made"] + i + 1)
            for tile, table in stores:
                sp.dma_start(rows_of(table, i), tile).then_inc(m.rows_out, 16)
            if stores:
                sp.wait_ge(m.rows_out, m.at["rows_out"] + 16 * len(stores) * (i + 1))
                sp.sem_inc(m.sync_passed, 1)

        turns(sp, BATCHES, body)

    def close(self, weights, loads, stores, products, for_pe, sides):
        at = self.m.at
        at["weights_in"] += 16 * len(weights)
        at["rows_in"] += 16 * len(loads) * BATCHES
        at["rows_out"] += 16 * len(stores) * BATCHES
        at["rows_made"] += BATCHES
        at["product"] += products * KB * BATCHES
        at["for_pe"] += for_pe * BATCHES
        v, a = sides
        at["vec"] = v.steps.value
        assert v.outs.value == (a.ins.value if a else v.outs.value)
        assert v.ins.value == (a.outs.value if a else v.ins.value)
        at["for_act"], at["for_vec"] = v.outs.value, v.ins.value
        if a:
            at["act"] = a.steps.value
        self.scope.close()


def per_block(row, shape):
    return row.rearrange("p (b w) -> p b w", b=1).to_broadcast(shape)


def per_row(col, shape):
    return col.rearrange("p (b w) -> p b w", w=1).to_broadcast(shape)


def on_all(row):
    return row.rearrange("(a n) -> a n", a=1).to_broadcast([P, row.shape[0]])


def chunks_of(w):
    return w.rearrange("(c p) n -> p c n", p=P)


def phase_0(nc, m, A):
    ph = NodePhase(nc, m, "n0")
    ph.buffers(2)
    x = ph.sb("x", [P, KB, D])
    rows = ph.sb("rows", [P, KB, D + 9])
    w = ph.sb("w", [P, 2, D + 16])
    wr = ph.sb("wr", [P, 2, D])
    heads = ph.sb("heads", [P, 2, 16])
    top = ph.sb("top", [P, 16])
    top_all = ph.sb("top_all", [P, 16])
    both = ph.sb("both", [P, 8])
    one = ph.sb("one", [P, 2])
    weights = [(w[:, :, 0:D], chunks_of(A["L0_WpT"])), (wr[:], chunks_of(A["L0_gnn_Wp"])), (heads[:], chunks_of(A["L0_heads"]))]
    loads, stores = [(x[:], A["x"])], [(rows[:], m.T[0])]
    at = dict(m.at)
    sides = [None, None]
    with nc.Block() as block:
        @block.sync
        def _(sp):
            ph.traffic(sp, weights, loads, stores)

        @block.tensor
        def _(pe):
            pe.wait_ge(m.weights_in, at["weights_in"] + 16 * len(weights))
            fold(pe, m, ph.ps_f, wr, heads, 2, 2, 16).then_inc(m.folded, 1)
            pe.wait_ge(m.fold_taken, at["fold"] + 1)

            def body(i):
                pe.wait_ge(m.rows_in, at["rows_in"] + 16 * (i + 1))
                make_products(pe, m, ph, at["product"] + KB * i, lambda kb: [x[:, kb, 0:P], x[:, kb, P:D]], w, D + 16)

            turns(pe, BATCHES, body)

        @block.scalar
        def _(act):
            turns(act, BATCHES, lambda i: copy_turned(act, m, ph, at["product"] + KB * i, 2))

        @block.vector
        def _(dve):
            v = sides[0] = vector_side(dve, m)
            dve.wait_ge(m.folded, at["fold"] + 1)
            dve.wait_ge(m.weights_in, at["weights_in"] + 16 * len(weights))
            dve.tensor_copy(w[:, :, D:D + 16], ph.ps_f[:, 0:32].rearrange("p (c h) -> p c h", h=16)).then_inc(m.fold_taken, 1)
            v.settled(dve.memset(rows[:, :, D + 8:D + 9], 1.0))

            def body(i):
                v.turn(i)
                dve.wait_ge(m.rows_in, at["rows_in"] + 16 * (i + 1))

                def take(kb, y):
                    dve.tensor_copy(m.sall[:, bass.ds(i * KB + kb, 1), :], y[:, D:D + 16].rearrange("p (b h) -> p b h", b=1))
                    return dve.tensor_copy(rows[:, kb, 0:D + 8], y[:, 0:D + 8])

                take_products(dve, m, ph, at["product"] + KB * i, take)
                dve.wait_ge(m.product_taken, at["product"] + KB * (i + 1))
                dve.memset(m.mark[:], 0.0).then_inc(m.rows_made, 1)

            turns(dve, BATCHES, body)
            v.settle()
            dve.tensor_reduce(top[:], m.sall[:].rearrange("p b h -> p h b"), AX_X, ALU.max).then_inc(m.for_pool, 1)
            dve.wait_ge(m.from_pool, at["pool"] + 1)
            v.settled(dve.tensor_tensor(both[:], top_all[:, 0:8], top_all[:, 8:16], ALU.add))
            v.settled(dve.tensor_reduce(one[:, 0:1], both[:], AX_X, ALU.max))
            v.settled(dve.scalar_tensor_tensor(one[:, 1:2], one[:, 0:1], SLOPE, one[:, 0:1], ALU.mult, ALU.max))
            v.settled(dve.tensor_scalar(m.neg_bound[:], one[:, 1:2], -1.0, None, ALU.mult))
            v.settle()

        @block.gpsimd
        def _(pool):
            pool.wait_ge(m.for_pool, at["pool"] + 1)
            pool.partition_all_reduce(top_all[:], top[:], P, RMAX).then_inc(m.from_pool, 1)

    m.at["pool"] += 1
    m.at["fold"] += 1
    ph.close(weights, loads, stores, 1, 0, sides)


def phase_1(nc, m, A):
    ph = NodePhase(nc, m, "n1")
    ph.buffers(2)
    x = ph.sb("x", [P, KB, D])
    z = ph.sb("z", [P, KB, D])
    e = ph.sb("e", [P, KB, D])
    den = ph.sb("den", [P, KB, 8])
    w = ph.sb("w", [P, 2, D])
    bias = ph.sb("bias", [P, D])
    top = ph.sb("top", [P, 1])
    top_all = ph.sb("top_all", [P, 1])
    weights = [(w[:], chunks_of(A["L0_WskipT"])), (bias[:], on_all(A["L0_gnn_bias"]))]
    loads, stores = [(x[:], A["x"])], [(e[:], m.T[1])]
    at = dict(m.at)
    sides = [None, None]
    acc = m.acc_view
    with nc.Block() as block:
        @block.sync
        def _(sp):
            ph.traffic(sp, weights, loads, stores)

        @block.tensor
        def _(pe):
            pe.wait_ge(m.weights_in, at["weights_in"] + 16 * len(weights))

            def body(i):
                pe.wait_ge(m.rows_in, at["rows_in"] + 16 * (i + 1))
                make_products(pe, m, ph, at["product"] + KB * i, lambda kb: [x[:, kb, 0:P], x[:, kb, P:D]], w, D)

            turns(pe, BATCHES, body)

        @block.scalar
        def _(act):
            a = sides[1] = scalar_side(act, m)
            a.take_over()
            a.hand_over(act.activation(m.eps_col[:], top_all[:], ACT.Exp, bias=m.neg_bound[:, 0:1]))

            def body(i):
                a.turn(i)
                copy_turned(act, m, ph, at["product"] + KB * i, 2)
                elu_parts(act, m, a, z[:], e[:])
                root(act, m, ph, a)

            turns(act, BATCHES, body)
            a.settle()

        @block.gpsimd
        def _(pool):
            pool.wait_ge(m.for_pool, at["pool"] + 1)
            pool.partition_all_reduce(top_all[:], top[:], P, RMAX).then_inc(m.from_pool, 1)

        @block.vector
        def _(dve):
            v = sides[0] = vector_side(dve, m)
            dve.tensor_reduce(top[:], m.score_max[:], AX_X, ALU.max).then_inc(m.for_pool, 1)
            dve.wait_ge(m.from_pool, at["pool"] + 1)
            v.hand_over(dve.memset(m.mark[:], 0.0))
            v.take_over()
            v.settled(dve.tensor_scalar(m.eps_col[:], m.eps_col[:], 1e-16, None, ALU.mult))
            v.settled(dve.tensor_scalar(m.rcnt[:], acc[:, :, D + 8], 1.0, None, ALU.max))
            v.settled(dve.reciprocal(m.rcnt[:], m.rcnt[:]))
            dve.wait_ge(m.weights_in, at["weights_in"] + 16 * len(weights))

            def body(i):
                v.turn(i)
                dve.wait_ge(m.rows_in, at["rows_in"] + 16 * (i + 1))
                v.settled(dve.tensor_scalar(den[:], acc[:, bass.ds(i * KB, KB), D:D + 8], m.eps_col[:, 0:1], None, ALU.add))
                v.settled(dve.reciprocal(den[:], den[:]))
                for kb in range(KB):
                    last = dve.tensor_tensor(z[:, kb, :].rearrange("p (h w) -> p h w", h=8),
                                             acc[:, bass.ds(i * KB + kb, 1), 0:D].rearrange("p b (h w) -> p (b h) w", h=8),
                                             den[:, kb, :].rearrange("p (h w) -> p h w", w=1).to_broadcast([P, 8, D // 8]), ALU.mult)
                v.settled(last)
                take_products(dve, m, ph, at["product"] + KB * i,
                              lambda kb, y: dve.tensor_tensor(z[:, kb, :], z[:, kb, :], y[:, 0:D], ALU.add))
                dve.wait_ge(m.product_taken, at["product"] + KB * (i + 1))
                v.hand_over(dve.tensor_tensor(z[:], z[:], per_block(bias[:], [P, KB, D]), ALU.add))
                v.take_over()
                v.settled(dve.scalar_tensor_tensor(e[:], e[:], -1.0, z[:], ALU.add, ALU.add))
                v.settled(dve.tensor_tensor(e[:], e[:], x[:], ALU.add))
                normalize(dve, m, ph, v, e)
                dve.memset(m.mark[:], 0.0).then_inc(m.rows_made, 1)

            turns(dve, BATCHES, body)
            v.settle()

    m.at["pool"] += 1
    ph.close(weights, loads, stores, 1, 0, sides)


def phase_sage(nc, m, A, layer):
    last_one = layer == 2
    ph = NodePhase(nc, m, f"n{layer + 1}")
    ph.buffers(4)
    h = ph.sb("h", [P, KB, D])
    mean = ph.sb("mean", [P, KB, D])
    z = ph.sb("z", [P, KB, D])
    w = ph.sb("w", [P, 4, D])
    bias = ph.sb("bias", [P, 3, D])
    name = f"L1_gnn_"
    weights = [(w[:, 0:2, :], chunks_of(A[f"{name}W_l{layer}"])), (w[:, 2:4, :], chunks_of(A[f"{name}W_r{layer}"])),
               (bias[:, 0, :], on_all(A[f"{name}b_l{layer}"])), (bias[:, 1, :], on_all(A[f"{name}ln{layer}_g"])),
               (bias[:, 2, :], on_all(A[f"{name}ln{layer}_b"]))]
    loads, stores = [(h[:], m.T[layer])], [(z[:], m.T[2])]
    if last_one:
        F = 2 * D
        x1 = ph.sb("x1", [P, KB, D])
        w2 = ph.sb("w2", [P, 2, F + 16])
        wr2 = ph.sb("wr2", [P, 4, D])
        heads = ph.sb("heads", [P, 4, 16])
        bias2 = ph.sb("bias2", [P, F + 16])
        bcol = ph.sb("bcol", [P, 4])
        brep = ph.sb("brep", [P, 4, P])
        rows = ph.sb("rows", [P, KB, F + 8])
        weights += [(w2[:, :, 0:F], chunks_of(A["L2_WT"])), (wr2[:], chunks_of(A["L2_W"])), (heads[:], chunks_of(A["L2_heads"])),
                    (bias2[:, 0:F], on_all(A["L2_b"])), (bcol[:], A["L2_b"].rearrange("(c p) -> p c", p=P))]
        loads.append((x1[:], m.T[1]))
        stores = [(z[:], m.x2), (rows[:], m.T[3])]
    products = 2 if last_one else 1
    at = dict(m.at)
    sides = [None, None]
    acc = m.acc_view
    with nc.Block() as block:
        @block.sync
        def _(sp):
            with nc.allow_non_contiguous_dma(reason="a small vector as columns"):
                ph.traffic(sp, weights, loads, stores)

        @block.tensor
        def _(pe):
            pe.wait_ge(m.weights_in, at["weights_in"] + 16 * len(weights))
            if last_one:
                fold(pe, m, ph.ps_f, wr2, heads, 4, 2, 16).then_inc(m.folded, 1)
                pe.wait_ge(m.fold_taken, at["fold"] + 1)
                for c in range(4):
                    last = pe.matmul(ph.ps_f[:, 64:80], brep[:, c, :], heads[:, c, :], start=(c == 0), stop=(c == 3))
                last.then_inc(m.folded, 1)
                pe.wait_ge(m.fold_taken, at["fold"] + 2)

            def body(i):
                pe.wait_ge(m.rows_in, at["rows_in"] + 16 * len(loads) * (i + 1))
                pe.wait_ge(m.for_pe, at["for_pe"] + products * i + 1)
                p = at["product"] + products * KB * i
                make_products(pe, m, ph, p, lambda kb: [mean[:, kb, 0:P], mean[:, kb, P:D], h[:, kb, 0:P], h[:, kb, P:D]], w, D)
                if last_one:
                    pe.wait_ge(m.for_pe, at["for_pe"] + products * i + 2)
                    make_products(pe, m, ph, p + KB, lambda kb: [z[:, kb, 0:P], z[:, kb, P:D]], w2, F + 16)

            turns(pe, BATCHES, body)

        @block.scalar
        def _(act):
            a = sides[1] = scalar_side(act, m)

            def body(i):
                a.turn(i)
                p = at["product"] + products * KB * i
                copy_turned(act, m, ph, p, 4)
                root(act, m, ph, a)
                a.take_over()
                a.hand_over(act.activation(z[:], z[:], ACT.Relu))
                if last_one:
                    root(act, m, ph, a)
                    copy_turned(act, m, ph, p + KB, 2)

            turns(act, BATCHES, body)
            a.settle()

        @block.vector
        def _(dve):
            v = sides[0] = vector_side(dve, m)
            dve.wait_ge(m.weights_in, at["weights_in"] + 16 * len(weights))
            if last_one:
                dve.wait_ge(m.folded, at["fold"] + 1)
                dve.tensor_copy(w2[:, :, F:F + 16], ph.ps_f[:, 0:32].rearrange("p (c h) -> p c h", h=16))
                dve.tensor_copy(brep[:], bcol[:].rearrange("p (c n) -> p c n", n=1).to_broadcast([P, 4, P])).then_inc(m.fold_taken, 1)
                dve.wait_ge(m.folded, at["fold"] + 2)
                v.settled(dve.tensor_copy(bias2[:, F:F + 16], ph.ps_f[:, 64:80]))
                dve.memset(m.mark[:], 0.0).then_inc(m.fold_taken, 1)

            def body(i):
                v.turn(i)
                p = at["product"] + products * KB * i
                dve.wait_ge(m.rows_in, at["rows_in"] + 16 * len(loads) * (i + 1))
                dve.tensor_tensor(mean[:], acc[:, bass.ds(i * KB, KB), :],
                                  m.rcnt[:, bass.ds(i * KB, KB)].rearrange("p (b w) -> p b w", w=1).to_broadcast([P, KB, D]),
                                  ALU.mult).then_inc(m.for_pe, 1)
                take_products(dve, m, ph, p, lambda kb, y: dve.tensor_tensor(z[:, kb, :], y[:, 0:D], bias[:, 0, :], ALU.add))
                dve.wait_ge(m.product_taken, p + KB)
                normalize(dve, m, ph, v, z)
                v.settled(dve.tensor_tensor(z[:], z[:], per_block(bias[:, 1, :], [P, KB, D]), ALU.mult))
                v.hand_over(dve.tensor_tensor(z[:], z[:], per_block(bias[:, 2, :], [P, KB, D]), ALU.add))
                v.take_over()
                if last_one:
                    v.settled(dve.tensor_tensor(z[:], z[:], x1[:], ALU.add))
                    normalize(dve, m, ph, v, z)
                    dve.memset(m.mark[:], 0.0).then_inc(m.for_pe, 1)

                    def take(kb, y):
                        dve.tensor_tensor(m.sall[:, bass.ds(i * KB + kb, 1), 8:16], y[:, F + 8:F + 16].rearrange("p (b h) -> p b h", b=1),
                                          bias2[:, F + 8:F + 16].rearrange("p (b h) -> p b h", b=1), ALU.add)
                        return dve.tensor_tensor(rows[:, kb, :], y[:, 0:F + 8], bias2[:, 0:F + 8], ALU.add)

                    take_products(dve, m, ph, p + KB, take)
                    dve.wait_ge(m.product_taken, p + 2 * KB)
                dve.memset(m.mark[:], 0.0).then_inc(m.rows_made, 1)

            turns(dve, BATCHES, body)
            v.settle()

    if last_one:
        m.at["fold"] += 2
    ph.close(weights, loads, stores, products, products, sides)


def phase_4(nc, m, A):
    ph = NodePhase(nc, m, "n4")
    ph.buffers(4)
    F, H = 2 * D, 8
    HW = F // H
    z = ph.sb("z", [P, KB, F])
    e = ph.sb("e", [P, KB, F])
    rows = ph.sb("rows", [P, KB, D + 1])
    mu = ph.sb("mu", [P, KB * H])
    var = ph.sb("var", [P, KB * H])
    w = ph.sb("w", [P, 4, D + 2])
    wr = ph.sb("wr", [P, 2, F])
    heads = ph.sb("heads", [P, 2, 16])
    gain = ph.sb("gain", [P, 2, F])
    bias = ph.sb("bias", [P, D + 2])
    bcol = ph.sb("bcol", [P, 2])
    brep = ph.sb("brep", [P, 2, P])
    weights = [(w[:, :, 0:D], chunks_of(A["L2_WoutT"])), (wr[:], chunks_of(A["L2_gnn_W_out"])), (heads[:, :, 0:2], chunks_of(A["L2_out_heads"])),
               (gain[:, 0, :], on_all(A["L2_g"])), (gain[:, 1, :], on_all(A["L2_beta"])),
               (bias[:, 0:D], on_all(A["L2_gnn_b_out"])), (bcol[:], A["L2_gnn_b_out"].rearrange("(c p) -> p c", p=P))]
    loads, stores = [], [(rows[:], m.T[4])]
    at = dict(m.at)
    sides = [None, None]
    acc = m.acc_view
    with nc.Block() as block:
        @block.sync
        def _(sp):
            with nc.allow_non_contiguous_dma(reason="a small vector as columns"):
                ph.traffic(sp, weights, loads, stores)

        @block.tensor
        def _(pe):
            pe.wait_ge(m.weights_in, at["weights_in"] + 16 * len(weights))
            fold(pe, m, ph.ps_f, wr, heads, 2, 4, 2).then_inc(m.folded, 1)
            pe.wait_ge(m.fold_taken, at["fold"] + 1)
            for c in range(2):
                last = pe.matmul(ph.ps_f[:, 80:82], brep[:, c, :], heads[:, c, 0:2], start=(c == 0), stop=(c == 1))
            last.then_inc(m.folded, 1)
            pe.wait_ge(m.fold_taken, at["fold"] + 2)

            def body(i):
                pe.wait_ge(m.for_pe, at["for_pe"] + i + 1)
                make_products(pe, m, ph, at["product"] + KB * i, lambda kb: [e[:, kb, c * P:(c + 1) * P] for c in range(4)], w, D + 2)

            turns(pe, BATCHES, body)

        @block.scalar
        def _(act):
            a = sides[1] = scalar_side(act, m)

            def body(i):
                a.turn(i)
                a.take_over()
                a.hand_over(act.activation(e[:], z[:], ACT.Square))
                a.take_over()
                a.hand_over(act.activation(var[:], var[:], ACT.Sqrt))
                elu_parts(act, m, a, z[:], e[:])
                copy_turned(act, m, ph, at["product"] + KB * i, 4)

            turns(act, BATCHES, body)
            a.settle()

        @block.vector
        def _(dve):
            v = sides[0] = vector_side(dve, m)
            dve.wait_ge(m.weights_in, at["weights_in"] + 16 * len(weights))
            dve.wait_ge(m.folded, at["fold"] + 1)
            dve.tensor_copy(w[:, :, D:D + 2], ph.ps_f[:, 0:64].rearrange("p (c h) -> p c h", h=16)[:, :, 0:2])
            dve.tensor_copy(brep[:], bcol[:].rearrange("p (c n) -> p c n", n=1).to_broadcast([P, 2, P])).then_inc(m.fold_taken, 1)
            dve.wait_ge(m.folded, at["fold"] + 2)
            v.settled(dve.tensor_copy(bias[:, D:D + 2], ph.ps_f[:, 80:82]))
            dve.memset(m.mark[:], 0.0).then_inc(m.fold_taken, 1)
            zh, eh = (t[:].rearrange("p b (h w) -> p (b h) w", h=H) for t in (z, e))

            def body(i):
                v.turn(i)
                if not is_first(i):
                    dve.wait_ge(m.rows_out, at["rows_out"] + 16 * i)
                sums = acc[:, bass.ds(i * KB, KB), :].rearrange("p b (h w) -> p (b h) w", h=H)
                v.settled(dve.tensor_reduce(mu[:], sums, AX_X, ALU.add))
                v.settled(dve.tensor_scalar(mu[:], mu[:], 1.0 / HW, None, ALU.mult))
                v.hand_over(dve.tensor_tensor(zh, sums, per_row(mu[:], [P, KB * H, HW]), ALU.subtract))
                v.take_over()
                v.settled(dve.tensor_reduce(var[:], eh, AX_X, ALU.add))
                v.hand_over(dve.tensor_scalar(var[:], var[:], 1.0 / HW, LN_EPS, ALU.mult, ALU.add))
                v.take_over()
                v.settled(dve.reciprocal(var[:], var[:]))
                v.settled(dve.tensor_tensor(zh, zh, per_row(var[:], [P, KB * H, HW]), ALU.mult))
                v.settled(dve.tensor_tensor(z[:], z[:], per_block(gain[:, 0, :], [P, KB, F]), ALU.mult))
                v.hand_over(dve.tensor_tensor(z[:], z[:], per_block(gain[:, 1, :], [P, KB, F]), ALU.add))
                v.take_over()
                dve.scalar_tensor_tensor(e[:], e[:], -1.0, z[:], ALU.add, ALU.add).then_inc(m.for_pe, 1)

                def take(kb, y):
                    dve.tensor_tensor(m.sall[:, bass.ds(i * KB + kb, 1), 8:9], y[:, D + 1:D + 2].rearrange("p (b h) -> p b h", b=1),
                                      bias[:, D + 1:D + 2].rearrange("p (b h) -> p b h", b=1), ALU.add)
                    return dve.tensor_tensor(rows[:, kb, :], y[:, 0:D + 1], bias[:, 0:D + 1], ALU.add)

                take_products(dve, m, ph, at["product"] + KB * i, take)
                dve.wait_ge(m.product_taken, at["product"] + KB * (i + 1))
                dve.memset(m.mark[:], 0.0).then_inc(m.rows_made, 1)

            turns(dve, BATCHES, body)
            v.settle()

    m.at["fold"] += 2
    ph.close(weights, loads, stores, 1, 1, sides)


def phase_5(nc, m, A):
    ph = NodePhase(nc, m, "n5")
    ph.buffers(2)
    x = ph.sb("x", [P, KB, D])
    z = ph.sb("z", [P, KB, D])
    e = ph.sb("e", [P, KB, D])
    rows = ph.sb("rows", [P, KB, D + 4])
    w = ph.sb("w", [P, 2, D + 8])
    wr = ph.sb("wr", [P, 2, D])
    heads = ph.sb("heads", [P, 2, 16])
    gain = ph.sb("gain", [P, 2, D])
    top = ph.sb("top", [P, 4])
    top_all = ph.sb("top_all", [P, 4])
    weights = [(w[:, :, 0:D], chunks_of(A["L3_gnn_W"])), (wr[:], chunks_of(A["L3_WT"])), (heads[:, :, 0:8], chunks_of(A["L3_heads"])),
               (gain[:, 0, :], on_all(A["L2_gnn_g_out"])), (gain[:, 1, :], on_all(A["L2_gnn_beta_out"]))]
    loads, stores = [(x[:], m.x2)], [(e[:], m.x3), (rows[:], m.T[5])]
    at = dict(m.at)
    sides = [None, None]
    acc = m.acc_view
    with nc.Block() as block:
        @block.sync
        def _(sp):
            ph.traffic(sp, weights, loads, stores)

        @block.tensor
        def _(pe):
            pe.wait_ge(m.weights_in, at["weights_in"] + 16 * len(weights))
            fold(pe, m, ph.ps_f, wr, heads, 2, 2, 8).then_inc(m.folded, 1)
            pe.wait_ge(m.fold_taken, at["fold"] + 1)

            def body(i):
                pe.wait_ge(m.for_pe, at["for_pe"] + i + 1)
                make_products(pe, m, ph, at["product"] + KB * i, lambda kb: [e[:, kb, 0:P], e[:, kb, P:D]], w, D + 8)

            turns(pe, BATCHES, body)

        @block.scalar
        def _(act):
            a = sides[1] = scalar_side(act, m)

            def body(i):
                a.turn(i)
                root(act, m, ph, a)
                elu_parts(act, m, a, z[:], e[:])
                root(act, m, ph, a)
                copy_turned(act, m, ph, at["product"] + KB * i, 2)

            turns(act, BATCHES, body)
            a.settle()

        @block.gpsimd
        def _(pool):
            pool.wait_ge(m.for_pool, at["pool"] + 1)
            pool.partition_all_reduce(top_all[:], top[:], P, RMAX).then_inc(m.from_pool, 1)

        @block.vector
        def _(dve):
            v = sides[0] = vector_side(dve, m)
            dve.wait_ge(m.weights_in, at["weights_in"] + 16 * len(weights))
            dve.wait_ge(m.folded, at["fold"] + 1)
            dve.tensor_copy(w[:, :, D:D + 8], ph.ps_f[:, 0:32].rearrange("p (c h) -> p c h", h=16)[:, :, 0:8]).then_inc(m.fold_taken, 1)

            def body(i):
                v.turn(i)
                dve.wait_ge(m.rows_in, at["rows_in"] + 16 * (i + 1))
                v.settled(dve.tensor_copy(z[:], acc[:, bass.ds(i * KB, KB), :]))
                normalize(dve, m, ph, v, z)
                v.settled(dve.tensor_tensor(z[:], z[:], per_block(gain[:, 0, :], [P, KB, D]), ALU.mult))
                v.hand_over(dve.tensor_tensor(z[:], z[:], per_block(gain[:, 1, :], [P, KB, D]), ALU.add))
                v.take_over()
                v.settled(dve.scalar_tensor_tensor(e[:], e[:], -1.0, z[:], ALU.add, ALU.add))
                v.settled(dve.tensor_tensor(e[:], e[:], x[:], ALU.add))
                normalize(dve, m, ph, v, e)
                dve.memset(m.mark[:], 0.0).then_inc(m.for_pe, 1)

                def take(kb, y):
                    s = m.sall[:, bass.ds(i * KB + kb, 1), :]
                    dve.tensor_copy(s[:, :, 8:12], y[:, D + 4:D + 8].rearrange("p (b h) -> p b h", b=1))
                    dve.tensor_copy(s[:, :, 0:4], y[:, D:D + 4].rearrange("p (b h) -> p b h", b=1))
                    return dve.tensor_copy(rows[:, kb, :], y[:, 0:D + 4])

                take_products(dve, m, ph, at["product"] + KB * i, take)
                dve.wait_ge(m.product_taken, at["product"] + KB * (i + 1))
                dve.memset(m.mark[:], 0.0).then_inc(m.rows_made, 1)

            turns(dve, BATCHES, body)
            v.settle()
            dve.tensor_reduce(top[:], m.sall[:, :, 0:4].rearrange("p b h -> p h b"), AX_X, ALU.max).then_inc(m.for_pool, 1)
            dve.wait_ge(m.from_pool, at["pool"] + 1)
            v.settled(dve.tensor_tensor(m.sall[:, :, 4:8], m.sall[:, :, 8:12], per_block(top_all[:], [P, NB, 4]), ALU.add))
            v.settled(dve.scalar_tensor_tensor(m.sall[:, :, 12:16], m.sall[:, :, 4:8], SLOPE, m.sall[:, :, 4:8], ALU.mult, ALU.max))
            v.settle()

    m.at["pool"] += 1
    m.at["fold"] += 1
    ph.close(weights, loads, stores, 1, 1, sides)


def phase_6(nc, m, A, out):
    ph = NodePhase(nc, m, "n6")
    ph.buffers(1)
    x = ph.sb("x", [P, KB, D])
    z = ph.sb("z", [P, KB, D])
    y = ph.sb("y", [P, KB, D])
    rows = ph.sb("rows", [P, KB, D + 4])
    s = ph.sb("s", [P, KB, 4])
    own = ph.sb("own", [P, KB, 4])
    den = ph.sb("den", [P, KB, 4])
    bias = ph.sb("bias", [P, 3, D])
    weights = [(bias[:, 0, :], on_all(A["L3_gnn_bias"])), (bias[:, 1, :], on_all(A["L3_gnn_gamma"])), (bias[:, 2, :], on_all(A["L3_gnn_beta"]))]
    loads, stores = [(x[:], m.x3), (rows[:], m.T[5])], [(z[:], out)]
    at = dict(m.at)
    sides = [None, None]
    acc = m.acc_view
    with nc.Block() as block:
        @block.sync
        def _(sp):
            ph.traffic(sp, weights, loads, stores)

        @block.scalar
        def _(act):
            a = sides[1] = scalar_side(act, m)

            def body(i):
                a.turn(i)
                a.take_over()
                a.hand_over(act.activation(own[:], s[:], ACT.Exp))
                a.take_over()
                a.hand_over(act.activation(z[:], z[:], ACT.Relu))
                root(act, m, ph, a)
                root(act, m, ph, a)

            turns(act, BATCHES, body)
            a.settle()

        @block.vector
        def _(dve):
            v = sides[0] = vector_side(dve, m)
            dve.wait_ge(m.weights_in, at["weights_in"] + 16 * len(weights))

            def body(i):
                v.turn(i)
                dve.wait_ge(m.rows_in, at["rows_in"] + 32 * (i + 1))
                mine = m.sall[:, bass.ds(i * KB, KB), :]
                v.settled(dve.tensor_tensor(s[:], rows[:, :, D:D + 4], mine[:, :, 8:12], ALU.add))
                v.settled(dve.scalar_tensor_tensor(s[:], s[:], SLOPE, s[:], ALU.mult, ALU.max))
                v.hand_over(dve.tensor_tensor(s[:], s[:], mine[:, :, 12:16], ALU.subtract))
                v.take_over()
                v.settled(dve.tensor_tensor(den[:], own[:], acc[:, bass.ds(i * KB, KB), D:D + 4], ALU.add))
                v.settled(dve.reciprocal(den[:], den[:]))
                for kb in range(KB):
                    last = dve.tensor_tensor(z[:, kb, :].rearrange("p (h w) -> p h w", h=4), rows[:, kb, 0:D].rearrange("p (h w) -> p h w", h=4),
                                             own[:, kb, :].rearrange("p (h w) -> p h w", w=1).to_broadcast([P, 4, D // 4]), ALU.mult)
                v.settled(last)
                v.settled(dve.tensor_tensor(z[:], z[:], acc[:, bass.ds(i * KB, KB), 0:D], ALU.add))
                for kb in range(KB):
                    zk = z[:, kb, :].rearrange("p (h w) -> p h w", h=4)
                    last = dve.tensor_tensor(zk, zk, den[:, kb, :].rearrange("p (h w) -> p h w", w=1).to_broadcast([P, 4, D // 4]), ALU.mult)
                v.settled(last)
                v.hand_over(dve.tensor_tensor(z[:], z[:], per_block(bias[:, 0, :], [P, KB, D]), ALU.add))
                v.take_over()
                v.settled(dve.tensor_tensor(z[:], z[:], x[:], ALU.add))
                normalize(dve, m, ph, v, z)
                v.settled(dve.tensor_tensor(z[:], z[:], per_block(bias[:, 1, :], [P, KB, D]), ALU.mult))
                v.settled(dve.tensor_tensor(z[:], z[:], per_block(bias[:, 2, :], [P, KB, D]), ALU.add))
                v.settled(dve.tensor_tensor(z[:], z[:], x[:], ALU.add))
                normalize(dve, m, ph, v, z)
                dve.memset(m.mark[:], 0.0).then_inc(m.rows_made, 1)

            turns(dve, BATCHES, body)
            v.settle()

    ph.close(weights, loads, stores, 0, 0, sides)


def build(nc, A, out):
    ctx = ExitStack()
    with ctx:
        def sb(name, shape, dt=F32):
            return ctx.enter_context(nc.sbuf_tensor(name, shape, dt))

        def sem(name):
            return ctx.enter_context(nc.semaphore(name))

        def dram(name, shape, dt=F32):
            return nc.dram_tensor(name, shape, dt, kind="Internal").ap()

        m = Shared()
        m.meta = [dram(f"slots_by_{k}", (P * TILES, 2), I32) for k in ("dst", "src")]
        m.T = [dram(f"table{k}", (NP, w)) for k, w in enumerate((D + 9, D, D, 2 * D + 8, D + 1, D + 4))]
        m.x2, m.x3 = dram("x2", (NP, D)), dram("x3", (NP, D))
        m.acc = sb("acc", [P, NB * 2 * D])
        m.sall = sb("sall", [P, NB, 16])
        m.rcnt = sb("rcnt", [P, NB])
        m.group_block = [sb(f"group_block{k}", [1, TG], I32) for k in range(2)]
        m.iota_row = sb("iota_row", [P, P])
        m.part_col = sb("part_col", [P, 1])
        m.ident = sb("ident", [P, P])
        m.ones = sb("ones", [P, P])
        m.neg_bound = sb("neg_bound", [P, 1])
        m.score_max = sb("score_max", [P, C * 8])
        m.eps_col = sb("eps_col", [P, 1])
        m.mark = sb("mark", [1, 1])

        m.consts_ready = sem("consts_ready")
        m.numbered = sem("numbered")
        m.loaded = sem("loaded")
        m.fill_made = sem("fill_made")
        m.prefilled = sem("prefilled")
        m.counted = sem("counted")
        m.summed_up = sem("summed_up")
        m.ended = sem("ended")
        m.slotted = sem("slotted")
        m.staged = sem("staged")
        m.scattered = [sem(f"scattered{h}") for h in range(2)]
        m.pool_passed = sem("pool_passed")
        m.sync_passed = sem("sync_passed")
        m.vec_step = sem("vec_step")
        m.act_step = sem("act_step")
        m.for_act = sem("for_act")
        m.for_vec = sem("for_vec")
        m.for_pe = sem("for_pe")
        m.for_pool = sem("for_pool")
        m.from_pool = sem("from_pool")
        m.weights_in = sem("weights_in")
        m.rows_in = sem("rows_in")
        m.rows_made = sem("rows_made")
        m.rows_out = sem("rows_out")
        m.folded = sem("folded")
        m.fold_taken = sem("fold_taken")
        m.x_turned = sem("x_turned")
        m.x_copied = sem("x_copied")
        m.product = sem("product")
        m.product_taken = sem("product_taken")
        m.slots_in = [sem(f"slots_in{u}") for u in range(U)]
        m.gathered = [sem(f"gathered{u}") for u in range(R)]
        m.onehot_built = sem("onehot_built")
        m.padded = sem("padded")
        m.onehot_turned = sem("onehot_turned")
        m.onehot_copied = sem("onehot_copied")
        m.own_scored = sem("own_scored")
        m.scored = sem("scored")
        m.exped = sem("exped")
        m.weighted = sem("weighted")
        m.summed = sem("summed")
        m.added = sem("added")

        m.at = {k: 0 for k in ("vec", "act", "for_act", "for_vec", "for_pe", "pool", "weights_in", "rows_in",
                               "rows_made", "rows_out", "fold", "product", "chunk", "wchunk",
                               "gathered", "slots")}

        with ExitStack() as sc:
            row_i = sc.enter_context(nc.sbuf_tensor("row_i", [P, P], I32))
            col_i = sc.enter_context(nc.sbuf_tensor("col_i", [P, 1], I32))
            with nc.Block() as block:
                @block.gpsimd
                def _(pool):
                    pool.iota(row_i[:], pattern=[[1, P]], base=0, channel_multiplier=0).then_inc(m.consts_ready, 1)
                    pool.iota(col_i[:], pattern=[[0, 1]], base=0, channel_multiplier=1).then_inc(m.consts_ready, 1)

                @block.vector
                def _(dve):
                    dve.memset(m.ones[:], 1.0)
                    dve.memset(m.score_max[:], -BIG)
                    dve.wait_ge(m.consts_ready, 2)
                    dve.tensor_copy(m.iota_row[:], row_i[:]).then_inc(m.consts_ready, 1)
                    dve.tensor_copy(m.part_col[:], col_i[:]).then_inc(m.consts_ready, 1)
                    dve.wait_ge(m.consts_ready, 4)
                    dve.tensor_scalar(m.ident[:], m.iota_row[:], m.part_col[:, 0:1], None, ALU.is_equal).then_inc(m.consts_ready, 1)
                    dve.wait_ge(m.consts_ready, 5)

        place_edges(nc, m, 0, A["dst"], A["src"])
        place_edges(nc, m, 1, A["src"], A["dst"])
        phase_0(nc, m, A)
        edge_phase(nc, m, way=0, table=0, width=D + 9, feat=D, heads=8, own=8, mode="gat")
        phase_1(nc, m, A)
        edge_phase(nc, m, way=0, table=1, width=D, feat=D, heads=0, own=0, mode="sum")
        phase_sage(nc, m, A, 1)
        edge_phase(nc, m, way=0, table=2, width=D, feat=D, heads=0, own=0, mode="sum")
        phase_sage(nc, m, A, 2)
        edge_phase(nc, m, way=1, table=3, width=2 * D + 8, feat=2 * D, heads=8, own=8, mode="neg")
        phase_4(nc, m, A)
        edge_phase(nc, m, way=1, table=4, width=D + 1, feat=D, heads=1, own=1, mode="neg")
        phase_5(nc, m, A)
        edge_phase(nc, m, way=0, table=5, width=D + 4, feat=D, heads=4, own=8, mode="shift")
        phase_6(nc, m, A, out)


def kernel(**inputs):
    import numpy as np
    from concourse import bacc
    from concourse.bass_utils import run_bass_kernel_spmd

    a = {k: np.asarray(v) for k, v in inputs.items()}

    def by_head(*vectors):
        h, w = vectors[0].shape
        out = np.zeros((h * w, h * len(vectors)), vectors[0].dtype)
        for n, v in enumerate(vectors):
            for k in range(h):
                out[k * w:(k + 1) * w, n * h + k] = v[k]
        return out

    x = np.zeros((NP, D), a["x"].dtype)
    x[:N_NODES] = a["x"]
    a_heads, a_out = a["L2_gnn_a_heads"], a["L2_gnn_a_out"].reshape(1, -1)
    half = a_heads.shape[1] // 2
    W2 = a["L2_gnn_W_heads"].reshape(-1, D)
    laid = {
        "x": x, "src": a["src"], "dst": a["dst"],
        "L0_WpT": a["L0_gnn_Wp"].T, "L0_gnn_Wp": a["L0_gnn_Wp"], "L0_WskipT": a["L0_gnn_Wskip"].T,
        "L0_heads": by_head(a["L0_gnn_a_src"][0], a["L0_gnn_a_trg"][0]), "L0_gnn_bias": a["L0_gnn_bias"],
        "L2_W": W2, "L2_WT": W2.T, "L2_b": a["L2_gnn_b_heads"].reshape(-1),
        "L2_heads": by_head(a_heads[:, half:], a_heads[:, :half]),
        "L2_g": a["L2_gnn_g_heads"].reshape(-1), "L2_beta": a["L2_gnn_beta_heads"].reshape(-1),
        "L2_gnn_W_out": a["L2_gnn_W_out"], "L2_WoutT": a["L2_gnn_W_out"].T, "L2_gnn_b_out": a["L2_gnn_b_out"],
        "L2_out_heads": by_head(a_out[:, D:], a_out[:, :D]),
        "L2_gnn_g_out": a["L2_gnn_g_out"], "L2_gnn_beta_out": a["L2_gnn_beta_out"],
        "L3_gnn_W": a["L3_gnn_W"], "L3_WT": a["L3_gnn_W"].T,
        "L3_heads": by_head(a["L3_gnn_att_src"], a["L3_gnn_att_dst"]),
        "L3_gnn_bias": a["L3_gnn_bias"], "L3_gnn_gamma": a["L3_gnn_gamma"], "L3_gnn_beta": a["L3_gnn_beta"],
    }
    for k in ("W_l1", "b_l1", "W_r1", "ln1_g", "ln1_b", "W_l2", "b_l2", "W_r2", "ln2_g", "ln2_b"):
        laid[f"L1_gnn_{k}"] = a[f"L1_gnn_{k}"]
    laid = {k: np.ascontiguousarray(v) for k, v in laid.items()}

    nc = bacc.Bacc("TRN2", target_bir_lowering=False, num_devices=1)
    A = {k: nc.dram_tensor(f"in_{k}", v.shape, mybir.dt.from_np(v.dtype), kind="ExternalInput").ap() for k, v in laid.items()}
    out = nc.dram_tensor("out", (NP, D), F32, kind="ExternalOutput").ap()
    build(nc, A, out)
    r = run_bass_kernel_spmd(nc, [{f"in_{k}": v for k, v in laid.items()}], core_ids=[0])
    return r.results[0]["out"][:N_NODES]
```

```python
from contextlib import ExitStack

import concourse.bass as bass
from concourse import mybir

F32 = mybir.dt.float32
BF16 = mybir.dt.bfloat16
I32 = mybir.dt.int32
ALU = mybir.AluOpType
ACT = mybir.ActivationFunctionType
AX_X = mybir.AxisListType.X
RMAX = bass.bass_isa.ReduceOp.max

P = 128
N_NODES = 6250
N_EDGES = 100000
D = 256
NB = -(-N_NODES // P)
KB = 5
STREAMS = 2
TURNS = -(-NB // (KB * STREAMS))
NN = TURNS * STREAMS * KB
NP = NN * P
EP = 125
EC = N_EDGES // EP
G = 2
C = 4
R = 5
U = 2 * R
GC = C // G
GB = GC * U
GROUPS = -(-((N_EDGES + NB * (G * P - 1)) // (G * P)) // GB) * GB
CHUNKS = GROUPS // GC
BODIES = CHUNKS // U
TILES = GROUPS * G
TG = 2 * GC + GROUPS + GB
SC = 8
STAGES = EC // SC
SLOTTED_AT = NB * EC // 2
BIG = 1.0e30
LN_EPS = 1e-5
SLOPE = 0.2
EMPTY = 200


class Shared:
    pass


class Tally:

    def __init__(self, start):
        self.start = start
        self.value = start
        self.n = 0
        self.per_turn = 0
        self.first = 0

    def turn(self, i, half=0):
        if half == 1:
            if isinstance(i, int) and i == 0:
                self.first = self.n
            self.value = self.start + i * self.per_turn
            self.n = self.first
            return
        if isinstance(i, int) and i == 0:
            self.settle()
            self.start, self.per_turn = self.value, 0
        else:
            self.per_turn = self.per_turn or self.n
            self.value = self.start + i * self.per_turn
        self.n = 0

    def next(self):
        self.n += 1
        return self.value + self.n

    def settle(self, turns=None):
        if turns is not None:
            self.value = self.start + (turns - 1) * self.per_turn
        self.value, self.n = self.value + self.n, 0


def wait(eng, sem, value):
    if isinstance(value, int) and value <= 0:
        return
    eng.wait_ge(sem, value)


def turns(eng, n, body):
    body(0)
    with eng.Fori(1, n - 1) as i:
        body(i)
    body(n - 1)


DONE = object()


def is_first(i):
    return isinstance(i, int) and i == 0


def wide(ap, shape):
    return ap.to_broadcast(shape)


def scatter_edges(pool, m, way, start, count):
    def pair(i):
        for h in range(2):
            part = 2 * i + h + start
            wait(pool, m.scattered[h], 16 * SC * (way * (STAGES // 2) + start // 2 + i))
            pool.sem_inc(m.pool_passed, 1)
            pool.tensor_copy(m.stage[:, h, :, :], m.slotted_edges[way][:, bass.ds(part * SC, SC), :]).then_inc(m.staged, 1)
            pool.wait_ge(m.staged, way * STAGES + part + 1)
            pool.sem_inc(m.pool_passed, 1)
            for j in range(SC):
                pool.indirect_dma_start(
                    m.meta[way], bass.IndirectOffsetOnAxis(ap=m.stage[:, h, j, 0:1], axis=0),
                    m.stage[:, h, j, 1:3], None).then_inc(m.scattered[h], 16)

    turns(pool, count // 2, pair)
    for h in range(2):
        pool.wait_ge(m.scattered[h], 16 * SC * (way * (STAGES // 2) + (start + count) // 2))


def place_edges(nc, m, way, key, other, scatters):
    sc = ExitStack()
    with sc:
        def sb(name, shape, dt=F32):
            return sc.enter_context(nc.sbuf_tensor(f"{name}_{way}", shape, dt))

        def ps(name):
            return sc.enter_context(nc.psum_tensor(f"{name}_{way}", [P, 512], F32))

        key_i = sb("key_i", [EP, EC], I32)
        other_i = sb("other_i", [EP, EC], I32)
        tile_i = sb("tile_i", [EP, EC], I32)
        slotted = m.slotted_edges[way]
        blk = sb("blk", [EP, EC], BF16)
        zero = sb("zero", [EP, EC], BF16)
        count = sb("count", [EP, EC])
        chosen = sb("chosen", [EP, EC])
        rank = sb("rank", [EP, EC])
        member = m.acc[:].bitcast(BF16)[0:EP, 0:NB * EC]
        below = sb("below", [P, P])
        total = sb("total", [EP, NB])
        groups_i = sb("groups_i", [P, NB], I32)
        groups_f = sb("groups_f", [P, NB])
        group_end = sb("group_end", [P, NB])
        zeros_b = sb("zeros_b", [P, NB])
        first = sb("first", [EP, NB])
        end_col = sb("end_col", [P, 1])
        group_i = sb("group_i", [NB, GROUPS], I32)
        passed = sb("passed", [NB, GROUPS])
        block_f = sb("block_f", [1, GROUPS])
        fill = sb("fill", [P, TILES, 2], I32)
        ps_before, ps_total, ps_end, ps_group = ps("ps_before"), ps("ps_total"), ps("ps_end"), ps("ps_group")
        chain0 = m.at["vec"]

        with nc.Block() as block:
            @block.sync
            def _(sp):
                sp.dma_start(key_i[:], key.rearrange("(p e) -> p e", e=EC)).then_inc(m.loaded, 16)
                sp.dma_start(other_i[:], other.rearrange("(p e) -> p e", e=EC)).then_inc(m.loaded, 16)
                if way == 0:
                    sp.wait_ge(m.fill_made, 2)
                    for slots in m.meta:
                        sp.dma_start(slots.rearrange("(p t) k -> p (t k)", p=P),
                                     fill[:].rearrange("p t k -> p (t k)")).then_inc(m.prefilled, 16)
                    sp.wait_ge(m.prefilled, 32)

            @block.gpsimd
            def _(pool):
                pool.iota(group_i[:], pattern=[[1, GROUPS]], base=0, channel_multiplier=0).then_inc(m.numbered, 1)
                scatters(pool)

            @block.tensor
            def _(pe):
                pe.wait_ge(m.counted, way + 1)
                pe.matmul(ps_before[0:EP, 0:NB], below[0:EP, 0:EP], total[:], start=True, stop=True)
                pe.matmul(ps_total[:, 0:NB], m.ones[0:EP, :], total[:], start=True, stop=True).then_inc(m.summed_up, 1)
                pe.wait_ge(m.ended, 2 * way + 1)
                pe.matmul(ps_end[0:NB, 0:1], group_end[0:1, 0:NB], m.ones[0:1, 0:1], start=True, stop=True).then_inc(m.summed_up, 1)
                pe.wait_ge(m.ended, 2 * way + 2)
                pe.matmul(ps_group[0:1, 0:GROUPS], m.ones[0:NB, 0:1], passed[:], start=True, stop=True).then_inc(m.summed_up, 1)

            @block.vector
            def _(dve):
                chain = Tally(chain0)

                def settled(ins):
                    ins.then_inc(m.vec_step, 1)
                    dve.wait_ge(m.vec_step, chain.next())

                if way == 0:
                    dve.memset(fill[:, :, 0:1], 0).then_inc(m.fill_made, 1)
                    dve.memset(fill[:, :, 1:2], EMPTY).then_inc(m.fill_made, 1)
                dve.memset(zero[:], 0.0)
                dve.memset(zeros_b[:], 0.0)
                dve.memset(rank[:], 0.0)
                dve.memset(m.group_block[way][:], 0)
                dve.tensor_scalar(below[:], m.iota_row[:], m.part_col[:, 0:1], None, ALU.is_gt)
                dve.wait_ge(m.loaded, 32 * (way + 1))
                dve.tensor_copy(slotted[:, :, 1], other_i[:])
                dve.tensor_scalar(slotted[:, :, 2], key_i[:], P - 1, None, ALU.bitwise_and)
                settled(dve.tensor_scalar(tile_i[:], key_i[:], 7, None, ALU.logical_shift_right))
                settled(dve.tensor_copy(blk[:], tile_i[:]))

                head = chain.value + chain.n
                with dve.Fori(0, NB) as b:
                    dve.tensor_scalar(member[:, bass.ds(b * EC, EC)], blk[:], m.iota_row[0:EP, bass.ds(b, 1)], 0.0,
                                      ALU.is_equal, ALU.add, accum_out=total[:, bass.ds(b, 1)]).then_inc(m.vec_step, 1)
                chain = Tally(head + NB)
                dve.wait_ge(m.vec_step, head + NB)
                dve.memset(m.mark[:], 0.0).then_inc(m.counted, 1)

                dve.wait_ge(m.summed_up, 3 * way + 1)
                settled(dve.tensor_scalar(groups_f[:], ps_total[:, 0:NB], float(G * P - 1), None, ALU.add))
                settled(dve.tensor_copy(groups_i[:], groups_f[:]))
                settled(dve.tensor_scalar(groups_i[:], groups_i[:], 8, None, ALU.logical_shift_right))
                settled(dve.tensor_copy(groups_f[:], groups_i[:]))
                dve.tensor_tensor_scan(group_end[:], groups_f[:], zeros_b[:], 0.0, ALU.add, ALU.add).then_inc(m.ended, 1)
                dve.wait_ge(m.ended, 2 * way + 1)
                settled(dve.tensor_tensor(groups_f[:], group_end[:], groups_f[:], ALU.subtract))
                settled(dve.scalar_tensor_tensor(first[:], groups_f[0:EP, :], float(G * P), ps_before[0:EP, 0:NB], ALU.mult, ALU.add))
                settled(dve.tensor_scalar(first[:], first[:], -1.0, None, ALU.add))

                dve.wait_ge(m.summed_up, 3 * way + 2)
                settled(dve.tensor_copy(end_col[0:NB, :], ps_end[0:NB, 0:1]))
                dve.wait_ge(m.numbered, way + 1)
                settled(dve.tensor_copy(passed[:], group_i[:]))
                dve.tensor_scalar(passed[:], passed[:], end_col[0:NB, 0:1], None, ALU.is_ge).then_inc(m.ended, 1)
                dve.wait_ge(m.summed_up, 3 * way + 3)
                settled(dve.tensor_scalar(block_f[:], ps_group[0:1, 0:GROUPS], float(NB - 1), None, ALU.min))
                settled(dve.tensor_copy(m.group_block[way][0:1, 2 * GC:2 * GC + GROUPS], block_f[:]))

                head = chain.value + chain.n
                with dve.Fori(0, NB) as b:
                    dve.tensor_tensor_scan(count[:], member[:, bass.ds(b * EC, EC)], zero[:], first[:, bass.ds(b, 1)], ALU.add, ALU.add).then_inc(m.vec_step, 1)
                    dve.wait_ge(m.vec_step, head + 3 * b + 1)
                    dve.tensor_tensor(chosen[:], count[:], member[:, bass.ds(b * EC, EC)], ALU.mult).then_inc(m.vec_step, 1)
                    dve.wait_ge(m.vec_step, head + 3 * b + 2)
                    dve.tensor_tensor(rank[:], rank[:], chosen[:], ALU.add).then_inc(m.vec_step, 1)
                    dve.wait_ge(m.vec_step, head + 3 * b + 3)
                chain = Tally(head + 3 * NB)

                settled(dve.tensor_copy(key_i[:], rank[:]))
                settled(dve.tensor_scalar(tile_i[:], key_i[:], 7, None, ALU.logical_shift_right))
                settled(dve.tensor_scalar(key_i[:], key_i[:], P - 1, None, ALU.bitwise_and))
                settled(dve.tensor_scalar(count[:], key_i[:], float(TILES), None, ALU.mult))
                dve.tensor_tensor(slotted[:, :, 0], count[:], tile_i[:], ALU.add).then_inc(m.slotted, 1)
                dve.wait_ge(m.slotted, way + 1)
                m.at["vec"] = chain.value + chain.n


def edge_phase(nc, m, way, table, width, feat, heads, own, mode):
    sc = ExitStack()
    summed_cols = feat if mode in ("sum", "neg") else width
    acc = m.acc[:, 0:NN * summed_cols].rearrange("p (b w) -> p b w", w=summed_cols)
    m.acc_view = acc
    weights = mode != "sum"
    T = m.T[table]
    at = dict(m.at)
    hw = feat // heads if heads else 0
    act_tiles = 1 if feat > D else 0
    slot_rows = m.meta[way].rearrange("(p t) k -> p t k", p=P)
    with sc:
        def sb(name, shape, dt=F32):
            return sc.enter_context(nc.sbuf_tensor(f"{name}_{table}", shape, dt))

        slots = sb("slots", [P, U, C, 2], I32)
        rows = sb("rows", [P, R, C, width])
        node = sb("node", [P, R, C])
        onehot = sb("onehot", [P, R, C, P])
        turned = sb("turned", [P, 2, C, P])
        raw = sb("raw", [P, 2, C, 8])
        score = sb("score", [P, 2, C, 8])
        pad = sb("pad", [P, R, C])
        ps_turned = [sc.enter_context(nc.psum_tensor(f"ps_turned{k}_{table}", [P, C, P], F32)) for k in range(2)]
        ps_own = [sc.enter_context(nc.psum_tensor(f"ps_own{k}_{table}", [P, 512], F32)) for k in range(2)]
        ps_sum = [sc.enter_context(nc.psum_tensor(f"ps_sum{k}_{table}", [P, 512], F32)) for k in range(2 * GC)]
        c0, w0, g0 = at["chunk"], at["wchunk"], at["chunk"] * GC
        iota_b = m.iota_row[:].rearrange("p (c n) -> p c n", c=1).to_broadcast([P, C, P])

        def rounds(i, u):
            return 2 * i + u // R

        with nc.Block() as block:
            @block.sync
            def _(sp):
                def body(i):
                    for u in range(U):
                        n = U * i + u
                        if not is_first(i):
                            sp.wait_ge(m.summed, g0 + GC * (n - U + 1))
                        sp.dma_start(slots[:, u, :, :], slot_rows[:, bass.ds(n * C, C), :]).then_inc(m.slots_in[u], 16)

                turns(sp, BODIES, body)

            @block.gpsimd
            def _(pool):
                def body(i):
                    for u in range(U):
                        n = U * i + u
                        if not (isinstance(n, int) and n < R):
                            pool.wait_ge(m.summed, g0 + GC * (n - R + 1))
                        pool.wait_ge(m.slots_in[u], at["slots"] + 16 * (i + 1))
                        pool.sem_inc(m.pool_passed, 1)
                        for j in range(C):
                            pool.indirect_dma_start(
                                rows[:, u % R, j, :], None, T,
                                bass.IndirectOffsetOnAxis(ap=slots[:, u, j, 0:1], axis=0)).then_inc(m.gathered[u % R], 16)

                turns(pool, BODIES, body)
                for r in range(R):
                    pool.wait_ge(m.gathered[r], at["gathered"] + 16 * C * 2 * BODIES)

            @block.scalar
            def _(act):
                if not weights:
                    return

                def copy_onehot(n, k):
                    act.wait_ge(m.onehot_turned, w0 + n + 1)
                    act.copy(turned[:, k, :, :], ps_turned[k][:]).then_inc(m.onehot_copied, 1)

                def weigh(n, u):
                    act.wait_ge(m.exped, w0 + n + 1)
                    for j in range(C - act_tiles, C):
                        for h in range(heads):
                            r = rows[:, u % R, j, h * hw:(h + 1) * hw]
                            last = act.activation(r, r, ACT.Copy, scale=raw[:, u % 2, j, h:h + 1])
                    last.then_inc(m.act_weighted, 1)

                def exponentials(n, u):
                    act.wait_ge(m.scored, w0 + n + 1)
                    out = raw[:, u % 2, :, 0:heads] if mode == "neg" else rows[:, u % R, :, feat:feat + heads]
                    act.activation(out, score[:, u % 2, :, 0:heads], ACT.Exp,
                                   bias=m.neg_bound[:, 0:1] if mode == "gat" else 0.0,
                                   scale=-1.0 if mode == "neg" else 1.0).then_inc(m.exped, 1)

                copy_onehot(0, 0)
                copy_onehot(1, 1)
                exponentials(0, 0)

                def body(i):
                    for u in range(U):
                        n = U * i + u
                        if not (isinstance(n, int) and n + 2 >= CHUNKS):
                            copy_onehot(n + 2, u % 2)
                        if not (isinstance(n, int) and n + 1 >= CHUNKS):
                            exponentials(n + 1, u + 1)
                        if act_tiles:
                            weigh(n, u)

                turns(act, BODIES, body)

            @block.tensor
            def _(pe):
                regs = [pe.alloc_register(f"pe_block{q}_{table}") for q in range(GB)]

                def load_blocks(start):
                    pe.reg_load(regs, m.group_block[way][0:1, bass.ds(start, GB)])
                    return [pe.snap(r, min_val=0, max_val=NB - 1) for r in regs]

                def turn_onehot(n, u):
                    pe.wait_ge(m.onehot_built, c0 + n + 1)
                    if not (isinstance(n, int) and n < 2):
                        pe.wait_ge(m.onehot_copied, w0 + n - 1)
                    for j in range(C):
                        last = pe.transpose(ps_turned[u % 2][:, j, :], onehot[:, u % R, j, :], m.ident[:])
                    last.then_inc(m.onehot_turned, 1)

                def own_scores(n, u, blocks):
                    pe.wait_ge(m.onehot_copied, w0 + n + 1)
                    if not (isinstance(n, int) and n < 2):
                        pe.wait_ge(m.scored, w0 + n - 1)
                    for j in range(C):
                        last = pe.matmul(ps_own[u % 2][:, j * 8:j * 8 + own], turned[:, u % 2, j, :],
                                         m.sall[:, bass.ds(blocks[j // G], 1), 8:8 + own],
                                         start=True, stop=True)
                    last.then_inc(m.own_scored, 1)

                def sums(n, i, u):
                    if weights:
                        pe.wait_ge(m.weighted, w0 + n + 1)
                        if act_tiles:
                            pe.wait_ge(m.act_weighted, n + 1)
                    else:
                        pe.wait_ge(m.onehot_built, c0 + n + 1)
                        pe.wait_ge(m.gathered[u % R], at["gathered"] + 16 * C * (rounds(i, u) + 1))
                    for q in range(GC):
                        if not (isinstance(n, int) and n < 2):
                            pe.wait_ge(m.added, g0 + GC * (n - 2) + q + 1)
                        for j in range(G):
                            last = pe.matmul(ps_sum[GC * (u % 2) + q][:, 0:summed_cols], onehot[:, u % R, G * q + j, :],
                                             rows[:, u % R, G * q + j, 0:summed_cols],
                                             start=(j == 0), stop=(j == G - 1))
                        last.then_inc(m.summed, 1)

                if weights:
                    turn_onehot(0, 0)
                    turn_onehot(1, 1)
                    own_scores(0, 0, load_blocks(2 * GC))

                def body(i):
                    if weights:
                        blocks = load_blocks(GB * i + 3 * GC)
                    for u in range(U):
                        n = U * i + u
                        if weights and not (isinstance(n, int) and n + 1 >= CHUNKS):
                            own_scores(n + 1, u + 1, blocks[GC * u:GC * u + GC])
                        if weights and not (isinstance(n, int) and n + 2 >= CHUNKS):
                            turn_onehot(n + 2, u + 2)
                        if u > 0:
                            sums(n - 1, i, u - 1)
                        elif not is_first(i):
                            sums(n - 1, i - 1, U - 1)

                turns(pe, BODIES, body)
                sums(CHUNKS - 1, BODIES - 1, U - 1)

            @block.vector
            def _(dve):
                regs = [dve.alloc_register(f"dve_block{q}_{table}") for q in range(GB)]
                steps = Tally(at["vec"])

                def step(ins):
                    ins.then_inc(m.vec_step, 1)
                    return steps.next()

                def number_nodes(n, i, u):
                    dve.wait_ge(m.slots_in[u % U], at["slots"] + 16 * (i + u // U + 1))
                    return step(dve.tensor_copy(node[:, u % R, :], slots[:, u % U, :, 1]))

                def build_onehot(n, u, numbered):
                    if not (isinstance(n, int) and n < R):
                        dve.wait_ge(m.summed, g0 + GC * (n - R + 1))
                    dve.wait_ge(m.vec_step, numbered)
                    if weights:
                        dve.tensor_scalar(pad[:, u % R, :], node[:, u % R, :], float(P), BIG if mode == "neg" else -BIG,
                                          ALU.is_ge, ALU.mult).then_inc(m.padded, 1)
                    dve.tensor_tensor(onehot[:, u % R, :, :], iota_b, wide(node[:, u % R, :].rearrange("p (c n) -> p c n", n=1), [P, C, P]),
                                      ALU.is_equal).then_inc(m.onehot_built, 1)

                def score_steps(n, i, u):
                    mine = ps_own[u % 2][:, 0:C * 8].rearrange("p (c h) -> p c h", h=8)
                    r, s = raw[:, u % 2, :, 0:heads], score[:, u % 2, :, 0:heads]
                    dve.wait_ge(m.own_scored, w0 + n + 1)
                    dve.wait_ge(m.gathered[u % R], at["gathered"] + 16 * C * (rounds(i, u) + 1))
                    if mode == "neg" and not (isinstance(n, int) and n < 2):
                        dve.wait_ge(m.weighted, w0 + n - 1)
                        if act_tiles:
                            dve.wait_ge(m.act_weighted, n - 1)
                    yield step(dve.tensor_tensor(r, mine[:, :, 0:heads], rows[:, u % R, :, feat:feat + heads], ALU.add))
                    yield step(dve.scalar_tensor_tensor(s, r, SLOPE, r, ALU.mult, ALU.max))
                    if mode == "shift":
                        yield step(dve.tensor_tensor(s, s, mine[:, :, heads:2 * heads], ALU.subtract))
                    dve.wait_ge(m.padded, w0 + n + 1)
                    last = dve.tensor_tensor(s, s, wide(pad[:, u % R, :].rearrange("p (c n) -> p c n", n=1), [P, C, heads]), ALU.add)
                    if mode == "gat":
                        yield step(last)
                        best = m.score_max[:].rearrange("p (c h) -> p c h", h=8)
                        last = dve.tensor_tensor(best, best, s, ALU.max)
                    last.then_inc(m.scored, 1)

                def weigh(u, j):
                    r = rows[:, u % R, j, 0:feat]
                    w = raw[:, u % 2, j, 0:heads] if mode == "neg" else rows[:, u % R, j, feat:feat + heads]
                    if heads == 1:
                        return dve.tensor_scalar(r, r, w, None, ALU.mult)
                    r = r.rearrange("p (h w) -> p h w", w=hw)
                    return dve.tensor_tensor(r, r, wide(w.rearrange("p (h w) -> p h w", w=1), [P, heads, hw]), ALU.mult)

                def add_sums(n, u, blocks):
                    for q in range(GC):
                        dve.wait_ge(m.summed, g0 + GC * n + q + 1)
                        wait(dve, m.added, g0 + GC * n + q)
                        place = acc[:, bass.ds(blocks[q], 1), :]
                        dve.tensor_tensor(place, place, ps_sum[GC * (u % 2) + q][:, 0:summed_cols].rearrange("p (b w) -> p b w", b=1),
                                          ALU.add).then_inc(m.added, 1)

                def load_blocks(start):
                    dve.reg_load(regs, m.group_block[way][0:1, bass.ds(start, GB)])
                    return [dve.snap(r, min_val=0, max_val=NB - 1) for r in regs]

                dve.wait_ge(m.vec_step, step(dve.memset(m.acc[:, 0:NN * summed_cols], 0.0)))
                for n in range(3):
                    build_onehot(n, n, number_nodes(n, 0, n))
                if weights:
                    for done in score_steps(0, 0, 0):
                        dve.wait_ge(m.vec_step, done)

                def body(i):
                    steps.turn(i)
                    blocks = load_blocks(GB * i)
                    for u in range(U):
                        n = U * i + u
                        last_one = isinstance(n, int) and n + 1 >= CHUNKS
                        last_three = isinstance(n, int) and n + 3 >= CHUNKS
                        if not last_three:
                            numbered = number_nodes(n + 3, i, u + 3)
                        if weights:
                            scores = iter(()) if last_one else score_steps(n + 1, i, u + 1)
                            done = next(scores, None)
                            dve.wait_ge(m.exped, w0 + n + 1)
                            for j in range(C - act_tiles):
                                last = weigh(u, j)
                                if j == C - act_tiles - 1:
                                    last.then_inc(m.weighted, 1)
                                if j == 0 and not last_three:
                                    build_onehot(n + 3, u + 3, numbered)
                                if done is not None:
                                    dve.wait_ge(m.vec_step, done)
                                    done = next(scores, None)
                            while done is not None:
                                dve.wait_ge(m.vec_step, done)
                                done = next(scores, None)
                        elif not last_three:
                            build_onehot(n + 3, u + 3, numbered)
                        if not (isinstance(n, int) and n < 2):
                            add_sums(n - 2, u, blocks[GC * u:GC * u + GC])

                turns(dve, BODIES, body)
                steps.settle()
                blocks = load_blocks(GROUPS)
                add_sums(CHUNKS - 2, 0, blocks[0:GC])
                add_sums(CHUNKS - 1, 1, blocks[GC:2 * GC])
                dve.wait_ge(m.added, g0 + GROUPS)
                m.at["vec"] = steps.value

    m.at["chunk"] += CHUNKS
    if weights:
        m.at["wchunk"] += CHUNKS
    m.at["gathered"] += 16 * C * 2 * BODIES
    m.at["slots"] += 16 * BODIES


def make_products(pe, m, st, p, tiles, w, cols):
    deep = 2 if cols <= 512 else 1

    def turned(kb):
        wait(pe, m.x_copied[st.s], p + kb - (kb > 0))
        for c, part in enumerate(tiles(kb)):
            last = pe.transpose(st.ps_x[:, kb % 2, c * P:(c + 1) * P], part, m.ident[:])
        last.then_inc(m.x_turned[st.s], 1)
        return c + 1

    n = turned(0)
    for kb in range(KB):
        if kb > 0:
            yield
        if kb + 1 < KB:
            turned(kb + 1)
        pe.wait_ge(m.x_copied[st.s], p + kb + 1)
        wait(pe, m.product_taken[st.s], p + max(kb - deep + 1, 0))
        for c in range(n):
            for a in range(0, cols, 512):
                b = min(a + 512, cols)
                last = pe.matmul(st.ps_y[:, kb % deep * 512 + a:kb % deep * 512 + b], st["xT"][:, kb % 2, c * P:(c + 1) * P], w[:, c, a:b],
                                 start=(c == 0), stop=(c == n - 1))
        last.then_inc(m.product[st.s], 1)


def copy_turned(act, m, st, p, n):
    def copy(kb):
        act.wait_ge(m.x_turned[st.s], p + kb + 1)
        wait(act, m.product[st.s], p + kb - (kb > 0))
        act.copy(st["xT"][:, kb % 2, 0:n * P], st.ps_x[:, kb % 2, 0:n * P]).then_inc(m.x_copied[st.s], 1)

    copy(0)
    for kb in range(1, KB):
        copy(kb)
        yield


def take_products(dve, m, st, p, take, deep=2):
    for kb in range(KB):
        yield
        dve.wait_ge(m.product[st.s], p + kb + 1)
        take(kb, st.ps_y[:, kb % deep * 512:]).then_inc(m.product_taken[st.s], 1)
    yield
    dve.wait_ge(m.product_taken[st.s], p + KB)


def normalize(dve, m, st, v, y, gain=None, shift=None, source=None):
    source = source or (lambda kb: y[:, kb, :])
    for kb in range(KB):
        last = dve.bn_stats(st["stats"][:, kb, :], source(kb))
    yield from v.step(last)
    t, s = st["stats"], st["small"]
    dve.tensor_tensor(s[:, :, 0], t[:, :, 1], t[:, :, 4], ALU.add)
    dve.tensor_tensor(s[:, :, 1], t[:, :, 1], t[:, :, 4], ALU.subtract)
    yield from v.step(dve.tensor_tensor(s[:, :, 2], t[:, :, 2], t[:, :, 5], ALU.add))
    dve.tensor_scalar(s[:, :, 3], s[:, :, 0], -0.5, None, ALU.mult)
    yield from v.step(dve.scalar_tensor_tensor(s[:, :, 4], s[:, :, 1], 0.25, s[:, :, 1], ALU.mult, ALU.mult))
    yield from v.step(dve.scalar_tensor_tensor(s[:, :, 5], s[:, :, 2], 1.0 / D, s[:, :, 4], ALU.mult, ALU.add))
    v.hand_over(dve.tensor_scalar(s[:, :, 6], s[:, :, 5], LN_EPS, None, ALU.add))
    yield from v.taken_over()
    yield from v.step(dve.reciprocal(s[:, :, 0], s[:, :, 7]))
    if gain is None:
        for kb in range(KB):
            last = dve.tensor_scalar(y[:, kb, :], y[:, kb, :], s[:, kb, 3:4], s[:, kb, 0:1], ALU.add, ALU.mult)
        yield from v.step(last)
        return
    for kb in range(KB):
        last = dve.scalar_tensor_tensor(y[:, kb, :], source(kb), s[:, kb, 3:4], gain, ALU.add, ALU.mult)
    yield from v.step(last)
    for kb in range(KB):
        last = dve.scalar_tensor_tensor(y[:, kb, :], y[:, kb, :], s[:, kb, 0:1], shift, ALU.mult, ALU.add)
    yield from v.step(last)


def root(act, st, a):
    a.take_over()
    a.hand_over(act.activation(st["small"][:, :, 7], st["small"][:, :, 6], ACT.Sqrt))


def elu_parts(act, a, z, e):
    a.take_over()
    act.activation(e, z, ACT.Exp).then_inc(a.own, 1)
    act.wait_ge(a.own, a.steps.next())
    a.hand_over(act.activation(z, z, ACT.Relu))


def rounds(n):
    for _ in range(n):
        yield


class Hand:

    def __init__(self, eng, own, out, into, at_own, at_out, at_in):
        self.eng, self.own, self.out, self.into = eng, own, out, into
        self.steps, self.outs, self.ins = Tally(at_own), Tally(at_out), Tally(at_in)

    def settled(self, ins):
        ins.then_inc(self.own, 1)
        self.eng.wait_ge(self.own, self.steps.next())

    def step(self, ins):
        ins.then_inc(self.own, 1)
        yield
        self.eng.wait_ge(self.own, self.steps.next())

    def hand_over(self, ins):
        ins.then_inc(self.out, 1)
        self.outs.next()

    def take_over(self):
        self.eng.wait_ge(self.into, self.ins.next())

    def taken_over(self):
        yield
        self.take_over()

    def turn(self, i, half=0):
        for t in (self.steps, self.outs, self.ins):
            t.turn(i, half)

    def settle(self):
        for t in (self.steps, self.outs, self.ins):
            t.settle()


def vector_side(dve, m):
    return Hand(dve, m.vec_step, m.for_act, m.for_vec, m.at["vec"], m.at["for_act"], m.at["for_vec"])


def scalar_side(act, m):
    return Hand(act, m.act_step, m.for_vec, m.for_act, m.at["act"], m.at["for_vec"], m.at["for_act"])


def rows_of(table, batch):
    return table.rearrange("(b p) w -> p b w", p=P)[:, bass.ds(batch * KB, KB), :]


def fold(pe, m, ps, rows, heads, n_rows, n_cols, count):
    for k in range(n_cols):
        for c in range(n_rows):
            last = pe.matmul(ps[:, k * 16:k * 16 + count], rows[:, c, k * P:(k + 1) * P], heads[:, c, 0:count],
                             start=(c == 0), stop=(c == n_rows - 1))
    return last


class Stream(dict):
    pass


class NodePhase:

    def __init__(self, nc, m, name, parts):
        self.nc, self.m, self.name = nc, m, name
        self.scope = ExitStack()
        self.spare_at = NN * (D + 9)
        self.streams = []
        for s in range(STREAMS):
            st = Stream()
            st.s = s
            self.streams.append(st)
            self.each(st, "mark", [1, 2])
            self.each(st, "stats", [P, KB, 6])
            self.each(st, "small", [P, KB, 8])
            self.each(st, "xT", [P, 2, parts * P])
            st.ps_x = self.scope.enter_context(nc.psum_tensor(f"ps_x{s}_{name}", [P, 2, 512], F32))
            st.ps_y = self.scope.enter_context(nc.psum_tensor(f"ps_y{s}_{name}", [P, 1024], F32))
        self.ps_f = self.streams[0].ps_y

    def sb(self, name, shape, dt=F32):
        return self.scope.enter_context(self.nc.sbuf_tensor(f"{name}_{self.name}", shape, dt))

    def each(self, st, name, shape):
        st[name] = self.sb(f"{name}{st.s}", shape)

    def buffers(self, **shapes):
        for st in self.streams:
            for name, shape in shapes.items():
                self.each(st, name, shape)

    def spare_buffers(self, **widths):
        for st in self.streams:
            for name, width in widths.items():
                n = KB * width
                st[name] = self.m.acc[:, self.spare_at:self.spare_at + n].rearrange("p (b w) -> p b w", w=width)
                self.spare_at += n
        assert self.spare_at <= SLOTTED_AT

    def traffic(self, sp, weights, loads, stores, skewed=True):
        m = self.m
        for tile, src in weights:
            sp.dma_start(tile, src).then_inc(m.weights_in, 16)

        def load(st, i):
            for name, table in loads:
                sp.dma_start(st[name][:], rows_of(table, STREAMS * i + st.s)).then_inc(m.rows_in[st.s], 16)

        for st in self.streams:
            load(st, 0)

        def load_next(st, i):
            if loads and not (isinstance(i, int) and i == TURNS - 1):
                sp.wait_ge(m.rows_used[st.s], m.at["rows_used"] + i + 1)
                load(st, i + 1)

        def store(st, i):
            sp.wait_ge(m.rows_made[st.s], m.at["rows_made"] + i + 1)
            for name, table in stores:
                sp.dma_start(rows_of(table, STREAMS * i + st.s), st[name][:]).then_inc(m.rows_out[st.s], 16)

        def body(i):
            if skewed:
                for st in self.streams:
                    load_next(st, i)
                    store(st, i)
            else:
                for st in self.streams:
                    load_next(st, i)
                for st in self.streams:
                    store(st, i)

        turns(sp, TURNS, body)
        for st in self.streams:
            sp.wait_ge(m.rows_out[st.s], m.at["rows_out"] + 16 * len(stores) * TURNS)

    def run(self, eng, first, second=None):
        a, b = self.streams

        def together(*steps):
            steps = list(steps)
            while steps:
                steps = [g for g in steps if next(g, DONE) is not DONE]

        def whole(i):
            together(first(i, a), first(i, b))

        def skewed(i):
            together(second(i, a), first(i, b))
            if isinstance(i, int) and i == TURNS - 1:
                together(second(i, b))
            else:
                together(first(i + 1, a), second(i, b))

        if second is None:
            turns(eng, TURNS, whole)
        else:
            together(first(0, a))
            turns(eng, TURNS, skewed)

    def used(self, dve, st):
        dve.memset(st["mark"][:, 1:2], 0.0).then_inc(self.m.rows_used[st.s], 1)

    def loaded(self, eng, st, loads, i):
        eng.wait_ge(self.m.rows_in[st.s], self.m.at["rows_in"] + 16 * len(loads) * (i + 1))

    def stored(self, eng, st, stores, i):
        if not is_first(i):
            eng.wait_ge(self.m.rows_out[st.s], self.m.at["rows_out"] + 16 * len(stores) * i)

    def vector_sides(self, dve):
        m = self.m
        for st in self.streams:
            st.v = Hand(dve, m.row_vec_step[st.s], m.rows_for_act[st.s], m.rows_for_vec[st.s],
                        m.at["row_vec"], m.at["rows_for_act"], m.at["rows_for_vec"])

    def scalar_sides(self, act):
        m = self.m
        for st in self.streams:
            st.a = Hand(act, m.row_act_step[st.s], m.rows_for_vec[st.s], m.rows_for_act[st.s],
                        m.at["row_act"], m.at["rows_for_vec"], m.at["rows_for_act"])

    def close(self, weights, loads, stores, products, for_pe):
        at = self.m.at
        at["weights_in"] += 16 * len(weights)
        at["rows_in"] += 16 * len(loads) * TURNS
        at["rows_out"] += 16 * len(stores) * TURNS
        at["rows_made"] += TURNS
        if loads:
            at["rows_used"] += TURNS
        at["product"] += products * KB * TURNS
        at["for_pe"] += for_pe * TURNS
        for st in self.streams:
            for t in (st.v, st.a):
                if t:
                    t.settle()
        st = self.streams[0]
        assert st.v.outs.value == (st.a.ins.value if st.a else st.v.outs.value)
        assert st.v.ins.value == (st.a.outs.value if st.a else st.v.ins.value)
        at["row_vec"], at["rows_for_act"], at["rows_for_vec"] = st.v.steps.value, st.v.outs.value, st.v.ins.value
        if st.a:
            at["row_act"] = st.a.steps.value
        self.scope.close()


def per_block(row, shape):
    return row.rearrange("p (b w) -> p b w", b=1).to_broadcast(shape)


def per_row(col, shape):
    return col.rearrange("p (b w) -> p b w", w=1).to_broadcast(shape)


def by_heads(row, heads):
    return row.rearrange("p (h w) -> p h w", h=heads)


def on_all(row):
    return row.rearrange("(a n) -> a n", a=1).to_broadcast([P, row.shape[0]])


def chunks_of(w):
    return w.rearrange("(c p) n -> p c n", p=P)


def nothing(i, st):
    yield from ()


def halves(rows):
    return lambda kb: [rows[:, kb, 0:P], rows[:, kb, P:D]]


def phase_0(nc, m, A, scatters):
    ph = NodePhase(nc, m, "n0", 2)
    ph.buffers(x=[P, KB, D], rows=[P, KB, D + 9])
    w = ph.sb("w", [P, 2, D + 16])
    wr = ph.sb("wr", [P, 2, D])
    heads = ph.sb("heads", [P, 2, 16])
    top = ph.sb("top", [P, 16])
    top_all = ph.sb("top_all", [P, 16])
    both = ph.sb("both", [P, 8])
    one = ph.sb("one", [P, 2])
    weights = [(w[:, :, 0:D], chunks_of(A["L0_WpT"])), (wr[:], chunks_of(A["L0_gnn_Wp"])), (heads[:], chunks_of(A["L0_heads"]))]
    loads, stores = [("x", A["x"])], [("rows", m.T[0])]
    at = dict(m.at)
    with nc.Block() as block:
        @block.sync
        def _(sp):
            ph.traffic(sp, weights, loads, stores, skewed=False)

        @block.tensor
        def _(pe):
            pe.wait_ge(m.weights_in, at["weights_in"] + 16 * len(weights))
            fold(pe, m, ph.ps_f, wr, heads, 2, 2, 16).then_inc(m.folded, 1)
            pe.wait_ge(m.fold_taken, at["fold"] + 1)

            def batch(i, st):
                ph.loaded(pe, st, loads, i)
                yield from make_products(pe, m, st, at["product"] + KB * i, halves(st["x"]), w, D + 16)

            ph.run(pe, batch)

        @block.scalar
        def _(act):
            ph.scalar_sides(act)
            ph.run(act, lambda i, st: copy_turned(act, m, st, at["product"] + KB * i, 2))

        @block.vector
        def _(dve):
            v = vector_side(dve, m)
            ph.vector_sides(dve)
            dve.wait_ge(m.folded, at["fold"] + 1)
            dve.wait_ge(m.weights_in, at["weights_in"] + 16 * len(weights))
            dve.tensor_copy(w[:, :, D:D + 16], ph.ps_f[:, 0:32].rearrange("p (c h) -> p c h", h=16)).then_inc(m.fold_taken, 1)
            for st in ph.streams:
                v.settled(dve.memset(st["rows"][:, :, D + 8:D + 9], 1.0))

            def batch(i, st):
                ph.stored(dve, st, stores, i)

                def take(kb, y):
                    dve.tensor_copy(m.sall[:, bass.ds((STREAMS * i + st.s) * KB + kb, 1), :], y[:, D:D + 16].rearrange("p (b h) -> p b h", b=1))
                    return dve.tensor_copy(st["rows"][:, kb, 0:D + 8], y[:, 0:D + 8])

                yield from take_products(dve, m, st, at["product"] + KB * i, take)
                ph.used(dve, st)
                dve.memset(st["mark"][:, 0:1], 0.0).then_inc(m.rows_made[st.s], 1)

            ph.run(dve, batch)
            dve.tensor_reduce(top[:], m.sall[:].rearrange("p b h -> p h b"), AX_X, ALU.max).then_inc(m.for_pool, 1)
            dve.wait_ge(m.from_pool, at["pool"] + 1)
            v.settled(dve.tensor_tensor(both[:], top_all[:, 0:8], top_all[:, 8:16], ALU.add))
            v.settled(dve.tensor_reduce(one[:, 0:1], both[:], AX_X, ALU.max))
            v.settled(dve.scalar_tensor_tensor(one[:, 1:2], one[:, 0:1], SLOPE, one[:, 0:1], ALU.mult, ALU.max))
            v.settled(dve.tensor_scalar(m.neg_bound[:], one[:, 1:2], -1.0, None, ALU.mult))
            v.settle()
            m.at["vec"] = v.steps.value

        @block.gpsimd
        def _(pool):
            scatters(pool)
            pool.wait_ge(m.for_pool, at["pool"] + 1)
            pool.partition_all_reduce(top_all[:], top[:], P, RMAX).then_inc(m.from_pool, 1)

    m.at["pool"] += 1
    m.at["fold"] += 1
    ph.close(weights, loads, stores, 1, 0)


def phase_1(nc, m, A, scatters):
    ph = NodePhase(nc, m, "n1", 2)
    ph.buffers(x=[P, KB, D], z=[P, KB, D], e=[P, KB, D], den=[P, KB, 8])
    w = ph.sb("w", [P, 2, D])
    bias = ph.sb("bias", [P, D])
    top = ph.sb("top", [P, 1])
    top_all = ph.sb("top_all", [P, 1])
    weights = [(w[:], chunks_of(A["L0_WskipT"])), (bias[:], on_all(A["L0_gnn_bias"]))]
    loads, stores = [("x", A["x"])], [("e", m.T[1])]
    at = dict(m.at)
    acc = m.acc_view
    with nc.Block() as block:
        @block.sync
        def _(sp):
            ph.traffic(sp, weights, loads, stores)

        @block.tensor
        def _(pe):
            pe.wait_ge(m.weights_in, at["weights_in"] + 16 * len(weights))

            def batch(i, st):
                ph.loaded(pe, st, loads, i)
                yield from rounds(2)
                yield from make_products(pe, m, st, at["product"] + KB * i, halves(st["x"]), w, D)

            ph.run(pe, batch, nothing)

        @block.scalar
        def _(act):
            a = scalar_side(act, m)
            ph.scalar_sides(act)
            a.take_over()
            a.hand_over(act.activation(m.eps_col[:], top_all[:], ACT.Exp, bias=m.neg_bound[:, 0:1]))
            a.settle()

            def first(i, st):
                st.a.turn(i)
                yield from rounds(2)
                yield from copy_turned(act, m, st, at["product"] + KB * i, 2)

            def second(i, st):
                st.a.turn(i, 1)
                elu_parts(act, st.a, st["z"][:], st["e"][:])
                yield from rounds(7)
                root(act, st, st.a)

            ph.run(act, first, second)

        @block.gpsimd
        def _(pool):
            pool.wait_ge(m.for_pool, at["pool"] + 1)
            pool.partition_all_reduce(top_all[:], top[:], P, RMAX).then_inc(m.from_pool, 1)
            scatters(pool)

        @block.vector
        def _(dve):
            v = vector_side(dve, m)
            ph.vector_sides(dve)
            dve.tensor_reduce(top[:], m.score_max[:], AX_X, ALU.max).then_inc(m.for_pool, 1)
            dve.wait_ge(m.from_pool, at["pool"] + 1)
            v.hand_over(dve.memset(m.mark[:], 0.0))
            v.take_over()
            v.settled(dve.tensor_scalar(m.eps_col[:], m.eps_col[:], 1e-16, 1e-37, ALU.mult, ALU.max))
            v.settled(dve.tensor_scalar(m.rcnt[:], acc[:, :, D + 8], 1.0, None, ALU.max))
            v.settled(dve.reciprocal(m.rcnt[:], m.rcnt[:]))
            dve.wait_ge(m.weights_in, at["weights_in"] + 16 * len(weights))
            v.settle()
            m.at["vec"], m.at["for_act"], m.at["for_vec"] = v.steps.value, v.outs.value, v.ins.value

            def first(i, st):
                v, z, den = st.v, st["z"], st["den"]
                v.turn(i)
                b0 = (STREAMS * i + st.s) * KB
                yield from v.step(dve.tensor_scalar(den[:], acc[:, bass.ds(b0, KB), D:D + 8], m.eps_col[:, 0:1], None, ALU.add))
                yield from v.step(dve.reciprocal(den[:], den[:]))
                for kb in range(KB):
                    last = dve.tensor_tensor(by_heads(z[:, kb, :], 8), acc[:, bass.ds(b0 + kb, 1), 0:D].rearrange("p b (h w) -> p (b h) w", h=8),
                                             den[:, kb, :].rearrange("p (h w) -> p h w", w=1).to_broadcast([P, 8, D // 8]), ALU.mult)
                yield from v.step(last)
                yield from take_products(dve, m, st, at["product"] + KB * i,
                                         lambda kb, y: dve.tensor_tensor(z[:, kb, :], z[:, kb, :], y[:, 0:D], ALU.add))

            def second(i, st):
                v, x, z, e = st.v, st["x"], st["z"], st["e"]
                v.turn(i, 1)
                ph.stored(dve, st, stores, i)
                v.hand_over(dve.tensor_tensor(z[:], z[:], per_block(bias[:], [P, KB, D]), ALU.add))
                yield from v.taken_over()
                yield from v.step(dve.scalar_tensor_tensor(e[:], e[:], 1.0, z[:], ALU.min, ALU.add))
                ph.loaded(dve, st, loads, i)
                yield from v.step(dve.scalar_tensor_tensor(e[:], e[:], -1.0, x[:], ALU.add, ALU.add))
                ph.used(dve, st)
                yield from normalize(dve, m, st, v, e)
                dve.memset(st["mark"][:, 0:1], 0.0).then_inc(m.rows_made[st.s], 1)

            ph.run(dve, first, second)

    m.at["pool"] += 1
    ph.close(weights, loads, stores, 1, 0)


def phase_sage(nc, m, A, layer, scatters):
    last_one = layer == 2
    ph = NodePhase(nc, m, f"n{layer + 1}", 4)
    ph.buffers(h=[P, KB, D], mean=[P, KB, D], z=[P, KB, D])
    w = ph.sb("w", [P, 4, D])
    bias = ph.sb("bias", [P, 3, D])
    name = "L1_gnn_"
    weights = [(w[:, 0:2, :], chunks_of(A[f"{name}W_l{layer}"])), (w[:, 2:4, :], chunks_of(A[f"{name}W_r{layer}"])),
               (bias[:, 0, :], on_all(A[f"{name}b_l{layer}"])), (bias[:, 1, :], on_all(A[f"{name}ln{layer}_g"])),
               (bias[:, 2, :], on_all(A[f"{name}ln{layer}_b"]))]
    loads, stores = [("h", m.T[layer])], [("z", m.T[2])]
    if last_one:
        F = 2 * D
        ph.buffers(x1=[P, KB, D])
        ph.spare_buffers(rows=F + 8)
        w2 = ph.sb("w2", [P, 2, F + 16])
        wr2 = ph.sb("wr2", [P, 4, D])
        heads = ph.sb("heads", [P, 4, 16])
        bias2 = ph.sb("bias2", [P, F + 16])
        bcol = ph.sb("bcol", [P, 4])
        brep = ph.sb("brep", [P, 4, P])
        weights += [(w2[:, :, 0:F], chunks_of(A["L2_WT"])), (wr2[:], chunks_of(A["L2_W"])), (heads[:], chunks_of(A["L2_heads"])),
                    (bias2[:, 0:F], on_all(A["L2_b"])), (bcol[:], A["L2_b"].rearrange("(c p) -> p c", p=P))]
        loads.append(("x1", m.T[1]))
        stores = [("z", m.x2), ("rows", m.T[3])]
    products = 2 if last_one else 1
    at = dict(m.at)
    acc = m.acc_view
    with nc.Block() as block:
        @block.sync
        def _(sp):
            with nc.allow_non_contiguous_dma(reason="a small vector as columns"):
                ph.traffic(sp, weights, loads, stores)

        @block.gpsimd
        def _(pool):
            scatters(pool)

        @block.tensor
        def _(pe):
            pe.wait_ge(m.weights_in, at["weights_in"] + 16 * len(weights))
            if last_one:
                fold(pe, m, ph.ps_f, wr2, heads, 4, 2, 16).then_inc(m.folded, 1)
                pe.wait_ge(m.fold_taken, at["fold"] + 1)
                for c in range(4):
                    last = pe.matmul(ph.ps_f[:, 64:80], brep[:, c, :], heads[:, c, :], start=(c == 0), stop=(c == 3))
                last.then_inc(m.folded, 1)
                pe.wait_ge(m.fold_taken, at["fold"] + 2)

            def first(i, st):
                ph.loaded(pe, st, loads, i)
                pe.wait_ge(m.for_pe[st.s], at["for_pe"] + products * i + 1)
                yield from make_products(pe, m, st, at["product"] + products * KB * i,
                                         lambda kb: halves(st["mean"])(kb) + halves(st["h"])(kb), w, D)

            def second(i, st):
                yield from rounds(8)
                pe.wait_ge(m.for_pe[st.s], at["for_pe"] + products * i + 2)
                yield from make_products(pe, m, st, at["product"] + products * KB * i + KB, halves(st["z"]), w2, F + 16)

            ph.run(pe, first, second if last_one else nothing)

        @block.scalar
        def _(act):
            ph.scalar_sides(act)

            def root_and_relu(st):
                yield from rounds(4)
                root(act, st, st.a)
                yield from rounds(4)
                st.a.take_over()
                st.a.hand_over(act.activation(st["z"][:], st["z"][:], ACT.Relu))

            def first(i, st):
                st.a.turn(i)
                yield from copy_turned(act, m, st, at["product"] + products * KB * i, 4)
                if last_one:
                    yield from rounds(2)
                    yield from root_and_relu(st)

            def second(i, st):
                st.a.turn(i, 1)
                if not last_one:
                    yield from root_and_relu(st)
                    return
                yield from rounds(5)
                root(act, st, st.a)
                yield from rounds(3)
                yield from copy_turned(act, m, st, at["product"] + products * KB * i + KB, 2)

            ph.run(act, first, second)

        @block.vector
        def _(dve):
            ph.vector_sides(dve)
            dve.wait_ge(m.weights_in, at["weights_in"] + 16 * len(weights))
            if last_one:
                v = vector_side(dve, m)
                dve.wait_ge(m.folded, at["fold"] + 1)
                dve.tensor_copy(w2[:, :, F:F + 16], ph.ps_f[:, 0:32].rearrange("p (c h) -> p c h", h=16))
                dve.tensor_copy(brep[:], bcol[:].rearrange("p (c n) -> p c n", n=1).to_broadcast([P, 4, P])).then_inc(m.fold_taken, 1)
                dve.wait_ge(m.folded, at["fold"] + 2)
                v.settled(dve.tensor_copy(bias2[:, F:F + 16], ph.ps_f[:, 64:80]))
                dve.memset(m.mark[:], 0.0).then_inc(m.fold_taken, 1)
                v.settle()
                m.at["vec"] = v.steps.value

            def norm_and_hand(st):
                yield from normalize(dve, m, st, st.v, st["z"], bias[:, 1, :], bias[:, 2, :])
                st.v.hand_over(dve.memset(st["mark"][:, 0:1], 0.0))

            def first(i, st):
                mean, z = st["mean"], st["z"]
                st.v.turn(i)
                b0 = (STREAMS * i + st.s) * KB
                dve.tensor_tensor(mean[:], acc[:, bass.ds(b0, KB), :],
                                  m.rcnt[:, bass.ds(b0, KB)].rearrange("p (b w) -> p b w", w=1).to_broadcast([P, KB, D]),
                                  ALU.mult).then_inc(m.for_pe[st.s], 1)
                ph.stored(dve, st, stores, i)
                yield from take_products(dve, m, st, at["product"] + products * KB * i,
                                         lambda kb, y: dve.tensor_tensor(z[:, kb, :], y[:, 0:D], bias[:, 0, :], ALU.add))
                if last_one:
                    yield from norm_and_hand(st)
                else:
                    ph.used(dve, st)

            def second(i, st):
                v, z = st.v, st["z"]
                v.turn(i, 1)
                if not last_one:
                    yield from norm_and_hand(st)
                    yield from v.taken_over()
                    dve.memset(st["mark"][:, 0:1], 0.0).then_inc(m.rows_made[st.s], 1)
                    return
                v.take_over()
                ph.loaded(dve, st, loads, i)
                yield from v.step(dve.tensor_tensor(z[:], z[:], st["x1"][:], ALU.add))
                ph.used(dve, st)
                yield from normalize(dve, m, st, v, z)
                dve.memset(st["mark"][:, 0:1], 0.0).then_inc(m.for_pe[st.s], 1)
                b0 = (STREAMS * i + st.s) * KB

                def take(kb, y):
                    dve.tensor_tensor(m.sall[:, bass.ds(b0 + kb, 1), 8:16], y[:, F + 8:F + 16].rearrange("p (b h) -> p b h", b=1),
                                      bias2[:, F + 8:F + 16].rearrange("p (b h) -> p b h", b=1), ALU.add)
                    return dve.tensor_tensor(st["rows"][:, kb, :], y[:, 0:F + 8], bias2[:, 0:F + 8], ALU.add)

                yield from take_products(dve, m, st, at["product"] + products * KB * i + KB, take, 1)
                dve.memset(st["mark"][:, 0:1], 0.0).then_inc(m.rows_made[st.s], 1)

            ph.run(dve, first, second)

    if last_one:
        m.at["fold"] += 2
    ph.close(weights, loads, stores, products, products)


def phase_4(nc, m, A):
    ph = NodePhase(nc, m, "n4", 4)
    F, H = 2 * D, 8
    HW = F // H
    ph.buffers(z=[P, KB, F], e=[P, KB, F], rows=[P, KB, D + 1], mu=[P, KB * H], var=[P, KB * H])
    w = ph.sb("w", [P, 4, D + 2])
    heads = ph.sb("heads", [P, 2, 16])
    gain = ph.sb("gain", [P, 2, F])
    bias = ph.sb("bias", [P, D + 2])
    bcol = ph.sb("bcol", [P, 2])
    wr = ph.streams[0]["z"][:, 0:2, :]
    brep = ph.streams[0]["z"][:, 2, 0:2 * P].rearrange("p (c n) -> p c n", n=P)
    weights = [(w[:, :, 0:D], chunks_of(A["L2_WoutT"])), (wr, chunks_of(A["L2_gnn_W_out"])), (heads[:, :, 0:2], chunks_of(A["L2_out_heads"])),
               (gain[:, 0, :], on_all(A["L2_g"])), (gain[:, 1, :], on_all(A["L2_beta"])),
               (bias[:, 0:D], on_all(A["L2_gnn_b_out"])), (bcol[:], A["L2_gnn_b_out"].rearrange("(c p) -> p c", p=P))]
    loads, stores = [], [("rows", m.T[4])]
    at = dict(m.at)
    acc = m.acc_view
    with nc.Block() as block:
        @block.sync
        def _(sp):
            with nc.allow_non_contiguous_dma(reason="a small vector as columns"):
                ph.traffic(sp, weights, loads, stores)

        @block.tensor
        def _(pe):
            pe.wait_ge(m.weights_in, at["weights_in"] + 16 * len(weights))
            fold(pe, m, ph.ps_f, wr, heads, 2, 4, 2).then_inc(m.folded, 1)
            pe.wait_ge(m.fold_taken, at["fold"] + 1)
            for c in range(2):
                last = pe.matmul(ph.ps_f[:, 80:82], brep[:, c, :], heads[:, c, 0:2], start=(c == 0), stop=(c == 1))
            last.then_inc(m.folded, 1)
            pe.wait_ge(m.fold_taken, at["fold"] + 2)

            def second(i, st):
                yield from rounds(1)
                pe.wait_ge(m.for_pe[st.s], at["for_pe"] + i + 1)
                yield from make_products(pe, m, st, at["product"] + KB * i, lambda kb: [st["e"][:, kb, c * P:(c + 1) * P] for c in range(4)], w, D + 2)

            ph.run(pe, nothing, second)

        @block.scalar
        def _(act):
            ph.scalar_sides(act)

            def first(i, st):
                a = st.a
                a.turn(i)
                yield from rounds(2)
                a.take_over()
                a.hand_over(act.activation(st["e"][:], st["z"][:], ACT.Square))
                yield from rounds(2)
                a.take_over()
                a.hand_over(act.activation(st["var"][:], st["var"][:], ACT.Sqrt))
                yield from rounds(4)
                a.take_over()
                a.hand_over(act.activation(st["e"][:], st["z"][:], ACT.Exp))

            def second(i, st):
                st.a.turn(i, 1)
                yield from rounds(1)
                yield from copy_turned(act, m, st, at["product"] + KB * i, 4)

            ph.run(act, first, second)

        @block.vector
        def _(dve):
            v = vector_side(dve, m)
            ph.vector_sides(dve)
            dve.wait_ge(m.weights_in, at["weights_in"] + 16 * len(weights))
            dve.wait_ge(m.folded, at["fold"] + 1)
            dve.tensor_copy(w[:, :, D:D + 2], ph.ps_f[:, 0:64].rearrange("p (c h) -> p c h", h=16)[:, :, 0:2])
            dve.tensor_copy(brep, bcol[:].rearrange("p (c n) -> p c n", n=1).to_broadcast([P, 2, P])).then_inc(m.fold_taken, 1)
            dve.wait_ge(m.folded, at["fold"] + 2)
            v.settled(dve.tensor_copy(bias[:, D:D + 2], ph.ps_f[:, 80:82]))
            dve.memset(m.mark[:], 0.0).then_inc(m.fold_taken, 1)
            v.settle()
            m.at["vec"] = v.steps.value

            def first(i, st):
                v, z, e, mu, var = st.v, st["z"], st["e"], st["mu"], st["var"]
                v.turn(i)
                zh, eh = (t[:].rearrange("p b (h w) -> p (b h) w", h=H) for t in (z, e))
                b0 = (STREAMS * i + st.s) * KB
                sums = acc[:, bass.ds(b0, KB), :].rearrange("p b (h w) -> p (b h) w", h=H)
                yield from v.step(dve.tensor_reduce(mu[:], sums, AX_X, ALU.add))
                yield from v.step(dve.tensor_scalar(mu[:], mu[:], 1.0 / HW, None, ALU.mult))
                v.hand_over(dve.tensor_tensor(zh, sums, per_row(mu[:], [P, KB * H, HW]), ALU.subtract))
                yield from v.taken_over()
                yield from v.step(dve.tensor_reduce(var[:], eh, AX_X, ALU.add))
                v.hand_over(dve.tensor_scalar(var[:], var[:], 1.0 / HW, LN_EPS, ALU.mult, ALU.add))
                yield from v.taken_over()
                yield from v.step(dve.reciprocal(var[:], var[:]))
                yield from v.step(dve.tensor_tensor(zh, zh, per_row(var[:], [P, KB * H, HW]), ALU.mult))
                yield from v.step(dve.tensor_tensor(z[:], z[:], per_block(gain[:, 0, :], [P, KB, F]), ALU.mult))
                v.hand_over(dve.tensor_tensor(z[:], z[:], per_block(gain[:, 1, :], [P, KB, F]), ALU.add))

            def second(i, st):
                z, e = st["z"], st["e"]
                b0 = (STREAMS * i + st.s) * KB
                st.v.turn(i, 1)
                st.v.take_over()
                yield from st.v.step(dve.tensor_scalar(e[:], e[:], 1.0, -1.0, ALU.min, ALU.add))
                dve.tensor_tensor(e[:], e[:], z[:], ALU.max).then_inc(m.for_pe[st.s], 1)
                ph.stored(dve, st, stores, i)

                def take(kb, y):
                    dve.tensor_tensor(m.sall[:, bass.ds(b0 + kb, 1), 8:9], y[:, D + 1:D + 2].rearrange("p (b h) -> p b h", b=1),
                                      bias[:, D + 1:D + 2].rearrange("p (b h) -> p b h", b=1), ALU.add)
                    return dve.tensor_tensor(st["rows"][:, kb, :], y[:, 0:D + 1], bias[:, 0:D + 1], ALU.add)

                yield from take_products(dve, m, st, at["product"] + KB * i, take)
                dve.memset(st["mark"][:, 0:1], 0.0).then_inc(m.rows_made[st.s], 1)

            ph.run(dve, first, second)

    m.at["fold"] += 2
    ph.close(weights, loads, stores, 1, 1)


def phase_5(nc, m, A):
    ph = NodePhase(nc, m, "n5", 2)
    ph.buffers(x=[P, KB, D], z=[P, KB, D], e=[P, KB, D], rows=[P, KB, D + 4])
    w = ph.sb("w", [P, 2, D + 8])
    wr = ph.sb("wr", [P, 2, D])
    heads = ph.sb("heads", [P, 2, 16])
    gain = ph.sb("gain", [P, 2, D])
    top = ph.sb("top", [P, 4])
    top_all = ph.sb("top_all", [P, 4])
    weights = [(w[:, :, 0:D], chunks_of(A["L3_gnn_W"])), (wr[:], chunks_of(A["L3_WT"])), (heads[:, :, 0:8], chunks_of(A["L3_heads"])),
               (gain[:, 0, :], on_all(A["L2_gnn_g_out"])), (gain[:, 1, :], on_all(A["L2_gnn_beta_out"]))]
    loads, stores = [("x", m.x2)], [("e", m.x3), ("rows", m.T[5])]
    at = dict(m.at)
    acc = m.acc_view
    with nc.Block() as block:
        @block.sync
        def _(sp):
            ph.traffic(sp, weights, loads, stores)

        @block.tensor
        def _(pe):
            pe.wait_ge(m.weights_in, at["weights_in"] + 16 * len(weights))
            fold(pe, m, ph.ps_f, wr, heads, 2, 2, 8).then_inc(m.folded, 1)
            pe.wait_ge(m.fold_taken, at["fold"] + 1)

            def second(i, st):
                yield from rounds(9)
                pe.wait_ge(m.for_pe[st.s], at["for_pe"] + i + 1)
                yield from make_products(pe, m, st, at["product"] + KB * i, halves(st["e"]), w, D + 8)

            ph.run(pe, nothing, second)

        @block.scalar
        def _(act):
            ph.scalar_sides(act)

            def first(i, st):
                st.a.turn(i)
                yield from rounds(4)
                root(act, st, st.a)
                yield from rounds(4)
                elu_parts(act, st.a, st["z"][:], st["e"][:])

            def second(i, st):
                st.a.turn(i, 1)
                yield from rounds(6)
                root(act, st, st.a)
                yield from rounds(3)
                yield from copy_turned(act, m, st, at["product"] + KB * i, 2)

            ph.run(act, first, second)

        @block.gpsimd
        def _(pool):
            pool.wait_ge(m.for_pool, at["pool"] + 1)
            pool.partition_all_reduce(top_all[:], top[:], P, RMAX).then_inc(m.from_pool, 1)

        @block.vector
        def _(dve):
            v = vector_side(dve, m)
            ph.vector_sides(dve)
            dve.wait_ge(m.weights_in, at["weights_in"] + 16 * len(weights))
            dve.wait_ge(m.folded, at["fold"] + 1)
            dve.tensor_copy(w[:, :, D:D + 8], ph.ps_f[:, 0:32].rearrange("p (c h) -> p c h", h=16)[:, :, 0:8]).then_inc(m.fold_taken, 1)

            def first(i, st):
                v, z = st.v, st["z"]
                v.turn(i)
                b0 = (STREAMS * i + st.s) * KB
                yield from normalize(dve, m, st, v, z, gain[:, 0, :], gain[:, 1, :],
                                     lambda kb: acc[:, bass.ds(b0 + kb, 1), :].rearrange("p b w -> p (b w)"))
                ph.stored(dve, st, stores, i)
                v.hand_over(dve.memset(st["mark"][:, 0:1], 0.0))

            def second(i, st):
                v, x, z, e = st.v, st["x"], st["z"], st["e"]
                v.turn(i, 1)
                b0 = (STREAMS * i + st.s) * KB
                v.take_over()
                yield from v.step(dve.scalar_tensor_tensor(e[:], e[:], 1.0, z[:], ALU.min, ALU.add))
                ph.loaded(dve, st, loads, i)
                yield from v.step(dve.scalar_tensor_tensor(e[:], e[:], -1.0, x[:], ALU.add, ALU.add))
                ph.used(dve, st)
                yield from normalize(dve, m, st, v, e)
                dve.memset(st["mark"][:, 0:1], 0.0).then_inc(m.for_pe[st.s], 1)

                def take(kb, y):
                    s = m.sall[:, bass.ds(b0 + kb, 1), :]
                    dve.tensor_copy(s[:, :, 8:12], y[:, D + 4:D + 8].rearrange("p (b h) -> p b h", b=1))
                    dve.tensor_copy(s[:, :, 0:4], y[:, D:D + 4].rearrange("p (b h) -> p b h", b=1))
                    return dve.tensor_copy(st["rows"][:, kb, :], y[:, 0:D + 4])

                yield from take_products(dve, m, st, at["product"] + KB * i, take)
                dve.memset(st["mark"][:, 0:1], 0.0).then_inc(m.rows_made[st.s], 1)

            ph.run(dve, first, second)
            dve.tensor_reduce(top[:], m.sall[:, :, 0:4].rearrange("p b h -> p h b"), AX_X, ALU.max).then_inc(m.for_pool, 1)
            dve.wait_ge(m.from_pool, at["pool"] + 1)
            v.settled(dve.tensor_tensor(m.sall[:, :, 4:8], m.sall[:, :, 8:12], per_block(top_all[:], [P, NN, 4]), ALU.add))
            v.settled(dve.scalar_tensor_tensor(m.sall[:, :, 12:16], m.sall[:, :, 4:8], SLOPE, m.sall[:, :, 4:8], ALU.mult, ALU.max))
            v.settle()
            m.at["vec"] = v.steps.value

    m.at["pool"] += 1
    m.at["fold"] += 1
    ph.close(weights, loads, stores, 1, 1)


def phase_6(nc, m, A, out):
    ph = NodePhase(nc, m, "n6", 1)
    ph.buffers(x=[P, KB, D], z=[P, KB, D], rows=[P, KB, D + 4], score=[P, KB, 4], own=[P, KB, 4], den=[P, KB, 4])
    bias = ph.sb("bias", [P, 3, D])
    weights = [(bias[:, 0, :], on_all(A["L3_gnn_bias"])), (bias[:, 1, :], on_all(A["L3_gnn_gamma"])), (bias[:, 2, :], on_all(A["L3_gnn_beta"]))]
    loads, stores = [("x", m.x3), ("rows", m.T[5])], [("z", out)]
    at = dict(m.at)
    acc = m.acc_view
    with nc.Block() as block:
        @block.sync
        def _(sp):
            ph.traffic(sp, weights, loads, stores, skewed=False)

        @block.scalar
        def _(act):
            ph.scalar_sides(act)

            def batch(i, st):
                a = st.a
                a.turn(i)
                yield from rounds(2)
                a.take_over()
                a.hand_over(act.activation(st["own"][:], st["score"][:], ACT.Exp))
                yield from rounds(6)
                a.take_over()
                a.hand_over(act.activation(st["z"][:], st["z"][:], ACT.Relu))
                yield from rounds(6)
                root(act, st, a)
                yield from rounds(9)
                root(act, st, a)

            ph.run(act, batch)

        @block.vector
        def _(dve):
            ph.vector_sides(dve)
            dve.wait_ge(m.weights_in, at["weights_in"] + 16 * len(weights))

            def batch(i, st):
                v, x, z, rows, score, own, den = st.v, st["x"], st["z"], st["rows"], st["score"], st["own"], st["den"]
                v.turn(i)
                ph.loaded(dve, st, loads, i)
                b0 = (STREAMS * i + st.s) * KB
                mine = m.sall[:, bass.ds(b0, KB), :]
                yield from v.step(dve.tensor_tensor(score[:], rows[:, :, D:D + 4], mine[:, :, 8:12], ALU.add))
                yield from v.step(dve.scalar_tensor_tensor(score[:], score[:], SLOPE, score[:], ALU.mult, ALU.max))
                v.hand_over(dve.tensor_tensor(score[:], score[:], mine[:, :, 12:16], ALU.subtract))
                yield from v.taken_over()
                yield from v.step(dve.tensor_tensor(den[:], own[:], acc[:, bass.ds(b0, KB), D:D + 4], ALU.add))
                yield from v.step(dve.reciprocal(den[:], den[:]))
                ph.stored(dve, st, stores, i)
                for kb in range(KB):
                    last = dve.tensor_tensor(by_heads(z[:, kb, :], 4), by_heads(rows[:, kb, 0:D], 4),
                                             own[:, kb, :].rearrange("p (h w) -> p h w", w=1).to_broadcast([P, 4, D // 4]), ALU.mult)
                yield from v.step(last)
                yield from v.step(dve.tensor_tensor(z[:], z[:], acc[:, bass.ds(b0, KB), 0:D], ALU.add))
                for kb in range(KB):
                    zk = by_heads(z[:, kb, :], 4)
                    last = dve.tensor_tensor(zk, zk, den[:, kb, :].rearrange("p (h w) -> p h w", w=1).to_broadcast([P, 4, D // 4]), ALU.mult)
                yield from v.step(last)
                v.hand_over(dve.tensor_tensor(z[:], z[:], per_block(bias[:, 0, :], [P, KB, D]), ALU.add))
                yield from v.taken_over()
                yield from v.step(dve.tensor_tensor(z[:], z[:], x[:], ALU.add))
                yield from normalize(dve, m, st, v, z, bias[:, 1, :], bias[:, 2, :])
                yield from v.step(dve.tensor_tensor(z[:], z[:], x[:], ALU.add))
                ph.used(dve, st)
                yield from normalize(dve, m, st, v, z)
                dve.memset(st["mark"][:, 0:1], 0.0).then_inc(m.rows_made[st.s], 1)

            ph.run(dve, batch)

    ph.close(weights, loads, stores, 0, 0)


def build(nc, A, out):
    ctx = ExitStack()
    with ctx:
        def sb(name, shape, dt=F32):
            return ctx.enter_context(nc.sbuf_tensor(name, shape, dt))

        def sem(name):
            return ctx.enter_context(nc.semaphore(name))

        def dram(name, shape, dt=F32):
            return nc.dram_tensor(name, shape, dt, kind="Internal").ap()

        m = Shared()
        m.meta = [dram(f"slots_by_{k}", (P * TILES, 2), I32) for k in ("dst", "src")]
        m.T = [dram(f"table{k}", (NP, w)) for k, w in enumerate((D + 9, D, D, 2 * D + 8, D + 1, D + 4))]
        m.x2, m.x3 = dram("x2", (NP, D)), dram("x3", (NP, D))
        m.acc = sb("acc", [P, NN * 2 * D])
        m.sall = sb("sall", [P, NN, 16])
        m.rcnt = sb("rcnt", [P, NN])
        m.group_block = [sb(f"group_block{k}", [1, TG], I32) for k in range(2)]
        m.slotted_edges = [m.acc[0:EP, SLOTTED_AT + w * 3 * EC:SLOTTED_AT + (w + 1) * 3 * EC].bitcast(I32).rearrange("p (e k) -> p e k", k=3)
                           for w in range(2)]
        m.stage = sb("stage", [EP, 2, SC, 3], I32)
        m.iota_row = sb("iota_row", [P, P])
        m.part_col = sb("part_col", [P, 1])
        m.ident = sb("ident", [P, P])
        m.ones = sb("ones", [P, P])
        m.neg_bound = sb("neg_bound", [P, 1])
        m.score_max = sb("score_max", [P, C * 8])
        m.eps_col = sb("eps_col", [P, 1])
        m.mark = sb("mark", [1, 1])

        m.consts_ready = sem("consts_ready")
        m.numbered = sem("numbered")
        m.loaded = sem("loaded")
        m.fill_made = sem("fill_made")
        m.prefilled = sem("prefilled")
        m.counted = sem("counted")
        m.summed_up = sem("summed_up")
        m.ended = sem("ended")
        m.slotted = sem("slotted")
        m.staged = sem("staged")
        m.scattered = [sem(f"scattered{h}") for h in range(2)]
        m.pool_passed = sem("pool_passed")
        m.sync_passed = sem("sync_passed")
        m.vec_step = sem("vec_step")
        m.act_step = sem("act_step")
        m.for_act = sem("for_act")
        m.for_vec = sem("for_vec")
        m.for_pe = [sem(f"for_pe{s}") for s in range(STREAMS)]
        m.row_vec_step = [sem(f"row_vec_step{s}") for s in range(STREAMS)]
        m.row_act_step = [sem(f"row_act_step{s}") for s in range(STREAMS)]
        m.rows_for_act = [sem(f"rows_for_act{s}") for s in range(STREAMS)]
        m.rows_for_vec = [sem(f"rows_for_vec{s}") for s in range(STREAMS)]
        m.for_pool = sem("for_pool")
        m.from_pool = sem("from_pool")
        m.weights_in = sem("weights_in")
        m.rows_in = [sem(f"rows_in{s}") for s in range(STREAMS)]
        m.rows_used = [sem(f"rows_used{s}") for s in range(STREAMS)]
        m.rows_made = [sem(f"rows_made{s}") for s in range(STREAMS)]
        m.rows_out = [sem(f"rows_out{s}") for s in range(STREAMS)]
        m.folded = sem("folded")
        m.fold_taken = sem("fold_taken")
        m.x_turned = [sem(f"x_turned{s}") for s in range(STREAMS)]
        m.x_copied = [sem(f"x_copied{s}") for s in range(STREAMS)]
        m.product = [sem(f"product{s}") for s in range(STREAMS)]
        m.product_taken = [sem(f"product_taken{s}") for s in range(STREAMS)]
        m.slots_in = [sem(f"slots_in{u}") for u in range(U)]
        m.gathered = [sem(f"gathered{u}") for u in range(R)]
        m.onehot_built = sem("onehot_built")
        m.padded = sem("padded")
        m.onehot_turned = sem("onehot_turned")
        m.onehot_copied = sem("onehot_copied")
        m.own_scored = sem("own_scored")
        m.scored = sem("scored")
        m.exped = sem("exped")
        m.weighted = sem("weighted")
        m.act_weighted = sem("act_weighted")
        m.summed = sem("summed")
        m.added = sem("added")

        m.at = {k: 0 for k in ("vec", "act", "for_act", "for_vec", "for_pe", "pool", "weights_in", "rows_in",
                               "rows_used", "rows_made", "rows_out", "row_vec", "row_act", "rows_for_act",
                               "rows_for_vec", "fold", "product", "chunk", "wchunk",
                               "gathered", "slots")}

        with ExitStack() as sc:
            row_i = sc.enter_context(nc.sbuf_tensor("row_i", [P, P], I32))
            col_i = sc.enter_context(nc.sbuf_tensor("col_i", [P, 1], I32))
            with nc.Block() as block:
                @block.gpsimd
                def _(pool):
                    pool.iota(row_i[:], pattern=[[1, P]], base=0, channel_multiplier=0).then_inc(m.consts_ready, 1)
                    pool.iota(col_i[:], pattern=[[0, 1]], base=0, channel_multiplier=1).then_inc(m.consts_ready, 1)

                @block.vector
                def _(dve):
                    dve.memset(m.ones[:], 1.0)
                    dve.memset(m.score_max[:], -BIG)
                    dve.wait_ge(m.consts_ready, 2)
                    dve.tensor_copy(m.iota_row[:], row_i[:]).then_inc(m.consts_ready, 1)
                    dve.tensor_copy(m.part_col[:], col_i[:]).then_inc(m.consts_ready, 1)
                    dve.wait_ge(m.consts_ready, 4)
                    dve.tensor_scalar(m.ident[:], m.iota_row[:], m.part_col[:, 0:1], None, ALU.is_equal).then_inc(m.consts_ready, 1)
                    dve.wait_ge(m.consts_ready, 5)

        def scatters(way, start, count):
            return lambda pool: scatter_edges(pool, m, way, start, count)

        place_edges(nc, m, 0, A["dst"], A["src"], lambda pool: None)
        place_edges(nc, m, 1, A["src"], A["dst"], scatters(0, 0, 30))
        phase_0(nc, m, A, scatters(0, 30, STAGES - 30))
        edge_phase(nc, m, way=0, table=0, width=D + 9, feat=D, heads=8, own=8, mode="gat")
        phase_1(nc, m, A, scatters(1, 0, 22))
        edge_phase(nc, m, way=0, table=1, width=D, feat=D, heads=0, own=0, mode="sum")
        phase_sage(nc, m, A, 1, scatters(1, 22, 24))
        edge_phase(nc, m, way=0, table=2, width=D, feat=D, heads=0, own=0, mode="sum")
        phase_sage(nc, m, A, 2, scatters(1, 46, STAGES - 46))
        edge_phase(nc, m, way=1, table=3, width=2 * D + 8, feat=2 * D, heads=8, own=8, mode="neg")
        phase_4(nc, m, A)
        edge_phase(nc, m, way=1, table=4, width=D + 1, feat=D, heads=1, own=1, mode="neg")
        phase_5(nc, m, A)
        edge_phase(nc, m, way=0, table=5, width=D + 4, feat=D, heads=4, own=8, mode="shift")
        phase_6(nc, m, A, out)


def kernel(**inputs):
    import numpy as np
    from concourse import bacc
    from concourse.bass_utils import run_bass_kernel_spmd

    a = {k: np.asarray(v) for k, v in inputs.items()}

    def by_head(*vectors):
        h, w = vectors[0].shape
        out = np.zeros((h * w, h * len(vectors)), vectors[0].dtype)
        for n, v in enumerate(vectors):
            for k in range(h):
                out[k * w:(k + 1) * w, n * h + k] = v[k]
        return out

    x = np.zeros((NP, D), a["x"].dtype)
    x[:N_NODES] = a["x"]
    a_heads, a_out = a["L2_gnn_a_heads"], a["L2_gnn_a_out"].reshape(1, -1)
    half = a_heads.shape[1] // 2
    W2 = a["L2_gnn_W_heads"].reshape(-1, D)
    laid = {
        "x": x, "src": a["src"], "dst": a["dst"],
        "L0_WpT": a["L0_gnn_Wp"].T, "L0_gnn_Wp": a["L0_gnn_Wp"], "L0_WskipT": a["L0_gnn_Wskip"].T,
        "L0_heads": by_head(a["L0_gnn_a_src"][0], a["L0_gnn_a_trg"][0]), "L0_gnn_bias": a["L0_gnn_bias"],
        "L2_W": W2, "L2_WT": W2.T, "L2_b": a["L2_gnn_b_heads"].reshape(-1),
        "L2_heads": by_head(a_heads[:, half:], a_heads[:, :half]),
        "L2_g": a["L2_gnn_g_heads"].reshape(-1), "L2_beta": a["L2_gnn_beta_heads"].reshape(-1),
        "L2_gnn_W_out": a["L2_gnn_W_out"], "L2_WoutT": a["L2_gnn_W_out"].T, "L2_gnn_b_out": a["L2_gnn_b_out"],
        "L2_out_heads": by_head(a_out[:, D:], a_out[:, :D]),
        "L2_gnn_g_out": a["L2_gnn_g_out"], "L2_gnn_beta_out": a["L2_gnn_beta_out"],
        "L3_gnn_W": a["L3_gnn_W"], "L3_WT": a["L3_gnn_W"].T,
        "L3_heads": by_head(a["L3_gnn_att_src"], a["L3_gnn_att_dst"]),
        "L3_gnn_bias": a["L3_gnn_bias"], "L3_gnn_gamma": a["L3_gnn_gamma"], "L3_gnn_beta": a["L3_gnn_beta"],
    }
    for k in ("W_l1", "b_l1", "W_r1", "ln1_g", "ln1_b", "W_l2", "b_l2", "W_r2", "ln2_g", "ln2_b"):
        laid[f"L1_gnn_{k}"] = a[f"L1_gnn_{k}"]
    laid = {k: np.ascontiguousarray(v) for k, v in laid.items()}

    nc = bacc.Bacc("TRN2", target_bir_lowering=False, num_devices=1)
    A = {k: nc.dram_tensor(f"in_{k}", v.shape, mybir.dt.from_np(v.dtype), kind="ExternalInput").ap() for k, v in laid.items()}
    out = nc.dram_tensor("out", (NP, D), F32, kind="ExternalOutput").ap()
    build(nc, A, out)
    r = run_bass_kernel_spmd(nc, [{f"in_{k}": v for k, v in laid.items()}], core_ids=[0])
    return r.results[0]["out"][:N_NODES]
```
